# Optimizing a Trainium2 kernel written in Bass

```python
import numpy as np
import jax
import jax.numpy as jnp

def _softmax(x, axis=-1):
    return jax.nn.softmax(x, axis=axis)

def _gelu(x):
    return jax.nn.gelu(x, approximate=True)

def _silu(x):
    return jax.nn.silu(x)

def _sigmoid(x):
    return jax.nn.sigmoid(x)

def _layernorm(x, axis=-1, eps=1e-05):
    m = jnp.mean(x, axis=axis, keepdims=True)
    v = jnp.var(x, axis=axis, keepdims=True)
    return (x - m) / jnp.sqrt(v + eps)

def _scatter_add(tgt, idx, src, axis=0):
    return tgt.at[idx].add(src)

def _segment_sum(src, seg, n):
    return jax.ops.segment_sum(src, seg, n)
kernel_name = 'mk_decoder_postln_d1_seqx_r4_336016'

def setup_inputs(seed: int=0):
    np.random.seed(seed)
    _w = jnp.asarray

    def _rec_inputs():
        import jax
        import jax.numpy as jnp
        _rk = jax.random.key(seed)
        x = 7.22e-05 + 1 * jax.random.normal(jax.random.fold_in(_rk, 1), (16, 256, 512), jnp.float32)
        _lenS = 256 - jax.random.randint(jax.random.fold_in(_rk, 7), (16,), 0, max(1, 256 // 4) + 1, jnp.int32)
        _lenS2 = 256 - jax.random.randint(jax.random.fold_in(_rk, 8), (16,), 0, max(1, 256 // 4) + 1, jnp.int32)
        _ctx_512P = jax.random.normal(jax.random.fold_in(_rk, 11), (16, 16, 128), jnp.float32)
        _ctx_512c = jax.random.dirichlet(jax.random.fold_in(_rk, 511), 0.3 * jnp.ones((16,), jnp.float32), (16, 256))
        _ctx_512t = jnp.einsum('bsk,bkd->bsd', _ctx_512c, _ctx_512P)
        _ctx_512t = _ctx_512t * jax.lax.rsqrt(jnp.mean(jnp.square(_ctx_512t)) + 1e-12) * 0.953939
        ctx_512 = -0.000514642 + 1.00011 * (_ctx_512t + 0.3 * jax.random.normal(jax.random.fold_in(_rk, 611), (16, 256, 128), jnp.float32))
        return (x, ctx_512)
    x, ctx_512 = _rec_inputs()

    def _L0_attn_setup():
        import jax, jax.numpy as jnp
        import numpy as np
        E = 512
        H = 3
        key = jax.random.key(seed)
        ks = jax.random.split(key, 6)
        B, N = (4, 512)
        x = jax.random.normal(ks[0], (B, N, E), dtype=jnp.float32)
        Wq = jax.random.normal(ks[1], (H, E, E), dtype=jnp.float32) * 0.02
        Wk = jax.random.normal(ks[2], (H, E, E), dtype=jnp.float32) * 0.02
        Wv = jax.random.normal(ks[3], (H, E, E), dtype=jnp.float32) * 0.02
        fc_w = jax.random.normal(ks[4], (E, E), dtype=jnp.float32) * 0.02
        fc_b = jax.random.normal(ks[5], (E,), dtype=jnp.float32) * 0.02
        return {'x': x, 'Wq': Wq, 'Wk': Wk, 'Wv': Wv, 'fc_w': fc_w, 'fc_b': fc_b}
    _L0_attn_all = _L0_attn_setup()
    _L0_attn_in = {k: v for k, v in _L0_attn_all.items() if k in ('Wq', 'Wk', 'Wv', 'fc_w', 'fc_b')}
    del _L0_attn_all

    def _L0_xattn_setup():
        import jax, jax.numpy as jnp
        import numpy as np
        B, S, H, NH, L = (2, 512, 512, 16, 128)
        HD = H // NH
        key = jax.random.key(seed)
        k1, k2, k3, k4, k5 = jax.random.split(key, 5)
        scale = 0.02
        return {'q': jax.random.normal(k1, (B, S, H), dtype=jnp.float32), 'latent_kv': jax.random.normal(k2, (B, S, L), dtype=jnp.float32), 'Wq': jax.random.normal(k3, (H, H), dtype=jnp.float32) * scale, 'Wkv_expand': jax.random.normal(k4, (2 * H, L), dtype=jnp.float32) * scale, 'Wout': jax.random.normal(k5, (H, H), dtype=jnp.float32) * scale}
    _L0_xattn_all = _L0_xattn_setup()
    _L0_xattn_in = {k: v for k, v in _L0_xattn_all.items() if k in ('Wq', 'Wkv_expand', 'Wout')}
    del _L0_xattn_all

    def _L0_ffn_setup():
        import jax, jax.numpy as jnp
        import numpy as np
        H = 512
        F = 352
        E = 64
        TOP_K = 6
        CAP = 128
        SCALE = 1.0
        F_SH = 2 * F
        B, S = (1, 512)
        key = jax.random.key(seed)
        ks = jax.random.split(key, 8)
        s = 0.02
        return {'hidden_states': jax.random.normal(ks[0], (B, S, H), jnp.float32), 'gate_w': jax.random.normal(ks[1], (E, H), jnp.float32) * s, 'w_gate': jax.random.normal(ks[2], (E, H, F), jnp.float32) * s, 'w_up': jax.random.normal(ks[3], (E, H, F), jnp.float32) * s, 'w_down': jax.random.normal(ks[4], (E, F, H), jnp.float32) * s, 'sh_gate': jax.random.normal(ks[5], (F_SH, H), jnp.float32) * s, 'sh_up': jax.random.normal(ks[6], (F_SH, H), jnp.float32) * s, 'sh_down': jax.random.normal(ks[7], (H, F_SH), jnp.float32) * s}
    _L0_ffn_all = _L0_ffn_setup()
    _L0_ffn_in = {k: v for k, v in _L0_ffn_all.items() if k in ('gate_w', 'w_gate', 'w_up', 'w_down', 'sh_gate', 'sh_up', 'sh_down')}
    del _L0_ffn_all
    return {'x': x, 'ctx_512': ctx_512, 'L0_attn_Wq': _L0_attn_in['Wq'], 'L0_attn_Wk': _L0_attn_in['Wk'], 'L0_attn_Wv': _L0_attn_in['Wv'], 'L0_attn_fc_w': _L0_attn_in['fc_w'], 'L0_attn_fc_b': _L0_attn_in['fc_b'], 'L0_xattn_Wq': _L0_xattn_in['Wq'], 'L0_xattn_Wkv_expand': _L0_xattn_in['Wkv_expand'], 'L0_xattn_Wout': _L0_xattn_in['Wout'], 'L0_ffn_gate_w': _L0_ffn_in['gate_w'], 'L0_ffn_w_gate': _L0_ffn_in['w_gate'], 'L0_ffn_w_up': _L0_ffn_in['w_up'], 'L0_ffn_w_down': _L0_ffn_in['w_down'], 'L0_ffn_sh_gate': _L0_ffn_in['sh_gate'], 'L0_ffn_sh_up': _L0_ffn_in['sh_up'], 'L0_ffn_sh_down': _L0_ffn_in['sh_down']}

def reference(x, ctx_512, L0_attn_Wq, L0_attn_Wk, L0_attn_Wv, L0_attn_fc_w, L0_attn_fc_b, L0_xattn_Wq, L0_xattn_Wkv_expand, L0_xattn_Wout, L0_ffn_gate_w, L0_ffn_w_gate, L0_ffn_w_up, L0_ffn_w_down, L0_ffn_sh_gate, L0_ffn_sh_up, L0_ffn_sh_down):
    import jax
    import jax.numpy as jnp

    def _L0_attn_ref(x, Wq, Wk, Wv, fc_w, fc_b):
        import jax, jax.numpy as jnp
        import numpy as np
        E = 512
        H = 3
        Q = jnp.einsum('bne,hde->hbnd', x, Wq)
        K = jnp.einsum('bne,hde->hbnd', x, Wk)
        V = jnp.einsum('bne,hde->hbnd', x, Wv)
        scale = 1.0 / jnp.sqrt(jnp.float32(E))
        scores = jnp.einsum('hbnd,hbmd->hbnm', Q, K) * scale
        w = jax.nn.softmax(scores, axis=2)
        attn = jnp.einsum('hbnm,hbmd->hbnd', w, V)
        mean = jnp.mean(attn, axis=0)
        return mean @ fc_w.T + fc_b

    def _L0_xattn_ref(q, latent_kv, Wq, Wkv_expand, Wout):
        import jax, jax.numpy as jnp
        import numpy as np
        B, S, H, NH, L = (2, 512, 512, 16, 128)
        HD = H // NH
        b, sq, _ = q.shape
        sk = latent_kv.shape[1]
        qp = q @ Wq.T
        kv = latent_kv @ Wkv_expand.T
        k, v = jnp.split(kv, 2, axis=-1)
        qh = qp.reshape(b, sq, NH, HD).transpose(0, 2, 1, 3)
        kh = k.reshape(b, sk, NH, HD).transpose(0, 2, 1, 3)
        vh = v.reshape(b, sk, NH, HD).transpose(0, 2, 1, 3)
        inv_sqrt_d = 1.0 / jnp.sqrt(jnp.float32(HD))
        scores = jnp.einsum('bhqd,bhkd->bhqk', qh, kh) * inv_sqrt_d
        causal = jnp.tril(jnp.ones((sq, sk), dtype=bool))
        scores = jnp.where(causal, scores, jnp.finfo(scores.dtype).min)
        attn = jax.nn.softmax(scores, axis=-1)
        out = jnp.einsum('bhqk,bhkd->bhqd', attn, vh)
        out = out.transpose(0, 2, 1, 3).reshape(b, sq, H)
        return out @ Wout.T

    def _L0_ffn_ref(hidden_states, gate_w, w_gate, w_up, w_down, sh_gate, sh_up, sh_down):
        import jax, jax.numpy as jnp
        import numpy as np
        H = 512
        F = 352
        E = 64
        TOP_K = 6
        CAP = 128
        SCALE = 1.0
        F_SH = 2 * F
        B, S = (1, 512)
        b, s, _ = hidden_states.shape
        x = hidden_states.reshape(-1, H)
        T = x.shape[0]
        logits = x.astype(jnp.float32) @ gate_w.astype(jnp.float32).T
        scores = jax.nn.softmax(logits, axis=-1)
        topk_w, topk_idx = jax.lax.top_k(scores, TOP_K)
        topk_w = topk_w * SCALE
        eid = topk_idx.reshape(-1)
        x_exp = jnp.repeat(x, TOP_K, axis=0)
        order = jnp.argsort(eid)
        eid_s = eid[order]
        counts = jnp.bincount(eid, length=E)
        starts = jnp.cumsum(counts) - counts
        pos = jnp.arange(T * TOP_K) - starts[eid_s]
        valid = pos < CAP
        pos_c = jnp.where(valid, pos, CAP)
        buf = jnp.zeros((E, CAP + 1, H), x.dtype).at[eid_s, pos_c].set(x_exp[order])
        g = jax.nn.silu(jnp.einsum('ech,ehf->ecf', buf, w_gate))
        u = jnp.einsum('ech,ehf->ecf', buf, w_up)
        d = jnp.einsum('ecf,efh->ech', g * u, w_down)
        out_s = jnp.where(valid[:, None], d[eid_s, pos_c], 0.0)
        out_exp = jnp.zeros_like(out_s).at[order].set(out_s)
        y = jnp.einsum('tkh,tk->th', out_exp.reshape(T, TOP_K, H), topk_w)
        y = y.astype(x.dtype).reshape(b, s, H)
        gs = jax.nn.silu(hidden_states @ sh_gate.T)
        us = hidden_states @ sh_up.T
        y = y + gs * us @ sh_down.T
        return y
    x = _layernorm(x + _L0_attn_ref(x, L0_attn_Wq, L0_attn_Wk, L0_attn_Wv, L0_attn_fc_w, L0_attn_fc_b), axis=-1)
    x = _layernorm(x + _L0_xattn_ref(x, ctx_512, L0_xattn_Wq, L0_xattn_Wkv_expand, L0_xattn_Wout), axis=-1)
    x = _layernorm(x + _L0_ffn_ref(x, L0_ffn_gate_w, L0_ffn_w_gate, L0_ffn_w_up, L0_ffn_w_down, L0_ffn_sh_gate, L0_ffn_sh_up, L0_ffn_sh_down), axis=-1)
    return x

_drawn_inputs = setup_inputs


def setup_inputs(seed=0):
    import zlib

    import numpy as np

    out = dict(_drawn_inputs(seed))
    spreads = {}
    factors = {'L0_attn_Wq': 8.0,
     'L0_attn_Wk': 8.0,
     'L0_attn_Wv': 7.444,
     'L0_attn_fc_w': 7.383,
     'L0_attn_fc_b': 2.756,
     'L0_xattn_Wq': 8.0,
     'L0_ffn_gate_w': 8.0,
     'L0_ffn_w_gate': 8.0,
     'L0_ffn_w_up': 8.0,
     'L0_ffn_w_down': 8.0}
    for name, (base, spread) in spreads.items():
        noise = np.random.default_rng([zlib.crc32(name.encode()), seed]).standard_normal(out[name].shape)
        drawn = base * np.exp(spread * noise) if base else spread * noise
        out[name] = jnp.asarray(drawn.astype(out[name].dtype))
    for name, factor in factors.items():
        out[name] = (out[name] * factor).astype(out[name].dtype)
    return out
```

```python
import math
from contextlib import ExitStack

import concourse.bass as bass
from concourse import mybir

F32 = mybir.dt.float32
F16 = mybir.dt.float16
U32 = mybir.dt.uint32
ALU = mybir.AluOpType
ACT = mybir.ActivationFunctionType
AX = mybir.AxisListType

P = 128
B, N, E = 16, 256, 512
T = B * N
H = 3
NH, HD, L = 16, 32, 128
NX, F, TOPK, CAP = 64, 352, 6, 128
FS = 2 * F
EC = E // P
NB = N // P
FC = 3
F_START = [0, P, F - P]
SC6 = 6
S_START = [0, P, 2 * P, 3 * P, 4 * P, FS - P]
EPS = 1e-5
W_SCALE = 64.0
SLOTS = NX * CAP
DUMMY = T
NO_SLOT = 16384.0
PASSES = [(0, 0), (0, 1), (1, 0)]


class Memory:

    def __init__(self, nc, stack):
        self.nc, self.stack = nc, stack

    def sb(self, name, shape, dt):
        return self.stack.enter_context(self.nc.sbuf_tensor(name, shape, dt))

    def ps(self, name, shape, dt):
        return self.stack.enter_context(self.nc.psum_tensor(name, shape, dt))

    def sem(self, name):
        return self.nc.alloc_semaphore(name)


def own_wait(eng, taken):
    eng.sem_inc(taken, 1)


def inverse_root(dve, link, out, variance, tmp):
    v, bits, t = tmp[:, 0], tmp[:, 1], tmp[:, 2]
    link(dve.tensor_scalar(v, variance, EPS, None, ALU.add))
    link(dve.tensor_scalar(bits.bitcast(U32), v.bitcast(U32), 1, None, ALU.logical_shift_right))
    link(dve.tensor_scalar(out.bitcast(U32), bits.bitcast(U32), -1.0, float(0x5F3759DF), ALU.mult, ALU.add))
    for _ in range(3):
        link(dve.tensor_tensor(t, out, out, ALU.mult))
        link(dve.scalar_tensor_tensor(t, t, -0.5, v, ALU.mult, ALU.mult))
        link(dve.scalar_tensor_tensor(out, t, 1.5, out, ALU.add, ALU.mult))


def build(nc, x, xT, ctxT, wq, wk, wv, fcT, fcb, xwqT, wkvT, woutT, gateT, w_gate, w_up, w_down,
          sgT, suT, sdT, out):
    x2_d = nc.dram_tensor("x2_rows", (T + CAP, E), F32).ap()
    x2T_d = nc.dram_tensor("x2_transposed", (T // P, P, 2 * EC * P), F16).ap()
    table_d = nc.dram_tensor("slot_table", (SLOTS, 2), U32).ap()
    moe_d = nc.dram_tensor("expert_sums", (T + CAP, E), F32).ap()
    z_d = nc.dram_tensor("x2_plus_shared", (T, E), F32).ap()
    with ExitStack() as outer:
        m = Memory(nc, outer)
        ident = m.sb("ident", [P, P], F32)
        with ExitStack() as s:
            mem = Memory(nc, s)
            w = dict(
                A=mem.sb("A_split", [P, 2, H, EC, E], F16),
                M=mem.sb("M_split", [P, 2, H, EC, E], F16),
                xwq=mem.sb("xwq_split", [P, 2, EC, E], F16),
                wkv=mem.sb("wkv_split", [P, 2, 2 * E], F16),
                wout=mem.sb("wout_split", [P, 2, EC, E], F16),
                gate=mem.sb("gate_split", [P, 2, EC, NX], F16),
                bias=mem.sb("bias_rows", [P, E], F32),
                causal=mem.sb("causal_penalty", [P, N], F32),
                pick=mem.sb("pick_head", [P, EC, P], F16),
                ones=mem.sb("ones", [P, P], F16),
                before=mem.sb("earlier_tokens", [P, P], F16),
                iota=mem.sb("expert_numbers", [P, NX], F32),
                first=mem.sb("first_slots", [P, NX], F32),
                token=mem.sb("token_numbers", [P, NB], F32),
            )
            with ExitStack() as t:
                prepare(nc, Memory(nc, t), ident, w, wq, wk, wv, fcT, fcb, xwqT, wkvT, woutT, gateT,
                        x2_d, table_d, moe_d)
            with ExitStack() as t:
                attend(nc, Memory(nc, t), ident, w, x, xT, ctxT, x2_d, x2T_d, table_d)
        with ExitStack() as s:
            experts(nc, Memory(nc, s), ident, w_gate, w_up, w_down, sgT, suT, sdT, x2_d, x2T_d,
                    table_d, moe_d, z_d)
        with ExitStack() as s:
            finish(nc, Memory(nc, s), moe_d, z_d, out)


def prepare(nc, mem, ident, w, wq, wk, wv, fcT, fcb, xwqT, wkvT, woutT, gateT, x2_d, table_d, moe_d):
    NSTAGE = 3
    stage = mem.sb("w_stage", [P, NSTAGE, EC * E], F32)
    zeros = mem.sb("zero_rows", [P, 4 * E], F32)
    empty = mem.sb("empty_slots", [P, NX, 2], U32)
    empty_id = mem.sb("empty_ids", [P, NX], F32)
    qs = mem.sb("wq_split", [P, 2, H, EC, E], F16)
    ks = mem.sb("wk_split", [P, 2, H, EC, E], F16)
    vs = mem.sb("wv_split", [P, 2, H, EC, E], F16)
    fs = mem.sb("fc_split", [P, 2, EC, E], F16)
    bank = [mem.ps(f"fold{k}", [P, E], F32) for k in range(4)]

    def rows(a):
        return a.rearrange("(c p) n -> p c n", p=P)

    items = [(rows(fcT), lambda k: fs[:, k, :, :], EC * E)]
    for h in range(H):
        items.append((rows(wv[h]), lambda k, h=h: vs[:, k, h, :, :], EC * E))
        items.append((rows(wq[h]), lambda k, h=h: qs[:, k, h, :, :], EC * E))
        items.append((rows(wk[h]), lambda k, h=h: ks[:, k, h, :, :], EC * E))
    items.append((rows(xwqT), lambda k: w["xwq"][:, k, :, :], EC * E))
    items.append((rows(woutT), lambda k: w["wout"][:, k, :, :], EC * E))
    items.append((rows(wkvT), lambda k: w["wkv"][:, k, :].rearrange("p (c n) -> p c n", c=1), 2 * E))
    items.append((rows(gateT), lambda k: w["gate"][:, k, :, :], EC * NX))
    folds = [(kind, h, c) for h in range(H) for kind in ("M", "A") for c in range(EC)]

    def operands_split(kind, h):
        return 2 + 3 * h if kind == "M" else 4 + 3 * h

    staged = [mem.sem(f"staged{k}") for k in range(NSTAGE)]
    high = mem.sem("weight_high_half")
    low = mem.sem("weight_low_half")
    folded = mem.sem("folded")
    fold_high = mem.sem("fold_high_half")
    fold_low = mem.sem("fold_low_half")
    const = mem.sem("constants")
    filled = mem.sem("dram_filled")
    cleared = mem.sem("zeros_ready")
    slots_ready = mem.sem("empty_slots_ready")
    bias_in = mem.sem("bias_loaded")

    def at(n):
        src, dst, cols = items[n]
        st = stage[:, n % NSTAGE, 0:cols]
        return st.rearrange("p (c n) -> p c n", c=src.shape[1]), dst

    with nc.Block() as block:
        @block.sync
        def _(sp):
            for n in range(len(items)):
                if n >= NSTAGE:
                    sp.wait_ge(low, n - NSTAGE + 1)
                sp.dma_start(at(n)[0], items[n][0]).then_inc(staged[n % NSTAGE], 16)
            sp.dma_start(w["bias"][:, :], fcb.rearrange("(a n) -> a n", a=1).broadcast_to([P, E]))\
              .then_inc(bias_in, 16)
            sp.wait_ge(cleared, 1)
            fills = 0
            for r in range(0, T, 4 * P):
                sp.dma_start(moe_d[r:r + 4 * P, :].rearrange("(p r) n -> p (r n)", r=4), zeros[:, :])\
                  .then_inc(filled, 16)
                fills += 1
            for d in (moe_d, x2_d):
                sp.dma_start(d[T:T + CAP, :], zeros[:, 0:E]).then_inc(filled, 16)
                fills += 1
            sp.wait_ge(slots_ready, 1)
            sp.dma_start(table_d.rearrange("(e p) c -> p e c", p=CAP), empty[:, :, :]).then_inc(filled, 16)
            fills += 1
            sp.wait_ge(filled, 16 * fills)
            sp.wait_ge(bias_in, 16)

        @block.gpsimd
        def _(pool):
            step = mem.sem("pool_const_step")
            done = [0]

            def then_wait(ins):
                ins.then_inc(step, 1)
                done[0] += 1
                pool.wait_ge(step, done[0])

            then_wait(pool.memset(ident[:, :], 0.0))
            pool.affine_select(out=ident[:, :], in_=ident[:, :], compare_op=ALU.not_equal, fill=1.0,
                               base=0, pattern=[[-1, P]], channel_multiplier=1).then_inc(const, 1)
            pool.memset(zeros[:, :], 0.0).then_inc(cleared, 1)
            then_wait(pool.memset(w["causal"][:, :], 0.0))
            pool.affine_select(out=w["causal"][:, P:N], in_=w["causal"][:, P:N], compare_op=ALU.is_ge,
                               fill=-1e30, base=0, pattern=[[-1, P]], channel_multiplier=1)\
                .then_inc(const, 1)
            then_wait(pool.memset(w["pick"][:, :, :], 0.0))
            for r in range(4):
                then_wait(pool.affine_select(
                    out=w["pick"][:, :, :], in_=w["pick"][:, :, :], compare_op=ALU.not_equal, fill=-1.0,
                    base=-32 * r, pattern=[[-1, EC], [0, P]], channel_multiplier=1))
            pool.memset(w["ones"][:, :], 1.0).then_inc(const, 1)
            then_wait(pool.memset(w["before"][:, :], 0.0))
            pool.affine_select(out=w["before"][:, :], in_=w["before"][:, :], compare_op=ALU.is_ge,
                               fill=1.0, base=0, pattern=[[-1, P]], channel_multiplier=1).then_inc(const, 1)
            pool.iota(w["iota"][:, :], pattern=[[1, NX]], base=0, channel_multiplier=0,
                      allow_small_or_imprecise_dtypes=True).then_inc(const, 1)
            pool.iota(w["first"][:, :], pattern=[[CAP, NX]], base=0, channel_multiplier=0,
                      allow_small_or_imprecise_dtypes=True).then_inc(const, 1)
            pool.iota(w["token"][:, :], pattern=[[P, NB]], base=0, channel_multiplier=1,
                      allow_small_or_imprecise_dtypes=True).then_inc(const, 1)
            then_wait(pool.iota(empty_id[:, :], pattern=[[0, NX]], base=DUMMY, channel_multiplier=1,
                                allow_small_or_imprecise_dtypes=True))
            then_wait(pool.memset(empty[:, :, :].bitcast(F32), 0.0))
            pool.tensor_copy(empty[:, :, 0], empty_id[:, :]).then_inc(slots_ready, 1)
            pool.wait_ge(const, 7)

        @block.scalar
        def _(act):
            def split(n):
                act.wait_ge(staged[n % NSTAGE], 16 * (n // NSTAGE + 1))
                src, dst = at(n)
                act.activation(dst(0), src, ACT.Copy, scale=W_SCALE).then_inc(high, 1)

            n = 0
            for j, (kind, h, c) in enumerate(folds):
                while n < operands_split(kind, h) or (n < len(items) and n < operands_split(kind, h) + 2 * (c == 3)):
                    split(n)
                    n += 1
                act.wait_ge(folded, j + 1)
                act.activation(w[kind][:, 0, h, c, :], bank[j % 4][:, :], ACT.Copy,
                               scale=1.0 / W_SCALE ** 2).then_inc(fold_high, 1)
            while n < len(items):
                split(n)
                n += 1
            act.wait_ge(high, len(items))
            act.wait_ge(fold_high, len(folds))

        @block.vector
        def _(dve):
            def split(n):
                dve.wait_ge(high, n + 1)
                src, dst = at(n)
                dve.scalar_tensor_tensor(dst(1), src, W_SCALE, dst(0), ALU.mult, ALU.subtract)\
                   .then_inc(low, 1)

            n = 0
            for j, (kind, h, c) in enumerate(folds):
                while n < operands_split(kind, h) or (n < len(items) and n < operands_split(kind, h) + 2 * (c == 3)):
                    split(n)
                    n += 1
                dve.wait_ge(fold_high, j + 1)
                dve.scalar_tensor_tensor(w[kind][:, 1, h, c, :], bank[j % 4][:, :], 1.0 / W_SCALE ** 2,
                                         w[kind][:, 0, h, c, :], ALU.mult, ALU.subtract)\
                   .then_inc(fold_low, 1)
            while n < len(items):
                split(n)
                n += 1
            dve.wait_ge(low, len(items))
            dve.wait_ge(fold_low, len(folds))

        @block.tensor
        def _(pe):
            for j, (kind, h, c) in enumerate(folds):
                pe.wait_ge(low, operands_split(kind, h))
                if j >= 4:
                    pe.wait_ge(fold_low, j - 3)
                left = (vs if kind == "M" else qs)
                right = fs if kind == "M" else ks
                k = 0
                for d in range(EC):
                    for a, b in PASSES:
                        moving = right[:, b, d, :] if kind == "M" else right[:, b, h, d, :]
                        last = pe.matmul(bank[j % 4][:, :], left[:, a, h, d, c * P:(c + 1) * P], moving,
                                         start=(k == 0), stop=(k == 3 * EC - 1))
                        k += 1
                last.then_inc(folded, 1)


BODY = [
    ("X", 0, 0), ("Y", 0, 0), ("Y", 0, 1), ("T", 0, 0), ("T", 1, 0), ("Q", 0, 0), ("Q", 1, 0),
    ("V", 0, 0), ("V", 0, 1), ("K", 0, 0), ("K", 1, 0), ("S", 0, 0), ("S", 0, 1), ("M", 0, 0),
    ("S1", 0, 0), ("Y", 1, 0), ("M", 1, 0), ("S2", 0, 0), ("Y", 1, 1), ("M", 2, 0), ("V", 1, 0),
    ("M", 3, 0), ("V", 1, 1), ("MT", 0, 0), ("MT", 1, 0), ("C", 0, 0), ("C", 1, 0), ("S", 1, 0),
    ("S", 1, 1), ("ST", 0, 0), ("S1", 1, 0), ("Y", 2, 0), ("S2", 1, 0), ("P", 0, 0), ("ST", 1, 0),
    ("Y", 2, 1), ("AV", 0, 0), ("P", 1, 0), ("ST", 2, 0), ("OM", 0, 0), ("V", 2, 0), ("AV", 1, 0),
    ("P", 2, 0), ("ST", 3, 0), ("OM", 1, 0), ("S", 2, 0), ("S", 2, 1), ("S1", 2, 0), ("AV", 2, 0),
    ("P", 3, 0), ("OM", 2, 0), ("S2", 2, 0), ("V", 2, 1), ("AV", 3, 0), ("OM", 3, 0), ("O", 0, 0),
    ("OUT", 0, 0), ("OUT", 1, 0), ("LN2", 0, 0), ("O", 1, 0), ("LN1", 0, 0), ("TX", 0, 0),
    ("TX", 1, 0), ("R", 0, 0), ("RM", 0, 0), ("CT", 0, 0), ("RS", 0, 0),
]
A_STEPS = {"X", "Y", "V", "S", "S1", "S2", "O", "LN1"}
RING_STEPS = {"Y", "V", "S", "O", "T", "Q", "K", "C", "MT", "AV", "OUT", "TX", "R", "CT"}
SPLIT_STEPS = {"Y", "V", "T", "Q", "K", "C", "TX"}
RING = 4
RING_A, RING_B = 20, 20
LINKS_A, LINKS_B = 20, 30


def done_before(i, per_a, per_b=0):
    if isinstance(i, int):
        return per_a * min(i, B) + per_b * max(i - 1, 0)
    return i * (per_a + per_b) - per_b


def attend(nc, mem, ident, w, x, xT, ctxT, x2_d, x2T_d, table_d):
    x_in = mem.sb("x_in", [P, NB, E], F32)
    xT_in = mem.sb("xT_in", [P, EC, N], F32)
    c_in = mem.sb("ctx_in", [P, N], F32)
    xb = mem.sb("x_plus_bias", [P, NB, E], F32)
    xs = mem.sb("xT_split", [P, 2, EC, N], F16)
    cs = mem.sb("ctx_split", [P, 2, N], F16)
    y = mem.sb("y_split", [P, 2, EC, N], F16)
    v = mem.sb("v_split", [P, 2, H, NB, E], F16)
    e32 = mem.sb("exp_scores", [P, NB, N], F32)
    ws = mem.sb("weights_split", [P, 2, H, NB, N], F16)
    srow = mem.sb("score_rows", [P, NB, 4], F32)
    pre = mem.sb("pre_norm", [P, NB, E], F32)
    pre2 = mem.sb("pre_norm_2", [P, NB, E], F32)
    stats = mem.sb("stats", [P, NB, 6], F32)
    mv = mem.sb("mean_var", [P, NB, 2], F32)
    rstd = mem.sb("rstd", [P, NB], F32)
    root_tmp = mem.sb("root_tmp", [P, 3, NB], F32)
    x1 = mem.sb("x1", [P, NB, E], F32)
    x1s = mem.sb("x1T_split", [P, 2, EC, N], F16)
    q = mem.sb("q_split", [P, 2, EC, N], F16)
    k = mem.sb("k_split", [P, 2, EC, N], F16)
    cv = mem.sb("cv_split", [P, 2, NB, E], F16)
    mx = mem.sb("maxima", [P, NB, P], F32)
    mT = mem.sb("maxima_T", [P, N], F16)
    p32 = mem.sb("exp_cross", [P, 2, 4, N + P], F32)
    ps = mem.sb("p_split", [P, 2, 2, 4, N + P], F16)
    rden = mem.sb("inv_denominator", [P, N], F32)
    o32 = mem.sb("cross_out", [P, 2, N], F32)
    os_ = mem.sb("cross_out_split", [P, 2, EC, N], F16)
    x2 = mem.sb("x2", [P, NB, E], F32)
    x2s = mem.sb("x2T_split", [P, NB, 2, EC, P], F16)
    lg = mem.sb("logits", [P, NB, NX], F32)
    ex = mem.sb("exp_logits", [P, NB, NX], F32)
    top = mem.sb("top8", [P, NB, 8], F32)
    topi = mem.sb("top8_index", [P, NB, 8], U32)
    topf = mem.sb("top8_index_float", [P, NB, 8], F32)
    etop = mem.sb("exp_top8", [P, NB, 8], F32)
    rrow = mem.sb("router_rows", [P, NB, 4], F32)
    hot = mem.sb("one_hot", [P, NB, TOPK, NX], F32)
    hit = mem.sb("one_hot_slots", [P, NB, TOPK, NX], F32)
    chosen = mem.sb("chosen", [P, NB, NX], F16)
    total = mem.sb("chosen_before", [P, NX], F16)
    over = mem.sb("over_capacity", [P, NB, NX], F32)
    slot = mem.sb("slots", [P, NB, NX], F32)
    slotk = mem.sb("slot_of_choice", [P, NB, TOPK], F32)
    sloti = mem.sb("slot_of_choice_int", [P, NB, TOPK], U32)
    rec = mem.sb("table_records", [P, NB, TOPK, 2], U32)
    bank = [mem.ps(f"ring{n}", [P, 512], F32) for n in range(RING)]
    quad = mem.ps("quad", [P, 4, 512], F32)

    xT_loaded, ctx_loaded, x_loaded = mem.sem("xT_loaded"), mem.sem("ctx_loaded"), mem.sem("x_loaded")
    xT_split, ctx_split_, xb_ready = mem.sem("xT_split_done"), mem.sem("ctx_split_done"), mem.sem("xb_ready")
    full = mem.sem("ring_full")
    high = mem.sem("ring_high_half")
    free = mem.sem("ring_free")
    smax = mem.sem("score_max")
    sexp = mem.sem("score_exp")
    whigh = mem.sem("attention_weight_high")
    wready = mem.sem("attention_weights_ready")
    ln1, ln2 = mem.sem("x1_ready"), mem.sem("x2_ready")
    quad_full = mem.sem("quad_full")
    quad_max = mem.sem("quad_max")
    pexp = mem.sem("quad_exp")
    pmask = mem.sem("causal_masked")
    phigh = mem.sem("p_high_half")
    pready = mem.sem("p_ready")
    ohigh = mem.sem("cross_out_high")
    oready = mem.sem("cross_out_ready")
    x2_stored = mem.sem("x2_stored")
    rmax, rexp = mem.sem("router_max"), mem.sem("router_exp")
    chosen_ready = mem.sem("chosen_ready")
    rec_ready = mem.sem("records_ready")
    scattered = mem.sem("records_scattered")
    dve_step = mem.sem("dve_step")
    xfer = mem.sem("pool_high_half")
    taken = mem.sem("waits_taken")

    FULL = lambda steps: {s: n for n, s in enumerate(x for x in steps if x[0] in RING_STEPS)}
    SPLIT = lambda steps: {s: n for n, s in enumerate(x for x in steps if x[0] in SPLIT_STEPS)}

    class Body:

        def __init__(self, i, scatters):
            self.i, self.scatters = i, scatters
            self.a = not (isinstance(i, int) and i >= B)
            self.b = not (isinstance(i, int) and i < 1)
            self.steps = [s for s in BODY if (self.a if s[0] in A_STEPS else self.b)]
            self.ring, self.split = FULL(self.steps), SPLIT(self.steps)

        def job(self, *step):
            return done_before(self.i, RING_A, RING_B) + (self.ring[step] + 1)

        def last_job(self, *step):
            steps = [s for s in BODY if self.scatters or s[0] in A_STEPS]
            jobs = RING_A + (RING_B if self.scatters else 0)
            return done_before(self.i, RING_A, RING_B) + (FULL(steps)[step] + 1 - jobs)

        def high(self, *step):
            return done_before(self.i, 12, 10) + (self.split[step] + 1)

        def n(self, per_a, per_b, extra):
            return done_before(self.i, per_a, per_b) + extra

        def bank(self, *step):
            return bank[self.ring[step] % RING]

        def reuse(self, eng, *step):
            j = self.ring[step]
            if not (isinstance(self.i, int) and self.i == 0 and j < RING):
                eng.wait_ge(free, done_before(self.i, RING_A, RING_B) + (j - RING + 1))

    def bodies(eng, emit):
        emit(Body(0, False))
        emit(Body(1, False))
        with eng.Fori(2, B) as i:
            emit(Body(i, True))
        emit(Body(B, True))

    x_d = x.rearrange("(t p) e -> p t e", p=P)
    xT_d = xT.rearrange("(c p) t -> p c t", p=P)

    with nc.Block() as block:
        @block.sync
        def _(sp):
            def store(n, i):
                sp.wait_ge(ln2, n)
                sp.dma_start(x2_d[bass.ds(i * N, N), :].rearrange("(t p) e -> p t e", p=P), x2[:, :, :])\
                  .then_inc(x2_stored, 16)

            def store_T(done, i):
                sp.wait_ge(free, done)
                sp.dma_start(x2T_d[bass.ds(i * NB, NB), :, :].rearrange("t p n -> p t n"),
                             x2s[:, :, :, :, :].rearrange("p t a c n -> p t (a c n)")).then_inc(x2_stored, 16)

            def emit(b):
                i = b.i
                if b.a:
                    if not (isinstance(i, int) and i == 0):
                        sp.wait_ge(xT_split, b.n(1, 0, 0))
                    sp.dma_start(xT_in[:, :, :], xT_d[:, :, bass.ds(i * N, N)]).then_inc(xT_loaded, 16)
                if b.b:
                    if not (isinstance(i, int) and i == 1):
                        sp.wait_ge(ctx_split_, b.n(0, 1, 0))
                    sp.dma_start(c_in[:, :], ctxT[:, bass.ds((i - 1) * N, N)]).then_inc(ctx_loaded, 16)
                if b.a:
                    if not (isinstance(i, int) and i == 0):
                        sp.wait_ge(xb_ready, b.n(1, 0, 0))
                    sp.dma_start(x_in[:, :, :], x_d[:, bass.ds(i * NB, NB), :]).then_inc(x_loaded, 16)
                if b.scatters:
                    store(i - 1, i - 2)
                    store_T(b.last_job("TX", 1, 0), i - 2)

            bodies(sp, emit)
            store(B, B - 1)
            store_T(Body(B, True).job("TX", 1, 0), B - 1)
            sp.wait_ge(x2_stored, 32 * B)

        @block.gpsimd
        def _(pool):
            def scatter(n):
                pool.wait_ge(rec_ready, n)
                own_wait(pool, taken)
                for tb in range(NB):
                    for c in range(TOPK):
                        pool.indirect_dma_start(
                            table_d, bass.IndirectOffsetOnAxis(ap=sloti[:, tb, c:c + 1], axis=0),
                            rec[:, tb, c, :], None, bounds_check=SLOTS - 1, oob_is_err=False)\
                            .then_inc(scattered, 16)

            def emit(b):
                i = b.i
                if b.a:
                    pool.wait_ge(xT_loaded, b.n(16, 0, 16))
                    if b.b:
                        pool.wait_ge(full, b.last_job("V", H - 1, 1))
                    own_wait(pool, taken)
                    pool.tensor_copy(xs[:, 0, :, :], xT_in[:, :, :]).then_inc(xfer, 1)
                    pool.wait_ge(xfer, b.n(1, 1, 1))
                    pool.tensor_tensor(xs[:, 1, :, :], xT_in[:, :, :], xs[:, 0, :, :], ALU.subtract)\
                        .then_inc(xT_split, 1)
                if b.b:
                    pool.wait_ge(ctx_loaded, b.n(0, 16, 16))
                    if b.scatters:
                        pool.wait_ge(full, b.last_job("C", 1, 0))
                    own_wait(pool, taken)
                    pool.tensor_copy(cs[:, 0, :], c_in[:, :]).then_inc(xfer, 1)
                    pool.wait_ge(xfer, b.n(1, 1, 2 if b.a else 1))
                    pool.tensor_tensor(cs[:, 1, :], c_in[:, :], cs[:, 0, :], ALU.subtract)\
                        .then_inc(ctx_split_, 1)
                if b.scatters:
                    scatter(i - 1)
                if b.a:
                    pool.wait_ge(x_loaded, b.n(16, 0, 16))
                    if b.b:
                        pool.wait_ge(ln1, b.n(1, 0, 0))
                    for t in range(NB):
                        last = pool.tensor_tensor(xb[:, t, :], x_in[:, t, :], w["bias"][:, :], ALU.add)
                    last.then_inc(xb_ready, 1)
                if b.b:
                    for g in range(EC):
                        pool.wait_ge(pexp, b.n(0, 4, g + 1))
                        own_wait(pool, taken)
                        pool.affine_select(
                            out=p32[:, g % 2, :, 0:2 * P], in_=p32[:, g % 2, :, 0:2 * P],
                            compare_op=ALU.is_ge, fill=0.0, base=0, pattern=[[0, 4], [0, 2], [1, P]],
                            channel_multiplier=-1).then_inc(pmask, 1)

            bodies(pool, emit)
            scatter(B)
            pool.wait_ge(scattered, 16 * NB * TOPK * B)

        @block.tensor
        def _(pe):
            def product(out_, left, right, chunks, inc=None):
                n = 0
                for c in range(chunks):
                    for a, b in PASSES:
                        last = pe.matmul(out_, left(a, c), right(b, c), start=(n == 0),
                                         stop=(n == 3 * chunks - 1))
                        n += 1
                return last

            def emit(b):
                for s in b.steps:
                    name, g, h = s
                    if s in b.ring:
                        b.reuse(pe, *s)
                        o = b.bank(*s)
                    if name == "Y":
                        if h == 0 and g == 0:
                            pe.wait_ge(xT_split, b.n(1, 0, 1))
                        for l in range(2):
                            f = 2 * h + l
                            last = product(o[:, l * N:(l + 1) * N],
                                           lambda a, c: w["A"][:, a, g, c, f * P:(f + 1) * P],
                                           lambda a, c: xs[:, a, c, :], EC)
                    elif name == "V":
                        last = product(o[:, :], lambda a, c: xs[:, a, c, h * P:(h + 1) * P],
                                       lambda a, c: w["M"][:, a, g, c, :], EC)
                    elif name == "S":
                        pe.wait_ge(free, b.job("Y", g, 1))
                        last = product(o[:, 0:N], lambda a, c: xs[:, a, c, h * P:(h + 1) * P],
                                       lambda a, c: y[:, a, c, :], EC)
                    elif name == "O":
                        pe.wait_ge(free, b.job("V", H - 1, 1))
                        pe.wait_ge(wready, b.n(H, 0, H))
                        last = product(o[:, :],
                                       lambda a, c: ws[:, a, c // NB, c % NB, g * P:(g + 1) * P],
                                       lambda a, c: v[:, a, c // NB, c % NB, :], H * NB)
                    elif name in ("T", "TX"):
                        src = x1 if name == "T" else x2
                        pe.wait_ge(ln1 if name == "T" else ln2, b.n(0, 1, 1))
                        for l in range(2):
                            for t in range(NB):
                                last = pe.transpose(o[:, (l * NB + t) * P:(l * NB + t + 1) * P],
                                                    src[:, t, (2 * g + l) * P:(2 * g + l + 1) * P],
                                                    ident[:, :])
                    elif name == "Q":
                        pe.wait_ge(free, b.job("T", 1, 0))
                        for l in range(2):
                            d = 2 * g + l
                            last = product(o[:, l * N:(l + 1) * N],
                                           lambda a, c: w["xwq"][:, a, c, d * P:(d + 1) * P],
                                           lambda a, c: x1s[:, a, c, :], EC)
                    elif name == "K":
                        if g == 0:
                            pe.wait_ge(ctx_split_, b.n(0, 1, 1))
                        for l in range(2):
                            d = 2 * g + l
                            last = product(o[:, l * N:(l + 1) * N],
                                           lambda a, c: w["wkv"][:, a, d * P:(d + 1) * P],
                                           lambda a, c: cs[:, a, :], 1)
                    elif name == "C":
                        last = product(o[:, :], lambda a, c: cs[:, a, g * P:(g + 1) * P],
                                       lambda a, c: w["wkv"][:, a, E:2 * E], 1)
                    elif name == "M":
                        if g == 0:
                            pe.wait_ge(free, b.job("K", 1, 0))
                            if not (isinstance(b.i, int) and b.i == 1):
                                pe.wait_ge(pexp, b.n(0, 4, 0))
                        else:
                            pe.wait_ge(quad_max, b.n(0, 4, g))
                        for lo, hi, q0 in ((0, P, 0), (P, P + N, P)):
                            for r in range(4):
                                rows = slice(32 * r, 32 * r + 32)
                                last = pe.matmul(quad[:, r, lo:hi], q[rows, 0, g, q0:q0 + P],
                                                 k[rows, 0, g, 0:hi - lo], start=True, stop=True)
                        last.then_inc(quad_full, 1)
                    elif name == "MT":
                        pe.wait_ge(quad_max, b.n(0, 4, 4))
                        last = pe.transpose(o[:, 0:P], mx[:, g, :], ident[:, :])
                    elif name == "ST":
                        if g == 0:
                            pe.wait_ge(free, b.job("MT", 1, 0))
                        else:
                            pe.wait_ge(pexp, b.n(0, 4, g))
                        for lo, hi, k0, q0 in ((0, P, P, P), (P, P + N, 0, 0)):
                            for n, (a, c) in enumerate(PASSES):
                                for r in range(4):
                                    rows = slice(32 * r, 32 * r + 32)
                                    pe.matmul(quad[:, r, lo:hi], k[rows, a, g, k0:k0 + P],
                                              q[rows, c, g, q0:N], start=(n == 0), stop=False)
                            for r in range(4):
                                rows = slice(32 * r, 32 * r + 32)
                                last = pe.matmul(quad[:, r, lo:hi], w["pick"][rows, g, :],
                                                 mT[rows, q0:N], start=False, stop=True)
                        last.then_inc(quad_full, 1)
                    elif name == "AV":
                        pe.wait_ge(pready, b.n(0, 4, g + 1))
                        if g == 0:
                            pe.wait_ge(free, b.job("C", 1, 0))
                        pg = ps[:, g % 2]
                        n = 0
                        for kb, q0, lo in ((0, 0, P), (1, P, 0)):
                            for a, c in PASSES:
                                for r in range(4):
                                    col = (4 * g + r) * HD
                                    pe.matmul(o[32 * r:32 * r + 32, q0:N], cv[:, a, kb, col:col + HD],
                                              ps[:, g % 2, c, r, lo:lo + N - q0],
                                              start=(n == 0), stop=(n == 5), tile_position=(0, 32 * r))
                                n += 1
                        n = 0
                        for kb, q0, lo in ((0, 0, P), (1, P, 0)):
                            for c in range(2):
                                for r in range(4):
                                    last = pe.matmul(o[32 * r:32 * r + 32, N + q0:2 * N],
                                                     w["ones"][:, 0:HD],
                                                     ps[:, g % 2, c, r, lo:lo + N - q0],
                                                     start=(n == 0), stop=(n == 3),
                                                     tile_position=(0, 32 * r))
                                n += 1
                    elif name == "OUT":
                        pe.wait_ge(oready, b.n(0, 4, 4))
                        last = product(o[:, :], lambda a, c: os_[:, a, c, g * P:(g + 1) * P],
                                       lambda a, c: w["wout"][:, a, c, :], EC)
                    elif name == "R":
                        pe.wait_ge(free, b.job("TX", 1, 0))
                        for t in range(NB):
                            last = product(o[:, t * NX:(t + 1) * NX],
                                           lambda a, c: x2s[:, t, a, c, :],
                                           lambda a, c: w["gate"][:, a, c, :], EC)
                    elif name == "CT":
                        pe.wait_ge(chosen_ready, b.n(0, 1, 1))
                        pe.matmul(o[:, 0:NX], w["before"][:, :], chosen[:, 0, :], start=True, stop=False)
                        pe.matmul(o[:, 0:NX], w["ones"][:, :], total[:, :], start=False, stop=True)
                        pe.matmul(o[:, NX:2 * NX], w["before"][:, :], chosen[:, 1, :], start=True, stop=False)
                        pe.matmul(o[:, NX:2 * NX], w["ones"][:, :], total[:, :], start=False, stop=False)
                        last = pe.matmul(o[:, NX:2 * NX], w["ones"][:, :], chosen[:, 0, :], start=False, stop=True)
                    if s in b.ring:
                        last.then_inc(full, 1)

            bodies(pe, emit)

        def halves(name, g, h, o):
            two = o[:, :].rearrange("p (l n) -> p l n", l=2)
            if name == "Y":
                return two, lambda a: y[:, a, 2 * h:2 * h + 2, :], 1.0
            if name == "V":
                return o[:, :], lambda a: v[:, a, g, h, :], 1.0
            if name == "T":
                return two, lambda a: x1s[:, a, 2 * g:2 * g + 2, :], 1.0
            if name == "Q":
                return two, lambda a: q[:, a, 2 * g:2 * g + 2, :], 1.0 / (W_SCALE * math.sqrt(HD))
            if name == "K":
                return two, lambda a: k[:, a, 2 * g:2 * g + 2, :], 1.0 / W_SCALE
            if name == "C":
                return o[:, :], lambda a: cv[:, a, g, :], 1.0 / W_SCALE
            return (o[:, :].rearrange("p (l t n) -> p t l n", l=2, t=NB),
                    lambda a: x2s[:, :, a, 2 * g:2 * g + 2, :], 1.0)

        SC = 1.0 / math.sqrt(E)

        @block.scalar
        def _(act):
            def emit(b):
                for s in b.steps:
                    name, g, h = s
                    if s in b.split:
                        act.wait_ge(full, b.job(*s))
                        if name == "TX" and g == 0 and b.scatters:
                            act.wait_ge(x2_stored, b.n(0, 32, 0))
                        src, half, scale = halves(name, g, h, b.bank(*s))
                        act.activation(half(0), src, ACT.Copy, scale=scale).then_inc(high, 1)
                    elif name == "S":
                        act.wait_ge(smax, b.n(2 * H, 0, 2 * g + h + 1))
                        if not (isinstance(b.i, int) and b.i == 0 and g == 0):
                            act.wait_ge(wready, b.n(H, 0, g))
                        act.activation(e32[:, h, :], b.bank(*s)[:, 0:N], ACT.Exp, scale=SC,
                                       bias=srow[:, h, 1:2], accum_out=srow[:, h, 2:3]).then_inc(sexp, 1)
                    elif name == "S1":
                        for t in range(NB):
                            act.wait_ge(free, b.job("S", g, t))
                            act.activation(ws[:, 0, g, t, :], e32[:, t, :], ACT.Copy,
                                           scale=srow[:, t, 3:4]).then_inc(whigh, 1)
                    elif name == "ST":
                        act.wait_ge(quad_full, b.n(0, 8, 4 + g + 1))
                        if not (isinstance(b.i, int) and b.i == 1 and g < 2):
                            act.wait_ge(pready, b.n(0, 4, g - 1))
                        act.activation(p32[:, g % 2, :, :], quad[:, :, 0:N + P], ACT.Exp).then_inc(pexp, 1)
                    elif name == "P":
                        act.wait_ge(pmask, b.n(0, 4, g + 1))
                        if g >= 2:
                            act.wait_ge(full, b.job("AV", g - 2, 0))
                        act.activation(ps[:, g % 2, 0, :, :], p32[:, g % 2, :, :], ACT.Copy).then_inc(phigh, 1)
                    elif name == "OM":
                        act.wait_ge(free, b.job("AV", g, 0))
                        act.activation(os_[:, 0, g, :], o32[:, g % 2, :], ACT.Copy).then_inc(ohigh, 1)
                    elif name == "RM":
                        act.wait_ge(rmax, b.n(0, 1, 1))
                        for t in range(NB):
                            act.activation(ex[:, t, :], lg[:, t, :], ACT.Exp, scale=1.0 / W_SCALE,
                                           bias=rrow[:, t, 0:1], accum_out=rrow[:, t, 1:2]).then_inc(rexp, 1)
                            act.activation(etop[:, t, :], top[:, t, :], ACT.Exp, scale=1.0 / W_SCALE,
                                           bias=rrow[:, t, 0:1]).then_inc(rexp, 1)

            bodies(act, emit)

        @block.vector
        def _(dve):
            links = [0]
            dve.memset(mx[:, :, :], 0.0)
            dve.memset(total[:, :], 0.0).then_inc(dve_step, 1)
            dve.wait_ge(dve_step, 1)

            def emit(b):
                links[0] = 0

                def link(ins):
                    ins.then_inc(dve_step, 1)
                    links[0] += 1
                    dve.wait_ge(dve_step, done_before(b.i, LINKS_A, LINKS_B) + (1 + links[0]))

                def norm(pre, dst, done):
                    for t in range(NB):
                        last = dve.bn_stats(stats[:, t, :], pre[:, t, :])
                    link(last)
                    own_wait(dve, taken)
                    for t in range(NB):
                        last = dve.bn_aggr(mv[:, t, :], stats[:, t, :])
                    link(last)
                    inverse_root(dve, link, rstd[:, :], mv[:, :, 1], root_tmp)
                    for t in range(NB):
                        last = dve.tensor_scalar(dst[:, t, :], pre[:, t, :], mv[:, t, 0:1], rstd[:, t:t + 1],
                                                 ALU.subtract, ALU.mult)
                    last.then_inc(done, 1)

                for s in b.steps:
                    name, g, h = s
                    o = b.bank(*s) if s in b.ring else None
                    if s in b.split:
                        dve.wait_ge(high, b.high(*s))
                        src, half, scale = halves(name, g, h, o)
                        if name == "TX":
                            for t in range(NB):
                                last = dve.scalar_tensor_tensor(half(1)[:, t], src[:, t], scale,
                                                                half(0)[:, t], ALU.mult, ALU.subtract)
                            last.then_inc(free, 1)
                        else:
                            dve.scalar_tensor_tensor(half(1), src, scale, half(0), ALU.mult, ALU.subtract)\
                               .then_inc(free, 1)
                    elif name == "S":
                        dve.wait_ge(full, b.job(*s))
                        link(dve.reduce_max(srow[:, h, 0:1], o[:, 0:N], axis=AX.X))
                        dve.tensor_scalar(srow[:, h, 1:2], srow[:, h, 0:1], -SC, None, ALU.mult)\
                           .then_inc(smax, 1)
                    elif name == "S1":
                        for t in range(NB):
                            dve.wait_ge(sexp, b.n(2 * H, 0, 2 * g + t + 1))
                            dve.reciprocal(srow[:, t, 3:4], srow[:, t, 2:3]).then_inc(free, 1)
                    elif name == "S2":
                        dve.wait_ge(whigh, b.n(2 * H, 0, 2 * g + 2))
                        for t in range(NB):
                            last = dve.scalar_tensor_tensor(ws[:, 1, g, t, :], e32[:, t, :], srow[:, t, 3:4],
                                                            ws[:, 0, g, t, :], ALU.mult, ALU.subtract)
                        last.then_inc(wready, 1)
                    elif name == "O":
                        dve.wait_ge(full, b.job(*s))
                        if g == 0:
                            dve.wait_ge(xb_ready, b.n(1, 0, 1))
                        dve.scalar_tensor_tensor(pre[:, g, :], o[:, :], 1.0 / H, xb[:, g, :],
                                                 ALU.mult, ALU.add).then_inc(free, 1)
                    elif name == "LN1":
                        dve.wait_ge(free, b.job("O", 1, 0))
                        norm(pre, x1, ln1)
                    elif name == "M":
                        dve.wait_ge(quad_full, b.n(0, 8, g + 1))
                        own_wait(dve, taken)
                        for qb, lo, n in ((0, 0, P), (1, P, N)):
                            for r in range(4):
                                last = dve.tensor_tensor_reduce(
                                    out=quad[:, r, lo:lo + n], in0=quad[:, r, lo:lo + n],
                                    in1=w["causal"][:, N - n:N], scale=1.0, scalar=-3e38,
                                    op0=ALU.add, op1=ALU.max, accum_out=mx[:, qb, 32 * r + g:32 * r + g + 1])
                        last.then_inc(quad_max, 1)
                    elif name == "MT":
                        dve.wait_ge(full, b.job(*s))
                        dve.tensor_copy(mT[:, g * P:(g + 1) * P], o[:, 0:P]).then_inc(free, 1)
                    elif name == "P":
                        dve.wait_ge(phigh, b.n(0, 4, g + 1))
                        dve.tensor_tensor(ps[:, g % 2, 1, :, :], p32[:, g % 2, :, :], ps[:, g % 2, 0, :, :],
                                          ALU.subtract).then_inc(pready, 1)
                    elif name == "AV":
                        dve.wait_ge(full, b.job(*s))
                        link(dve.reciprocal(rden[:, :], o[:, N:2 * N]))
                        dve.tensor_tensor(o32[:, g % 2, :], o[:, 0:N], rden[:, :], ALU.mult)\
                           .then_inc(free, 1)
                    elif name == "OM":
                        dve.wait_ge(ohigh, b.n(0, 4, g + 1))
                        dve.tensor_tensor(os_[:, 1, g, :], o32[:, g % 2, :], os_[:, 0, g, :], ALU.subtract)\
                           .then_inc(oready, 1)
                    elif name == "OUT":
                        dve.wait_ge(full, b.job(*s))
                        dve.scalar_tensor_tensor(pre2[:, g, :], o[:, :], 1.0 / W_SCALE, x1[:, g, :],
                                                 ALU.mult, ALU.add).then_inc(free, 1)
                    elif name == "LN2":
                        dve.wait_ge(free, b.job("OUT", 1, 0))
                        if b.scatters:
                            dve.wait_ge(x2_stored, b.n(0, 32, 0))
                        norm(pre2, x2, ln2)
                    elif name == "R":
                        dve.wait_ge(full, b.job(*s))
                        dve.tensor_copy(lg[:, :, :], o[:, 0:NB * NX].rearrange("p (t n) -> p t n", t=NB))\
                           .then_inc(free, 1)
                        dve.wait_ge(free, b.job(*s))
                        own_wait(dve, taken)
                        for t in range(NB):
                            last = dve.max(top[:, t, :], lg[:, t, :])
                        link(last)
                        dve.tensor_scalar(rrow[:, :, 0:1], top[:, :, 0:1], -1.0 / W_SCALE, None, ALU.mult)\
                           .then_inc(rmax, 1)
                        for t in range(NB):
                            last = dve.max_index(topi[:, t, :], top[:, t, :], lg[:, t, :])
                        link(last)
                        link(dve.tensor_copy(topf[:, :, :], topi[:, :, :]))
                        for t in range(NB):
                            last = dve.tensor_tensor(
                                hot[:, t, :, :], w["iota"][:, :].unsqueeze(1).to_broadcast([P, TOPK, NX]),
                                topf[:, t, 0:TOPK].unsqueeze(2).to_broadcast([P, TOPK, NX]), ALU.is_equal)
                        link(last)
                        for t in range(NB):
                            with nc.allow_low_precision(reason="the sum is 0 or 1"):
                                last = dve.tensor_reduce(
                                    chosen[:, t, :], hot[:, t, :, :].rearrange("p k e -> p e k"),
                                    axis=AX.X, op=ALU.add)
                        last.then_inc(chosen_ready, 1)
                    elif name == "RM":
                        if b.scatters:
                            dve.wait_ge(scattered, b.n(0, 16 * NB * TOPK, 0))
                        dve.wait_ge(rexp, b.n(0, 2 * NB, 2 * NB))
                        link(dve.reciprocal(rrow[:, :, 2:3], rrow[:, :, 1:2]))
                        for t in range(NB):
                            dve.tensor_scalar(rec[:, t, :, 1].bitcast(F32), etop[:, t, 0:TOPK], rrow[:, t, 2:3],
                                              1.0 / W_SCALE, ALU.mult, ALU.mult)
                            last = dve.tensor_copy(rec[:, t, :, 0], w["token"][:, t:t + 1].to_broadcast([P, TOPK]))
                        link(last)
                        link(dve.tensor_scalar(w["token"][:, :], w["token"][:, :], float(N), None, ALU.add))
                    elif name == "CT":
                        dve.wait_ge(full, b.job(*s))
                        count = o[:, 0:NB * NX].rearrange("p (t n) -> p t n", t=NB)
                        dve.tensor_scalar(over[:, :, :], count, float(CAP), NO_SLOT, ALU.is_ge, ALU.mult)
                        dve.tensor_tensor(slot[:, :, :], count,
                                          w["first"][:, :].unsqueeze(1).to_broadcast([P, NB, NX]),
                                          ALU.add).then_inc(free, 1)
                        link(dve.tensor_tensor(total[:, :], total[:, :], chosen[:, 0, :], ALU.add))
                        link(dve.tensor_tensor(total[:, :], total[:, :], chosen[:, 1, :], ALU.add))
                    elif name == "RS":
                        dve.wait_ge(free, b.job("CT", 0, 0))
                        link(dve.tensor_tensor(slot[:, :, :], slot[:, :, :], over[:, :, :], ALU.add))
                        for t in range(NB):
                            last = dve.tensor_tensor(hit[:, t, :, :], hot[:, t, :, :],
                                                     slot[:, t, :].unsqueeze(1).to_broadcast([P, TOPK, NX]),
                                                     ALU.mult)
                        link(last)
                        link(dve.tensor_reduce(slotk[:, :, :], hit[:, :, :, :], axis=AX.X, op=ALU.add))
                        dve.tensor_copy(sloti[:, :, :], slotk[:, :, :]).then_inc(rec_ready, 1)
                assert links[0] == (LINKS_A if b.a else 0) + (LINKS_B if b.b else 0), (links[0], b.a, b.b)

            bodies(dve, emit)


MOE = [
    ("X", 0), ("X", 1), ("WG", 0), ("WU", 0), ("SG", 0), ("SU", 0), ("SH", 0), ("WD", 0), ("G", 0), ("U", 0),
    ("WG", 1), ("EH", 0), ("SG", 1), ("SU", 1), ("SH", 1), ("WU", 1), ("D", 0), ("WD", 1), ("G", 1), ("U", 1),
    ("EH", 1), ("SD", 0), ("D", 1),
]
MOE_JOBS = {s: n for n, s in enumerate(x for x in MOE if x[0] in ("X", "SG", "SU", "G", "U", "D", "SD"))}
MOE_BANKS = 8


def experts(nc, mem, ident, w_gate, w_up, w_down, sgT, suT, sdT, x2_d, x2T_d, table_d, moe_d, z_d):
    BODIES = T // P
    assert NX == 2 * BODIES
    NJ = len(MOE_JOBS)
    shared = dict(SG=mem.sb("shared_gate", [P, 2, EC, FS], F16), SU=mem.sb("shared_up", [P, 2, EC, FS], F16))
    sd = mem.sb("shared_down", [P, 2, SC6, E], F16)
    wf = dict(WG=mem.sb("gate_in", [P, 2, EC * F], F32), WU=mem.sb("up_in", [P, 2, EC * F], F32),
              WD=mem.sb("down_in", [P, 2, FC * E], F32))
    wh = dict(WG=mem.sb("w_gate_split", [P, 2, 2, EC * F], F16), WU=mem.sb("w_up_split", [P, 2, 2, EC * F], F16),
              WD=mem.sb("w_down_split", [P, 2, 2, FC * E], F16))
    records = mem.sb("records", [P, NX, 2], U32)
    gi = mem.sb("gather_index", [P, 2, 1], U32)
    si = mem.sb("scatter_index", [P, 2, 1], U32)
    xg = mem.sb("gathered", [P, 2, E], F32)
    xgs = mem.sb("gathered_T_split", [P, 2, 2, EC, P], F16)
    x2t = mem.sb("x2T_block", [P, 2, EC, P], F16)
    x2n = mem.sb("x2_block", [P, E], F32)
    act32 = mem.sb("silu_out", [P, 2, FC * P], F32)
    h32 = mem.sb("hidden", [P, 2, FC * P], F32)
    hs = mem.sb("hidden_split", [P, 2, 2, FC, P], F16)
    sact = mem.sb("shared_silu", [P, 2, FC * P], F32)
    sh32 = mem.sb("shared_hidden", [P, 2, FC * P], F32)
    shs = mem.sb("shared_hidden_split", [P, 2, SC6, P], F16)
    d32 = mem.sb("expert_out", [P, 2, E], F32)
    z = mem.sb("z_block", [P, E], F32)
    banks = [mem.ps(f"moe_bank{n}", [P, 512], F32) for n in range(MOE_BANKS)]

    shared_in = [mem.sem(f"shared_in{n}") for n in range(3)]
    shared_high, shared_low = mem.sem("shared_high"), mem.sem("shared_low")
    zero_rows = mem.sem("unused_down_rows_zero")
    records_in = mem.sem("records_in")
    w_in = {(k, s): mem.sem(f"{k}{s}_in") for k in wf for s in range(2)}
    w_high = mem.sem("expert_weight_high")
    w_low = mem.sem("expert_weight_low")
    x2t_in, x2n_in = mem.sem("x2T_in"), mem.sem("x2_in")
    index_ready = mem.sem("index_ready")
    gathered = [mem.sem(f"gathered{s}") for s in range(2)]
    full, high, free = mem.sem("moe_full"), mem.sem("moe_high"), mem.sem("moe_free")
    silu = mem.sem("silu_ready")
    prod = mem.sem("hidden_ready")
    hhigh, hlow = mem.sem("hidden_high"), mem.sem("hidden_low")
    added = mem.sem("expert_added")
    z_stored = mem.sem("z_stored")
    taken = mem.sem("waits_taken_3")

    W_ORDER = [s for s in MOE if s[0] in wf]
    H_ORDER = [s for s in MOE if s[0] in ("EH", "SH")]

    def job(i, *step):
        return i * NJ + (MOE_JOBS[step] + 1)

    def weight(i, *step):
        return i * len(W_ORDER) + (W_ORDER.index(step) + 1)

    def hidden(i, *step):
        return i * len(H_ORDER) + (H_ORDER.index(step) + 1)

    def bank_of(step):
        return banks[MOE_JOBS[step] % MOE_BANKS]

    def reuse(eng, i, step, first):
        j = MOE_JOBS[step]
        if j >= MOE_BANKS:
            eng.wait_ge(free, i * NJ + (j - MOE_BANKS + 1))
        elif not first:
            before = max(n for n in range(NJ) if n % MOE_BANKS == j)
            eng.wait_ge(free, i * NJ + (before + 1 - NJ))

    def bodies(eng, emit):
        emit(0, True)
        with eng.Fori(1, BODIES) as i:
            emit(i, False)

    def down_rows(a):
        n = a.shape[0] // P * P
        return a[0:n, :].rearrange("(c p) n -> p c n", p=P), a[n:, :]

    stage = [wf["WG"], wf["WU"], wf["WD"]]
    flat = [a[:, :, :].rearrange("p s n -> p (s n)") for a in stage]

    with nc.Block() as block:
        @block.sync
        def _(sp):
            for n, a in enumerate((sgT, suT)):
                sp.dma_start(flat[n][:, 0:EC * FS].rearrange("p (c n) -> p c n", c=EC),
                             a.rearrange("(c p) n -> p c n", p=P)).then_inc(shared_in[n], 16)
            whole, rest = down_rows(sdT)
            sp.wait_ge(zero_rows, 1)
            dst = flat[2][:, 0:SC6 * E].rearrange("p (c n) -> p c n", c=SC6)
            sp.dma_start(dst[:, 0:SC6 - 1, :], whole).then_inc(shared_in[2], 16)
            sp.dma_start(dst[P - rest.shape[0]:P, SC6 - 1, :], rest).then_inc(shared_in[2], 16)
            sp.dma_start(records[:, :, :], table_d.rearrange("(e p) c -> p e c", p=CAP)).then_inc(records_in, 16)
            sp.wait_ge(shared_low, 3)
            sp.wait_ge(zero_rows, 2)

            def emit(i, first):
                for s in range(2):
                    e = 2 * i + s
                    for k, a in (("WG", w_gate), ("WU", w_up)):
                        if not first:
                            sp.wait_ge(w_low, weight(i - 1, k, s))
                        sp.dma_start(wf[k][:, s, :],
                                     a[bass.ds(e, 1), :, :].rearrange("o (p c) f -> p (o c f)", c=EC))\
                          .then_inc(w_in[k, s], 16)
                    if s == 0:
                        if not first:
                            sp.wait_ge(full, job(i - 1, "SU", 1))
                        sp.dma_start(x2t[:, :, :, :].rearrange("p a c n -> p (a c n)"),
                                     x2T_d[bass.ds(i, 1), :, :].rearrange("o p n -> p (o n)")).then_inc(x2t_in, 16)
                    if not first:
                        sp.wait_ge(w_low, weight(i - 1, "WD", s))
                    down = wf["WD"][:, s, :].rearrange("p (c n) -> p c n", c=FC)
                    sp.dma_start(down[:, 0:FC - 1, :],
                                 w_down[bass.ds(e, 1), 0:(FC - 1) * P, :].rearrange("o (c p) n -> p (o c) n", p=P))\
                      .then_inc(w_in["WD", s], 16)
                    sp.dma_start(down[FC * P - F:P, FC - 1, :],
                                 w_down[bass.ds(e, 1), (FC - 1) * P:F, :].rearrange("o p n -> p (o n)"))\
                      .then_inc(w_in["WD", s], 16)
                if not first:
                    sp.wait_ge(free, job(i - 1, "SD", 0))
                sp.dma_start(x2n[:, :], x2_d[bass.ds(i * P, P), :]).then_inc(x2n_in, 16)
                if not first:
                    sp.dma_start(z_d[bass.ds(i * P - P, P), :], z[:, :]).then_inc(z_stored, 16)

            bodies(sp, emit)
            sp.wait_ge(free, job(BODIES - 1, "SD", 0))
            sp.dma_start(z_d[T - P:T, :], z[:, :]).then_inc(z_stored, 16)
            sp.wait_ge(z_stored, 16 * BODIES)

        @block.gpsimd
        def _(pool):
            def gather(i, first):
                for s in range(2):
                    if not first:
                        pool.wait_ge(gathered[s], 16 * i)
                        pool.wait_ge(full, job(i - 1, "X", s))
                        own_wait(pool, taken)
                    pool.tensor_copy(gi[:, s, :], records[:, bass.ds(2 * i + s, 1), 0]).then_inc(index_ready, 1)
                    pool.wait_ge(index_ready, (4 * i - 2 if not first else 0) + (s + 1))
                    own_wait(pool, taken)
                    pool.indirect_dma_start(xg[:, s, :], None, x2_d,
                                            bass.IndirectOffsetOnAxis(ap=gi[:, s, :], axis=0),
                                            bounds_check=T + CAP - 1).then_inc(gathered[s], 16)

            def add(i, first):
                for s in range(2):
                    pool.wait_ge(free, job(i, "D", s))
                    if not (first and s == 0):
                        pool.wait_ge(added, 32 * i + 16 * s)
                    own_wait(pool, taken)
                    pool.tensor_copy(si[:, s, :], records[:, bass.ds(2 * i + s, 1), 0]).then_inc(index_ready, 1)
                    pool.wait_ge(index_ready, 4 * i + (4 + s + 1))
                    own_wait(pool, taken)
                    pool.indirect_dma_start(moe_d, bass.IndirectOffsetOnAxis(ap=si[:, s, :], axis=0),
                                            d32[:, s, :], None, bounds_check=T + CAP - 1,
                                            compute_op=ALU.add).then_inc(added, 16)

            pool.wait_ge(records_in, 16)
            gather(0, True)
            gather(1, False)
            add(0, True)
            with pool.Fori(2, BODIES) as i:
                gather(i, False)
                add(i - 1, False)
            for s in range(2):
                i = BODIES - 1
                pool.wait_ge(free, job(i, "D", s))
                pool.wait_ge(added, 32 * i + 16 * s)
                pool.tensor_copy(si[:, s, :], records[:, 2 * i + s:2 * i + s + 1, 0]).then_inc(index_ready, 1)
                pool.wait_ge(index_ready, 4 * i + (2 + s + 1))
                pool.indirect_dma_start(moe_d, bass.IndirectOffsetOnAxis(ap=si[:, s, :], axis=0),
                                        d32[:, s, :], None, bounds_check=T + CAP - 1,
                                        compute_op=ALU.add).then_inc(added, 16)
            pool.wait_ge(added, 32 * BODIES)

        @block.tensor
        def _(pe):
            def emit(i, first):
                for step in MOE:
                    name, s = step
                    if step not in MOE_JOBS:
                        continue
                    reuse(pe, i, step, first)
                    o = bank_of(step)
                    if name == "X":
                        pe.wait_ge(gathered[s], 16 * i + 16)
                        for c in range(EC):
                            last = pe.transpose(o[:, c * P:(c + 1) * P],
                                                xg[:, s, :].rearrange("p (q c) -> p c q", c=EC)[:, c, :],
                                                ident[:, :])
                    elif name in ("G", "U"):
                        kind = "W" + name
                        pe.wait_ge(w_low, weight(i, kind, s))
                        if name == "G":
                            pe.wait_ge(free, job(i, "X", s))
                        wt = wh[kind][:, s, :, :].rearrange("p a (c f) -> p a c f", c=EC)
                        for f in range(FC):
                            n = 0
                            for c in range(EC):
                                for a, b in PASSES:
                                    last = pe.matmul(o[:, f * P:(f + 1) * P],
                                                     wt[:, a, c, F_START[f]:F_START[f] + P],
                                                     xgs[:, s, b, c, :], start=(n == 0), stop=(n == 3 * EC - 1))
                                    n += 1
                    elif name in ("SG", "SU"):
                        if s == 0 and name == "SG":
                            pe.wait_ge(x2t_in, 16 * i + 16)
                            if first:
                                pe.wait_ge(shared_low, 3)
                        for f in range(FC):
                            f0 = S_START[FC * s + f]
                            n = 0
                            for c in range(EC):
                                for a, b in PASSES:
                                    last = pe.matmul(o[:, f * P:(f + 1) * P], shared[name][:, a, c, f0:f0 + P],
                                                     x2t[:, b, c, :], start=(n == 0), stop=(n == 3 * EC - 1))
                                    n += 1
                    elif name == "D":
                        pe.wait_ge(w_low, weight(i, "WD", s))
                        pe.wait_ge(hlow, hidden(i, "EH", s))
                        n = 0
                        for f in range(FC):
                            for a, b in PASSES:
                                last = pe.matmul(o[:, :], hs[:, s, a, f, :],
                                                 wh["WD"][:, s, b, f * E:(f + 1) * E],
                                                 start=(n == 0), stop=(n == 3 * FC - 1))
                                n += 1
                    elif name == "SD":
                        pe.wait_ge(hlow, hidden(i, "SH", 1))
                        n = 0
                        for f in range(SC6):
                            for a, b in PASSES:
                                last = pe.matmul(o[:, :], shs[:, a, f, :], sd[:, b, f, :],
                                                 start=(n == 0), stop=(n == 3 * SC6 - 1))
                                n += 1
                    last.then_inc(full, 1)

            bodies(pe, emit)

        def part(step):
            name, s = step
            if name == "EH":
                return h32[:, s, :], lambda a: hs[:, s, a, :, :].rearrange("p f n -> p (f n)")
            return sh32[:, s, :], lambda a: shs[:, a, FC * s:FC * (s + 1), :].rearrange("p f n -> p (f n)")

        shared_dst = [shared["SG"], shared["SU"], sd]
        shared_cols = [EC * FS, EC * FS, SC6 * E]

        @block.scalar
        def _(act):
            for n in range(3):
                act.wait_ge(shared_in[n], 32 if n == 2 else 16)
                act.activation(shared_dst[n][:, 0, :, :].rearrange("p c n -> p (c n)"),
                               flat[n][:, 0:shared_cols[n]], ACT.Copy, scale=W_SCALE).then_inc(shared_high, 1)

            def emit(i, first):
                for step in MOE:
                    name, s = step
                    if name == "X":
                        act.wait_ge(full, job(i, *step))
                        act.activation(xgs[:, s, 0, :, :].rearrange("p c n -> p (c n)"), bank_of(step)[:, :],
                                       ACT.Copy).then_inc(high, 1)
                    elif name in wf:
                        act.wait_ge(w_in[name, s], (16 * i + 16) * (2 if name == "WD" else 1))
                        if not first:
                            act.wait_ge(full, job(i - 1, name[1], s))
                        act.activation(wh[name][:, s, 0, :], wf[name][:, s, :], ACT.Copy, scale=W_SCALE)\
                           .then_inc(w_high, 1)
                    elif name in ("G", "SG"):
                        act.wait_ge(full, job(i, *step))
                        if not first:
                            act.wait_ge(prod, hidden(i - 1, "EH" if name == "G" else "SH", s))
                        act.activation((act32 if name == "G" else sact)[:, s, :], bank_of(step)[:, 0:FC * P],
                                       ACT.Silu, scale=1.0 / W_SCALE).then_inc(silu, 1)
                    elif name in ("EH", "SH"):
                        act.wait_ge(prod, hidden(i, *step))
                        if name == "EH" and not first:
                            act.wait_ge(full, job(i - 1, "D", s))
                        if name == "SH" and not first:
                            act.wait_ge(full, job(i - 1, "SD", 0))
                        src, half = part(step)
                        act.activation(half(0), src, ACT.Copy).then_inc(hhigh, 1)

            bodies(act, emit)

        @block.vector
        def _(dve):
            over_s = SC6 * P - FS
            dve.memset(flat[2][0:over_s, (SC6 - 1) * E:SC6 * E], 0.0).then_inc(zero_rows, 1)
            for n in range(3):
                dve.wait_ge(shared_high, n + 1)
                dst = shared_dst[n]
                dve.scalar_tensor_tensor(dst[:, 1, :, :].rearrange("p c n -> p (c n)"),
                                         flat[n][:, 0:shared_cols[n]], W_SCALE,
                                         dst[:, 0, :, :].rearrange("p c n -> p (c n)"),
                                         ALU.mult, ALU.subtract).then_inc(shared_low, 1)
            dve.wait_ge(shared_low, 3)
            for s in range(2):
                last = dve.memset(wf["WD"][0:FC * P - F, s, (FC - 1) * E:FC * E], 0.0)
            last.then_inc(zero_rows, 1)

            SILU = [s for s in MOE if s[0] in ("G", "SG")]

            def emit(i, first):
                for step in MOE:
                    name, s = step
                    if name == "X":
                        dve.wait_ge(high, 2 * i + (s + 1))
                        dve.tensor_tensor(xgs[:, s, 1, :, :].rearrange("p c n -> p (c n)"), bank_of(step)[:, :],
                                          xgs[:, s, 0, :, :].rearrange("p c n -> p (c n)"), ALU.subtract)\
                           .then_inc(free, 1)
                    elif name in wf:
                        dve.wait_ge(w_high, weight(i, *step))
                        dve.scalar_tensor_tensor(wh[name][:, s, 1, :], wf[name][:, s, :], W_SCALE,
                                                 wh[name][:, s, 0, :], ALU.mult, ALU.subtract).then_inc(w_low, 1)
                    elif name in ("U", "SU"):
                        gate = ("G" if name == "U" else "SG", s)
                        dve.wait_ge(full, job(i, *step))
                        dve.wait_ge(silu, i * len(SILU) + (SILU.index(gate) + 1))
                        if not first:
                            dve.wait_ge(hlow, hidden(i - 1, "EH" if name == "U" else "SH", s))
                        dst, src = (h32, act32) if name == "U" else (sh32, sact)
                        dve.scalar_tensor_tensor(dst[:, s, :], bank_of(step)[:, 0:FC * P], 1.0 / W_SCALE,
                                                 src[:, s, :], ALU.mult, ALU.mult).then_inc(prod, 1)
                        dve.wait_ge(prod, hidden(i, "EH" if name == "U" else "SH", s))
                        dve.sem_inc(free, 2)
                    elif name in ("EH", "SH"):
                        dve.wait_ge(hhigh, hidden(i, *step))
                        src, half = part(step)
                        dve.tensor_tensor(half(1), src, half(0), ALU.subtract).then_inc(hlow, 1)
                    elif name == "D":
                        dve.wait_ge(full, job(i, *step))
                        if first:
                            dve.wait_ge(records_in, 16)
                        else:
                            dve.wait_ge(added, 32 * i + (16 * s - 16))
                        dve.tensor_scalar(d32[:, s, :], bank_of(step)[:, :],
                                          records[:, bass.ds(2 * i + s, 1), 1].bitcast(F32), None, ALU.mult)\
                           .then_inc(free, 1)
                    elif name == "SD":
                        dve.wait_ge(full, job(i, *step))
                        dve.wait_ge(x2n_in, 16 * i + 16)
                        if not first:
                            dve.wait_ge(z_stored, 16 * i)
                        dve.scalar_tensor_tensor(z[:, :], bank_of(step)[:, :], 1.0 / W_SCALE, x2n[:, :],
                                                 ALU.mult, ALU.add).then_inc(free, 1)

            bodies(dve, emit)


def finish(nc, mem, moe_d, z_d, out):
    R = 4
    TILES = T // (P * R)
    a = mem.sb("expert_rows", [P, 2, R, E], F32)
    z = mem.sb("z_rows", [P, 2, R, E], F32)
    r = mem.sb("summed", [P, 2, R, E], F32)
    o = mem.sb("out_rows", [P, 2, R, E], F32)
    stats = mem.sb("final_stats", [P, 2, R, 6], F32)
    mv = mem.sb("final_mean_var", [P, 2, R, 2], F32)
    sc = mem.sb("final_scale_shift", [P, 2, 2, R], F32)
    root_tmp = mem.sb("final_root_tmp", [P, 3, R], F32)
    loaded = [mem.sem(f"rows_loaded{s}") for s in range(2)]
    summed, scaled, normed = mem.sem("summed"), mem.sem("row_scales"), mem.sem("normed")
    stored = [mem.sem(f"rows_stored{s}") for s in range(2)]
    step = mem.sem("final_step")

    def rows(d, n):
        return d[n * P * R:(n + 1) * P * R, :].rearrange("(p r) n -> p r n", r=R)

    with nc.Block() as block:
        @block.sync
        def _(sp):
            for n in range(TILES):
                if n >= 2:
                    sp.wait_ge(summed, n - 1)
                sp.dma_start(a[:, n % 2], rows(moe_d, n)).then_inc(loaded[n % 2], 16)
                sp.dma_start(z[:, n % 2], rows(z_d, n)).then_inc(loaded[n % 2], 16)

        @block.vector
        def _(dve):
            links = [0]

            def link(ins):
                ins.then_inc(step, 1)
                links[0] += 1
                dve.wait_ge(step, links[0])

            for n in range(TILES):
                s = n % 2
                dve.wait_ge(loaded[s], 32 * (n // 2 + 1))
                if n >= 2:
                    dve.wait_ge(normed, n - 1)
                dve.tensor_tensor(r[:, s], a[:, s], z[:, s], ALU.add).then_inc(summed, 1)
                dve.wait_ge(summed, n + 1)
                for k in range(R):
                    last = dve.bn_stats(stats[:, s, k, :], r[:, s, k, :])
                link(last)
                for k in range(R):
                    last = dve.bn_aggr(mv[:, s, k, :], stats[:, s, k, :])
                link(last)
                inverse_root(dve, link, sc[:, s, 0, :], mv[:, s, :, 1], root_tmp)
                link(dve.scalar_tensor_tensor(sc[:, s, 1, :], mv[:, s, :, 0], -1.0, sc[:, s, 0, :],
                                              ALU.mult, ALU.mult))
                dve.sem_inc(scaled, 1)

        @block.scalar
        def _(act):
            for n in range(TILES):
                s = n % 2
                act.wait_ge(scaled, n + 1)
                if n >= 2:
                    act.wait_ge(stored[s], 16 * (n // 2))
                for k in range(R):
                    last = act.activation(o[:, s, k, :], r[:, s, k, :], ACT.Identity, scale=sc[:, s, 0, k:k + 1],
                                          bias=sc[:, s, 1, k:k + 1])
                last.then_inc(normed, 1)
                act.wait_ge(normed, n + 1)
                act.dma_start(rows(out, n), o[:, s]).then_inc(stored[s], 16)
            for s in range(2):
                act.wait_ge(stored[s], 16 * ((TILES + 1 - s) // 2))


def kernel(x, ctx_512, L0_attn_Wq, L0_attn_Wk, L0_attn_Wv, L0_attn_fc_w, L0_attn_fc_b, L0_xattn_Wq,
           L0_xattn_Wkv_expand, L0_xattn_Wout, L0_ffn_gate_w, L0_ffn_w_gate, L0_ffn_w_up, L0_ffn_w_down,
           L0_ffn_sh_gate, L0_ffn_sh_up, L0_ffn_sh_down):
    import numpy as np
    import concourse.bacc as bacc
    from concourse.bass_utils import run_bass_kernel_spmd

    def rows(a):
        return np.ascontiguousarray(a)

    flat = np.asarray(x).reshape(T, E)
    arrays = {
        "x": rows(flat), "xT": rows(flat.T), "ctxT": rows(np.asarray(ctx_512).reshape(T, L).T),
        "wq": rows(L0_attn_Wq), "wk": rows(L0_attn_Wk), "wv": rows(L0_attn_Wv),
        "fcT": rows(np.asarray(L0_attn_fc_w).T), "fcb": rows(L0_attn_fc_b),
        "xwqT": rows(np.asarray(L0_xattn_Wq).T), "wkvT": rows(np.asarray(L0_xattn_Wkv_expand).T),
        "woutT": rows(np.asarray(L0_xattn_Wout).T), "gateT": rows(np.asarray(L0_ffn_gate_w).T),
        "w_gate": rows(L0_ffn_w_gate), "w_up": rows(L0_ffn_w_up), "w_down": rows(L0_ffn_w_down),
        "sgT": rows(np.asarray(L0_ffn_sh_gate).T), "suT": rows(np.asarray(L0_ffn_sh_up).T),
        "sdT": rows(np.asarray(L0_ffn_sh_down).T),
    }
    nc = bacc.Bacc("TRN2", target_bir_lowering=False, num_devices=1)
    args = [nc.dram_tensor(f"in_{k}", a.shape, mybir.dt.from_np(a.dtype), kind="ExternalInput").ap()
            for k, a in arrays.items()]
    out = nc.dram_tensor("out_rows_dram", (T, E), F32, kind="ExternalOutput").ap()
    build(nc, *args, out)
    r = run_bass_kernel_spmd(nc, [{f"in_{k}": a for k, a in arrays.items()}], core_ids=[0])
    return r.results[0]["out_rows_dram"].reshape(B, N, E)
```

```python
import math
from contextlib import ExitStack

import concourse.bass as bass
from concourse import mybir

F32 = mybir.dt.float32
F16 = mybir.dt.float16
U32 = mybir.dt.uint32
ALU = mybir.AluOpType
ACT = mybir.ActivationFunctionType
AX = mybir.AxisListType

P = 128
B, N, E = 16, 256, 512
T = B * N
H = 3
NH, HD, L = 16, 32, 128
NX, F, TOPK, CAP = 64, 352, 6, 128
FS = 2 * F
EC = E // P
NB = N // P
FC = 3
F_START = [0, P, F - P]
SC6 = 6
S_START = [0, P, 2 * P, 3 * P, 4 * P, FS - P]
EPS = 1e-5
W_SCALE = 64.0
SLOTS = NX * CAP
DUMMY = T
NO_SLOT = 16384.0
PASSES = [(0, 0), (0, 1), (1, 0)]


class Memory:

    def __init__(self, nc, stack):
        self.nc, self.stack = nc, stack

    def sb(self, name, shape, dt):
        return self.stack.enter_context(self.nc.sbuf_tensor(name, shape, dt))

    def ps(self, name, shape, dt):
        return self.stack.enter_context(self.nc.psum_tensor(name, shape, dt))

    def sem(self, name):
        return self.nc.alloc_semaphore(name)


def own_wait(eng, taken):
    eng.sem_inc(taken, 1)


def inverse_root(dve, link, out, variance, tmp):
    v, bits, t = tmp[:, 0], tmp[:, 1], tmp[:, 2]
    link(dve.tensor_scalar(v, variance, EPS, None, ALU.add))
    link(dve.tensor_scalar(bits.bitcast(U32), v.bitcast(U32), 1, None, ALU.logical_shift_right))
    link(dve.tensor_scalar(out.bitcast(U32), bits.bitcast(U32), -1.0, float(0x5F3759DF), ALU.mult, ALU.add))
    for _ in range(3):
        link(dve.tensor_tensor(t, out, out, ALU.mult))
        link(dve.scalar_tensor_tensor(t, t, -0.5, v, ALU.mult, ALU.mult))
        link(dve.scalar_tensor_tensor(out, t, 1.5, out, ALU.add, ALU.mult))


def build(nc, x, xT, ctxT, wq, wk, wv, fcT, fcb, xwqT, wkvT, woutT, gateT, w_gate, w_up, w_down,
          sgT, suT, sdT, out):
    x2_d = nc.dram_tensor("x2_rows", (T + CAP, E), F32).ap()
    x2T_d = nc.dram_tensor("x2_transposed", (T // P, P, 2 * EC * P), F16).ap()
    table_d = nc.dram_tensor("slot_table", (SLOTS, 2), U32).ap()
    moe_d = nc.dram_tensor("expert_sums", (T + CAP, E), F32).ap()
    with ExitStack() as outer:
        m = Memory(nc, outer)
        ident = m.sb("ident", [P, P], F32)
        z = m.sb("x2_plus_shared", [P, T // P, E], F32)
        z_cols = z[:, :, :].rearrange("p t n -> p (t n)")
        stage, col = {}, T // P * E
        for name, cols in (("SG", EC * FS), ("SU", EC * FS), ("SD", SC6 * E)):
            stage[name] = z_cols[:, col - cols:col]
            col -= cols
        with ExitStack() as s:
            mem = Memory(nc, s)
            w = dict(
                A=mem.sb("A_split", [P, 2, H, EC, E], F16),
                M=mem.sb("M_split", [P, 2, H, EC, E], F16),
                xwq=mem.sb("xwq_split", [P, 2, EC, E], F16),
                wkv=mem.sb("wkv_split", [P, 2, 2 * E], F16),
                wout=mem.sb("wout_split", [P, 2, EC, E], F16),
                gate=mem.sb("gate_split", [P, 2, EC, NX], F16),
                bias=mem.sb("bias_rows", [P, E], F32),
                causal=mem.sb("causal_penalty", [P, N], F32),
                pick=mem.sb("pick_head", [P, EC, P], F16),
                ones=mem.sb("ones", [P, P], F16),
                before=mem.sb("earlier_tokens", [P, P], F16),
                iota=mem.sb("expert_numbers", [P, NX], F32),
                first=mem.sb("first_slots", [P, NX], F32),
                token=mem.sb("token_numbers", [P, NB], F32),
                empty=mem.sb("empty_slots", [P, NX, 2], U32),
                zeros=mem.sb("zero_rows", [P, 2 * E], F32),
            )
            with ExitStack() as t:
                prepare(nc, Memory(nc, t), ident, w, z_cols, wq, wk, wv, fcT, fcb, xwqT, wkvT, woutT, gateT)
            with ExitStack() as t:
                attend(nc, Memory(nc, t), ident, w, z_cols, x, xT, ctxT, x2_d, x2T_d, table_d, moe_d)
        with ExitStack() as s:
            experts(nc, Memory(nc, s), ident, z, w_gate, w_up, w_down, x2_d, x2T_d, table_d, moe_d, stage,
                    sgT, suT, sdT)
        with ExitStack() as s:
            finish(nc, Memory(nc, s), moe_d, z, out)


def prepare(nc, mem, ident, w, z_cols, wq, wk, wv, fcT, fcb, xwqT, wkvT, woutT, gateT):
    NSTAGE = 4
    stage = z_cols[:, 0:NSTAGE * EC * E].rearrange("p (k n) -> p k n", k=NSTAGE)
    empty_id = mem.sb("empty_ids", [P, NX], F32)
    qs = mem.sb("wq_split", [P, 2, H, EC, E], F16)
    ks = mem.sb("wk_split", [P, 2, H, EC, E], F16)
    at_col = NSTAGE * EC * E
    vs = z_cols[:, at_col:at_col + H * EC * E].bitcast(F16)\
        .rearrange("p (a h c n) -> p a h c n", a=2, h=H, c=EC)
    fs = z_cols[:, at_col + H * EC * E:at_col + (H + 1) * EC * E].bitcast(F16)\
        .rearrange("p (a c n) -> p a c n", a=2, c=EC)
    bank = [mem.ps(f"fold{k}", [P, E], F32) for k in range(4)]

    def rows(a):
        return a.rearrange("(c p) n -> p c n", p=P)

    items = [(rows(fcT), lambda k: fs[:, k, :, :], EC * E)]
    for h in range(H):
        items.append((rows(wv[h]), lambda k, h=h: vs[:, k, h, :, :], EC * E))
        items.append((rows(wq[h]), lambda k, h=h: qs[:, k, h, :, :], EC * E))
        items.append((rows(wk[h]), lambda k, h=h: ks[:, k, h, :, :], EC * E))
    items.append((rows(xwqT), lambda k: w["xwq"][:, k, :, :], EC * E))
    items.append((rows(woutT), lambda k: w["wout"][:, k, :, :], EC * E))
    items.append((rows(wkvT), lambda k: w["wkv"][:, k, :].rearrange("p (c n) -> p c n", c=1), 2 * E))
    items.append((rows(gateT), lambda k: w["gate"][:, k, :, :], EC * NX))
    folds = [(kind, h, c) for h in range(H) for kind in ("M", "A") for c in range(EC)]

    def operands_split(kind, h):
        return 2 + 3 * h if kind == "M" else 4 + 3 * h

    staged = [mem.sem(f"staged{k}") for k in range(NSTAGE)]
    high = mem.sem("weight_high_half")
    low = mem.sem("weight_low_half")
    folded = mem.sem("folded")
    fold_high = mem.sem("fold_high_half")
    fold_low = mem.sem("fold_low_half")
    const = mem.sem("constants")
    bias_in = mem.sem("bias_loaded")

    def at(n):
        src, dst, cols = items[n]
        st = stage[:, n % NSTAGE, 0:cols]
        return st.rearrange("p (c n) -> p c n", c=src.shape[1]), dst

    with nc.Block() as block:
        @block.sync
        def _(sp):
            for n in range(len(items)):
                if n >= NSTAGE:
                    sp.wait_ge(low, n - NSTAGE + 1)
                sp.dma_start(at(n)[0], items[n][0]).then_inc(staged[n % NSTAGE], 16)
            sp.dma_start(w["bias"][:, :], fcb.rearrange("(a n) -> a n", a=1).broadcast_to([P, E]))\
              .then_inc(bias_in, 16)
            sp.wait_ge(bias_in, 16)

        @block.gpsimd
        def _(pool):
            step = mem.sem("pool_const_step")
            done = [0]

            def then_wait(ins):
                ins.then_inc(step, 1)
                done[0] += 1
                pool.wait_ge(step, done[0])

            then_wait(pool.memset(ident[:, :], 0.0))
            pool.affine_select(out=ident[:, :], in_=ident[:, :], compare_op=ALU.not_equal, fill=1.0,
                               base=0, pattern=[[-1, P]], channel_multiplier=1).then_inc(const, 1)
            pool.memset(w["zeros"][:, :], 0.0).then_inc(const, 1)
            then_wait(pool.memset(w["causal"][:, :], 0.0))
            pool.affine_select(out=w["causal"][:, P:N], in_=w["causal"][:, P:N], compare_op=ALU.is_ge,
                               fill=-1e30, base=0, pattern=[[-1, P]], channel_multiplier=1)\
                .then_inc(const, 1)
            then_wait(pool.memset(w["pick"][:, :, :], 0.0))
            for r in range(4):
                then_wait(pool.affine_select(
                    out=w["pick"][:, :, :], in_=w["pick"][:, :, :], compare_op=ALU.not_equal, fill=-1.0,
                    base=-32 * r, pattern=[[-1, EC], [0, P]], channel_multiplier=1))
            pool.memset(w["ones"][:, :], 1.0).then_inc(const, 1)
            then_wait(pool.memset(w["before"][:, :], 0.0))
            pool.affine_select(out=w["before"][:, :], in_=w["before"][:, :], compare_op=ALU.is_ge,
                               fill=1.0, base=0, pattern=[[-1, P]], channel_multiplier=1).then_inc(const, 1)
            pool.iota(w["iota"][:, :], pattern=[[1, NX]], base=0, channel_multiplier=0,
                      allow_small_or_imprecise_dtypes=True).then_inc(const, 1)
            pool.iota(w["first"][:, :], pattern=[[CAP, NX]], base=0, channel_multiplier=0,
                      allow_small_or_imprecise_dtypes=True).then_inc(const, 1)
            pool.iota(w["token"][:, :], pattern=[[P, NB]], base=0, channel_multiplier=1,
                      allow_small_or_imprecise_dtypes=True).then_inc(const, 1)
            then_wait(pool.iota(empty_id[:, :], pattern=[[0, NX]], base=DUMMY, channel_multiplier=1,
                                allow_small_or_imprecise_dtypes=True))
            then_wait(pool.memset(w["empty"][:, :, :].bitcast(F32), 0.0))
            pool.tensor_copy(w["empty"][:, :, 0], empty_id[:, :]).then_inc(const, 1)
            pool.wait_ge(const, 9)

        @block.scalar
        def _(act):
            def split(n):
                act.wait_ge(staged[n % NSTAGE], 16 * (n // NSTAGE + 1))
                src, dst = at(n)
                act.activation(dst(0), src, ACT.Copy, scale=W_SCALE).then_inc(high, 1)

            n = 0
            for j, (kind, h, c) in enumerate(folds):
                while n < min(len(items), operands_split(kind, h) + (c + 1) // 2):
                    split(n)
                    n += 1
                act.wait_ge(folded, j + 1)
                act.activation(w[kind][:, 0, h, c, :], bank[j % 4][:, :], ACT.Copy,
                               scale=1.0 / W_SCALE ** 2).then_inc(fold_high, 1)
            while n < len(items):
                split(n)
                n += 1
            act.wait_ge(high, len(items))
            act.wait_ge(fold_high, len(folds))

        @block.vector
        def _(dve):
            def split(n):
                dve.wait_ge(high, n + 1)
                src, dst = at(n)
                dve.scalar_tensor_tensor(dst(1), src, W_SCALE, dst(0), ALU.mult, ALU.subtract)\
                   .then_inc(low, 1)

            n = 0
            for j, (kind, h, c) in enumerate(folds):
                while n < min(len(items), operands_split(kind, h) + (c + 1) // 2):
                    split(n)
                    n += 1
                dve.wait_ge(fold_high, j + 1)
                dve.scalar_tensor_tensor(w[kind][:, 1, h, c, :], bank[j % 4][:, :], 1.0 / W_SCALE ** 2,
                                         w[kind][:, 0, h, c, :], ALU.mult, ALU.subtract)\
                   .then_inc(fold_low, 1)
            while n < len(items):
                split(n)
                n += 1
            dve.wait_ge(low, len(items))
            dve.wait_ge(fold_low, len(folds))

        @block.tensor
        def _(pe):
            for j, (kind, h, c) in enumerate(folds):
                pe.wait_ge(low, operands_split(kind, h))
                if j >= 4:
                    pe.wait_ge(fold_low, j - 3)
                left = (vs if kind == "M" else qs)
                right = fs if kind == "M" else ks
                k = 0
                for d in range(EC):
                    for a, b in PASSES:
                        moving = right[:, b, d, :] if kind == "M" else right[:, b, h, d, :]
                        last = pe.matmul(bank[j % 4][:, :], left[:, a, h, d, c * P:(c + 1) * P], moving,
                                         start=(k == 0), stop=(k == 3 * EC - 1))
                        k += 1
                last.then_inc(folded, 1)


BODY = [
    ("Y", 0, 0), ("Y", 0, 1), ("V", 0, 0), ("V", 0, 1), ("T", 0, 0), ("T", 1, 0), ("K", 0, 0),
    ("K", 1, 0), ("TX", 0, 0), ("TX", 1, 0), ("Q", 0, 0), ("Q", 1, 0), ("R", 0, 0), ("C", 0, 0),
    ("C", 1, 0), ("M", 0, 0), ("S", 0, 0), ("S", 0, 1), ("S1", 0, 0), ("Y", 1, 0), ("M", 1, 0),
    ("Y", 1, 1), ("M", 2, 0), ("V", 1, 0), ("M", 3, 0), ("V", 1, 1), ("S2", 0, 0), ("S", 1, 0),
    ("S", 1, 1), ("S1", 1, 0), ("MT", 0, 0), ("MT", 1, 0), ("RC", 0, 0), ("Y", 2, 0), ("ST", 0, 0),
    ("S2", 1, 0), ("Y", 2, 1), ("P", 0, 0), ("CT", 0, 0), ("RM", 0, 0), ("ST", 1, 0), ("P", 1, 0),
    ("RS", 0, 0), ("V", 2, 0), ("AV", 0, 0), ("ST", 2, 0), ("OM", 0, 0), ("S", 2, 0), ("S", 2, 1),
    ("S1", 2, 0), ("AV", 1, 0), ("P", 2, 0), ("S2", 2, 0), ("ST", 3, 0), ("V", 2, 1), ("OM", 1, 0),
    ("P", 3, 0), ("AV", 2, 0), ("OM", 2, 0), ("O", 0, 0), ("AV", 3, 0), ("OM", 3, 0), ("O", 1, 0),
    ("OUT", 0, 0), ("OUT", 1, 0), ("LN", 0, 0),
]
A_STEPS = {"Y", "V", "S", "S1", "S2", "O"}
X_READER = [s for s in BODY if s[0] in ("Y", "V", "S")][-1]
C_STEPS = {"TX", "R", "RC", "RM", "CT", "RS"}
RING_STEPS = {"Y", "V", "S", "O", "T", "Q", "K", "C", "MT", "AV", "OUT", "TX", "R", "CT"}
SPLIT_STEPS = {"Y", "V", "T", "Q", "K", "C", "TX"}
RING = 4
RING_A, RING_B, RING_C = 20, 16, 4
LINKS_A, LINKS_B, LINKS_C, LINKS_LN = 6, 4, 12, 14


def done_before(i, per_a, per_b=0, per_c=0):
    if isinstance(i, int):
        return per_a * min(i, B) + per_b * min(max(i - 1, 0), B) + per_c * min(max(i - 2, 0), B)
    return i * (per_a + per_b + per_c) - (per_b + 2 * per_c)


def attend(nc, mem, ident, w, spare, x, xT, ctxT, x2_d, x2T_d, table_d, moe_d):
    x_in = mem.sb("x_in", [P, NB, E], F32)
    xT_in = mem.sb("xT_in", [P, EC, N], F32)
    c_in = mem.sb("ctx_in", [P, N], F32)
    xb = mem.sb("x_plus_bias", [P, NB, E], F32)
    xs = mem.sb("xT_split", [P, 2, EC, N], F16)
    cs = mem.sb("ctx_split", [P, 2, N], F16)
    e32 = mem.sb("exp_scores", [P, NB, N], F32)
    ws = mem.sb("weights_split", [P, 2, H, NB, N], F16)
    srow = mem.sb("score_rows", [P, NB, 4], F32)
    pre = mem.sb("pre_norm", [P, NB, E], F32)
    stats = mem.sb("stats", [P, 2 * NB, 6], F32)
    mv = mem.sb("mean_var", [P, 2 * NB, 2], F32)
    rstd = mem.sb("rstd", [P, 2 * NB], F32)
    root_tmp = mem.sb("root_tmp", [P, 3, 2 * NB], F32)
    x1 = mem.sb("x1", [P, NB, E], F32)
    x1s = mem.sb("x1T_split", [P, 2, EC, N], F16)
    q = mem.sb("q_split", [P, 2, EC, N], F16)
    k = mem.sb("k_split", [P, 2, EC, N], F16)
    cv = mem.sb("cv_split", [P, 2, NB, E], F16)
    mx = mem.sb("maxima", [P, NB, P], F32)
    mT = mem.sb("maxima_T", [P, N], F16)
    at_col = [0]

    def spare_cols(n):
        at_col[0] += n
        return spare[:, at_col[0] - n:at_col[0]]

    p32 = spare_cols(2 * 4 * (N + P)).rearrange("p (s r n) -> p s r n", s=2, r=4)
    ps = spare_cols(2 * 4 * (N + P)).bitcast(F16).rearrange("p (s a r n) -> p s a r n", s=2, a=2, r=4)
    v = spare_cols(H * NB * E).bitcast(F16).rearrange("p (a h t n) -> p a h t n", a=2, h=H, t=NB)
    os_ = spare_cols(EC * N).bitcast(F16).rearrange("p (a c n) -> p a c n", a=2, c=EC)
    x2s = spare_cols(NB * EC * P).bitcast(F16).rearrange("p (t a c n) -> p t a c n", t=NB, a=2, c=EC)
    hot = spare_cols(NB * TOPK * NX).rearrange("p (t k n) -> p t k n", t=NB, k=TOPK)
    hit = spare_cols(NB * TOPK * NX).rearrange("p (t k n) -> p t k n", t=NB, k=TOPK)
    y = spare_cols(EC * N).bitcast(F16).rearrange("p (a c n) -> p a c n", a=2, c=EC)
    pre2 = spare_cols(NB * E).rearrange("p (t n) -> p t n", t=NB)
    x2 = spare_cols(NB * E).rearrange("p (t n) -> p t n", t=NB)
    rden = mem.sb("inv_denominator", [P, N], F32)
    o32 = mem.sb("cross_out", [P, 2, N], F32)
    lg = mem.sb("logits", [P, NB, NX], F32)
    ex = mem.sb("exp_logits", [P, NB, NX], F32)
    top = mem.sb("top8", [P, NB, 8], F32)
    topi = mem.sb("top8_index", [P, NB, 8], U32)
    topf = mem.sb("top8_index_float", [P, NB, 8], F32)
    etop = mem.sb("exp_top8", [P, NB, 8], F32)
    rrow = mem.sb("router_rows", [P, NB, 4], F32)
    chosen = mem.sb("chosen", [P, NB, NX], F16)
    total = mem.sb("chosen_before", [P, NX], F16)
    over = mem.sb("over_capacity", [P, NB, NX], F32)
    slot = mem.sb("slots", [P, NB, NX], F32)
    slotk = mem.sb("slot_of_choice", [P, NB, TOPK], F32)
    sloti = mem.sb("slot_of_choice_int", [P, NB, TOPK], U32)
    rec = mem.sb("table_records", [P, NB, TOPK, 2], U32)
    bank = [mem.ps(f"ring{n}", [P, 512], F32) for n in range(RING)]
    quad = mem.ps("quad", [P, 4, 512], F32)

    xT_loaded, ctx_loaded, x_loaded = mem.sem("xT_loaded"), mem.sem("ctx_loaded"), mem.sem("x_loaded")
    xT_split, ctx_split_, xb_ready = mem.sem("xT_split_done"), mem.sem("ctx_split_done"), mem.sem("xb_ready")
    full = mem.sem("ring_full")
    high = mem.sem("ring_high_half")
    free = mem.sem("ring_free")
    smax = mem.sem("score_max")
    sexp = mem.sem("score_exp")
    whigh = mem.sem("attention_weight_high")
    wready = mem.sem("attention_weights_ready")
    ln1, ln2 = mem.sem("x1_ready"), mem.sem("x2_ready")
    quad_full = mem.sem("quad_full")
    quad_max = mem.sem("quad_max")
    pexp = mem.sem("quad_exp")
    pmask = mem.sem("causal_masked")
    phigh = mem.sem("p_high_half")
    pready = mem.sem("p_ready")
    ohigh = mem.sem("cross_out_high")
    oready = mem.sem("cross_out_ready")
    x2_stored, x2T_stored = mem.sem("x2_stored"), mem.sem("x2T_stored")
    filled, slots_empty = mem.sem("dram_filled"), mem.sem("slots_empty")
    rmax, rexp = mem.sem("router_max"), mem.sem("router_exp")
    chosen_ready = mem.sem("chosen_ready")
    rec_ready = mem.sem("records_ready")
    scattered = mem.sem("records_scattered")
    rec_used = mem.sem("records_used")
    dve_step = mem.sem("dve_step")
    xfer = mem.sem("pool_high_half")
    taken = mem.sem("waits_taken")

    FULL = lambda steps: {s: n for n, s in enumerate(x for x in steps if x[0] in RING_STEPS)}
    SPLIT = lambda steps: {s: n for n, s in enumerate(x for x in steps if x[0] in SPLIT_STEPS)}

    class Body:

        def __init__(self, i):
            self.i = i
            self.a = not (isinstance(i, int) and i >= B)
            self.b = not (isinstance(i, int) and not 1 <= i <= B)
            self.c = not (isinstance(i, int) and i < 2)
            self.steps = [s for s in BODY if
                          (self.a if s[0] in A_STEPS else self.c if s[0] in C_STEPS else
                           self.a or self.b if s[0] == "LN" else self.b)]
            self.ring, self.split = FULL(self.steps), SPLIT(self.steps)

        def is_(self, i):
            return isinstance(self.i, int) and self.i == i

        def job(self, *step):
            return done_before(self.i, RING_A, RING_B, RING_C) + (self.ring[step] + 1)

        def last_job(self, *step):
            steps = [s for s in BODY if s in FULL(BODY) and (s[0] in A_STEPS or not self.is_(1))]
            after = len(steps) - 1 - steps.index(step)
            return done_before(self.i, RING_A, RING_B, RING_C) - after

        def high(self, *step):
            return done_before(self.i, 12, 8, 2) + (self.split[step] + 1)

        def n(self, per_a, per_b, per_c, extra):
            return done_before(self.i, per_a, per_b, per_c) + extra

        def bank(self, *step):
            return bank[self.ring[step] % RING]

        def reuse(self, eng, *step):
            j = self.ring[step]
            if not (self.is_(0) and j < RING):
                eng.wait_ge(free, done_before(self.i, RING_A, RING_B, RING_C) + (j - RING + 1))

    def bodies(eng, emit):
        emit(Body(0))
        emit(Body(1))
        with eng.Fori(2, B) as i:
            emit(Body(i))
        emit(Body(B))
        emit(Body(B + 1))

    x_d = x.rearrange("(t p) e -> p t e", p=P)
    xT_d = xT.rearrange("(c p) t -> p c t", p=P)

    with nc.Block() as block:
        @block.sync
        def _(sp):
            def fills():
                sp.dma_start(table_d.rearrange("(e p) c -> p e c", p=CAP), w["empty"][:, :, :])\
                  .then_inc(slots_empty, 16)
                n = 0
                for r in range(0, T, 2 * P):
                    sp.dma_start(moe_d[r:r + 2 * P, :].rearrange("(p r) n -> p (r n)", r=2), w["zeros"][:, :])\
                      .then_inc(filled, 16)
                    n += 1
                for d in (moe_d, x2_d):
                    sp.dma_start(d[T:T + CAP, :], w["zeros"][:, 0:E]).then_inc(filled, 16)
                    n += 1
                return n

            filling = [0]

            def emit(b):
                i = b.i
                if b.a:
                    if not b.is_(0):
                        sp.wait_ge(xT_split, b.n(1, 0, 0, 0))
                    sp.dma_start(xT_in[:, :, :], xT_d[:, :, bass.ds(i * N, N)]).then_inc(xT_loaded, 16)
                if b.b:
                    if not b.is_(1):
                        sp.wait_ge(ctx_split_, b.n(0, 1, 0, 0))
                    sp.dma_start(c_in[:, :], ctxT[:, bass.ds((i - 1) * N, N)]).then_inc(ctx_loaded, 16)
                if b.a:
                    if not b.is_(0):
                        sp.wait_ge(xb_ready, b.n(1, 0, 0, 0))
                    sp.dma_start(x_in[:, :, :], x_d[:, bass.ds(i * NB, NB), :]).then_inc(x_loaded, 16)
                if b.c:
                    sp.wait_ge(ln2, b.n(0, 0, 1, 1))
                    sp.dma_start(x2_d[bass.ds((i - 2) * N, N), :].rearrange("(t p) e -> p t e", p=P),
                                 x2[:, :, :]).then_inc(x2_stored, 16)
                    sp.wait_ge(free, b.job("TX", 1, 0))
                    sp.dma_start(x2T_d[bass.ds((i - 2) * NB, NB), :, :].rearrange("t p n -> p t n"),
                                 x2s[:, :, :, :, :].rearrange("p t a c n -> p t (a c n)"))\
                      .then_inc(x2T_stored, 16)
                if b.is_(0):
                    filling[0] = fills()

            sp.sem_inc(x2_stored, 1)
            sp.sem_inc(x2T_stored, 1)
            bodies(sp, emit)
            sp.wait_ge(x2_stored, 16 * B + 1)
            sp.wait_ge(x2T_stored, 16 * B + 1)
            sp.wait_ge(filled, 16 * filling[0])

        @block.gpsimd
        def _(pool):
            def emit(b):
                if b.a:
                    pool.wait_ge(xT_loaded, b.n(16, 0, 0, 16))
                    if not b.is_(0):
                        pool.wait_ge(full, b.last_job(*X_READER))
                    own_wait(pool, taken)
                    pool.tensor_copy(xs[:, 0, :, :], xT_in[:, :, :]).then_inc(xfer, 1)
                    pool.wait_ge(xfer, b.n(1, 1, 0, 1))
                    pool.tensor_tensor(xs[:, 1, :, :], xT_in[:, :, :], xs[:, 0, :, :], ALU.subtract)\
                        .then_inc(xT_split, 1)
                if b.b:
                    pool.wait_ge(ctx_loaded, b.n(0, 16, 0, 16))
                    if not b.is_(1):
                        pool.wait_ge(full, b.last_job("C", 1, 0))
                    own_wait(pool, taken)
                    pool.tensor_copy(cs[:, 0, :], c_in[:, :]).then_inc(xfer, 1)
                    pool.wait_ge(xfer, b.n(1, 1, 0, 2 if b.a else 1))
                    pool.tensor_tensor(cs[:, 1, :], c_in[:, :], cs[:, 0, :], ALU.subtract)\
                        .then_inc(ctx_split_, 1)
                if b.a:
                    pool.wait_ge(x_loaded, b.n(16, 0, 0, 16))
                    if not b.is_(0):
                        pool.wait_ge(ln1, b.n(1, 0, 0, 0))
                    for t in range(NB):
                        last = pool.tensor_tensor(xb[:, t, :], x_in[:, t, :], w["bias"][:, :], ALU.add)
                    last.then_inc(xb_ready, 1)
                def scatter(first, end):
                    if first == 0:
                        pool.wait_ge(rec_ready, b.n(0, 0, 1, 1))
                        own_wait(pool, taken)
                    for tb, c in [(tb, c) for tb in range(NB) for c in range(TOPK)][first:end]:
                        pool.indirect_dma_start(
                            table_d, bass.IndirectOffsetOnAxis(ap=sloti[:, tb, c:c + 1], axis=0),
                            rec[:, tb, c, :], None, bounds_check=SLOTS - 1, oob_is_err=False)\
                            .then_inc(scattered, 16)

                if b.b:
                    for g in range(EC):
                        pool.wait_ge(pexp, b.n(0, 4, 0, g + 1))
                        own_wait(pool, taken)
                        pool.affine_select(
                            out=p32[:, g % 2, :, 0:2 * P], in_=p32[:, g % 2, :, 0:2 * P],
                            compare_op=ALU.is_ge, fill=0.0, base=0, pattern=[[0, 4], [0, 2], [1, P]],
                            channel_multiplier=-1).then_inc(pmask, 1)
                        if b.c and g > 0:
                            scatter((g - 1) * NB * TOPK // (EC - 1), g * NB * TOPK // (EC - 1))
                elif b.c:
                    scatter(0, NB * TOPK)
                if b.is_(0):
                    pool.wait_ge(slots_empty, 16)
                    pool.sem_inc(rec_used, 1)
                if b.c:
                    pool.wait_ge(scattered, 16 * NB * TOPK * b.n(0, 0, 1, 1))
                    pool.sem_inc(rec_used, 1)

            bodies(pool, emit)
            pool.wait_ge(scattered, 16 * NB * TOPK * B)

        @block.tensor
        def _(pe):
            def product(out_, left, right, chunks, inc=None):
                n = 0
                for c in range(chunks):
                    for a, b in PASSES:
                        last = pe.matmul(out_, left(a, c), right(b, c), start=(n == 0),
                                         stop=(n == 3 * chunks - 1))
                        n += 1
                return last

            def emit(b):
                for s in b.steps:
                    name, g, h = s
                    if s in b.ring:
                        b.reuse(pe, *s)
                        o = b.bank(*s)
                    if name == "Y":
                        if h == 0 and g == 0:
                            pe.wait_ge(xT_split, b.n(1, 0, 0, 1))
                        for l in range(2):
                            f = 2 * h + l
                            last = product(o[:, l * N:(l + 1) * N],
                                           lambda a, c: w["A"][:, a, g, c, f * P:(f + 1) * P],
                                           lambda a, c: xs[:, a, c, :], EC)
                    elif name == "V":
                        last = product(o[:, :], lambda a, c: xs[:, a, c, h * P:(h + 1) * P],
                                       lambda a, c: w["M"][:, a, g, c, :], EC)
                    elif name == "S":
                        pe.wait_ge(free, b.job("Y", g, 1))
                        last = product(o[:, 0:N], lambda a, c: xs[:, a, c, h * P:(h + 1) * P],
                                       lambda a, c: y[:, a, c, :], EC)
                    elif name == "O":
                        pe.wait_ge(free, b.job("V", H - 1, 1))
                        pe.wait_ge(wready, b.n(H, 0, 0, H))
                        last = product(o[:, :],
                                       lambda a, c: ws[:, a, c // NB, c % NB, g * P:(g + 1) * P],
                                       lambda a, c: v[:, a, c // NB, c % NB, :], H * NB)
                    elif name in ("T", "TX"):
                        src = x1 if name == "T" else x2
                        pe.wait_ge(ln1 if name == "T" else ln2, b.n(0, 1, 0, 1) if name == "T" else b.n(0, 0, 1, 1))
                        for l in range(2):
                            for t in range(NB):
                                last = pe.transpose(o[:, (l * NB + t) * P:(l * NB + t + 1) * P],
                                                    src[:, t, (2 * g + l) * P:(2 * g + l + 1) * P],
                                                    ident[:, :])
                    elif name == "Q":
                        pe.wait_ge(free, b.job("T", 1, 0))
                        for l in range(2):
                            d = 2 * g + l
                            last = product(o[:, l * N:(l + 1) * N],
                                           lambda a, c: w["xwq"][:, a, c, d * P:(d + 1) * P],
                                           lambda a, c: x1s[:, a, c, :], EC)
                    elif name == "K":
                        if g == 0:
                            pe.wait_ge(ctx_split_, b.n(0, 1, 0, 1))
                        for l in range(2):
                            d = 2 * g + l
                            last = product(o[:, l * N:(l + 1) * N],
                                           lambda a, c: w["wkv"][:, a, d * P:(d + 1) * P],
                                           lambda a, c: cs[:, a, :], 1)
                    elif name == "C":
                        last = product(o[:, :], lambda a, c: cs[:, a, g * P:(g + 1) * P],
                                       lambda a, c: w["wkv"][:, a, E:2 * E], 1)
                    elif name == "M":
                        if g == 0:
                            pe.wait_ge(free, b.job("K", 1, 0))
                            pe.wait_ge(free, b.job("Q", 1, 0))
                            if not b.is_(1):
                                pe.wait_ge(pexp, b.n(0, 4, 0, 0))
                        else:
                            pe.wait_ge(quad_max, b.n(0, 4, 0, g))
                        for lo, hi, q0 in ((0, P, 0), (P, P + N, P)):
                            for r in range(4):
                                rows = slice(32 * r, 32 * r + 32)
                                last = pe.matmul(quad[:, r, lo:hi], q[rows, 0, g, q0:q0 + P],
                                                 k[rows, 0, g, 0:hi - lo], start=True, stop=True)
                        last.then_inc(quad_full, 1)
                    elif name == "MT":
                        pe.wait_ge(quad_max, b.n(0, 4, 0, 4))
                        last = pe.transpose(o[:, 0:P], mx[:, g, :], ident[:, :])
                    elif name == "ST":
                        if g == 0:
                            pe.wait_ge(free, b.job("MT", 1, 0))
                        else:
                            pe.wait_ge(pexp, b.n(0, 4, 0, g))
                        for lo, hi, k0, q0 in ((0, P, P, P), (P, P + N, 0, 0)):
                            for n, (a, c) in enumerate(PASSES):
                                for r in range(4):
                                    rows = slice(32 * r, 32 * r + 32)
                                    pe.matmul(quad[:, r, lo:hi], k[rows, a, g, k0:k0 + P],
                                              q[rows, c, g, q0:N], start=(n == 0), stop=False)
                            for r in range(4):
                                rows = slice(32 * r, 32 * r + 32)
                                last = pe.matmul(quad[:, r, lo:hi], w["pick"][rows, g, :],
                                                 mT[rows, q0:N], start=False, stop=True)
                        last.then_inc(quad_full, 1)
                    elif name == "AV":
                        pe.wait_ge(pready, b.n(0, 4, 0, g + 1))
                        if g == 0:
                            pe.wait_ge(free, b.job("C", 1, 0))
                        pg = ps[:, g % 2]
                        n = 0
                        for kb, q0, lo in ((0, 0, P), (1, P, 0)):
                            for a, c in PASSES:
                                for r in range(4):
                                    col = (4 * g + r) * HD
                                    pe.matmul(o[32 * r:32 * r + 32, q0:N], cv[:, a, kb, col:col + HD],
                                              ps[:, g % 2, c, r, lo:lo + N - q0],
                                              start=(n == 0), stop=(n == 5), tile_position=(0, 32 * r))
                                n += 1
                        n = 0
                        for kb, q0, lo in ((0, 0, P), (1, P, 0)):
                            for c in range(2):
                                for r in range(4):
                                    last = pe.matmul(o[32 * r:32 * r + 32, N + q0:2 * N],
                                                     w["ones"][:, 0:HD],
                                                     ps[:, g % 2, c, r, lo:lo + N - q0],
                                                     start=(n == 0), stop=(n == 3),
                                                     tile_position=(0, 32 * r))
                                n += 1
                    elif name == "OUT":
                        pe.wait_ge(oready, b.n(0, 4, 0, 4))
                        last = product(o[:, :], lambda a, c: os_[:, a, c, g * P:(g + 1) * P],
                                       lambda a, c: w["wout"][:, a, c, :], EC)
                    elif name == "R":
                        pe.wait_ge(free, b.job("TX", 1, 0))
                        for t in range(NB):
                            last = product(o[:, t * NX:(t + 1) * NX],
                                           lambda a, c: x2s[:, t, a, c, :],
                                           lambda a, c: w["gate"][:, a, c, :], EC)
                    elif name == "CT":
                        pe.wait_ge(chosen_ready, b.n(0, 0, 1, 1))
                        pe.matmul(o[:, 0:NX], w["before"][:, :], chosen[:, 0, :], start=True, stop=False)
                        pe.matmul(o[:, 0:NX], w["ones"][:, :], total[:, :], start=False, stop=True)
                        pe.matmul(o[:, NX:2 * NX], w["before"][:, :], chosen[:, 1, :], start=True, stop=False)
                        pe.matmul(o[:, NX:2 * NX], w["ones"][:, :], total[:, :], start=False, stop=False)
                        last = pe.matmul(o[:, NX:2 * NX], w["ones"][:, :], chosen[:, 0, :], start=False, stop=True)
                    if s in b.ring:
                        last.then_inc(full, 1)

            bodies(pe, emit)

        def halves(name, g, h, o):
            two = o[:, :].rearrange("p (l n) -> p l n", l=2)
            if name == "Y":
                return two, lambda a: y[:, a, 2 * h:2 * h + 2, :], 1.0
            if name == "V":
                return o[:, :], lambda a: v[:, a, g, h, :], 1.0
            if name == "T":
                return two, lambda a: x1s[:, a, 2 * g:2 * g + 2, :], 1.0
            if name == "Q":
                return two, lambda a: q[:, a, 2 * g:2 * g + 2, :], 1.0 / (W_SCALE * math.sqrt(HD))
            if name == "K":
                return two, lambda a: k[:, a, 2 * g:2 * g + 2, :], 1.0 / W_SCALE
            if name == "C":
                return o[:, :], lambda a: cv[:, a, g, :], 1.0 / W_SCALE
            return (o[:, :].rearrange("p (l t n) -> p t l n", l=2, t=NB),
                    lambda a: x2s[:, :, a, 2 * g:2 * g + 2, :], 1.0)

        SC = 1.0 / math.sqrt(E)

        @block.scalar
        def _(act):
            def emit(b):
                for s in b.steps:
                    name, g, h = s
                    if s in b.split:
                        act.wait_ge(full, b.job(*s))
                        if name == "TX" and g == 0:
                            act.wait_ge(x2T_stored, b.n(0, 0, 16, 1))
                        src, half, scale = halves(name, g, h, b.bank(*s))
                        act.activation(half(0), src, ACT.Copy, scale=scale).then_inc(high, 1)
                    elif name == "S":
                        act.wait_ge(smax, b.n(2 * H, 0, 0, 2 * g + h + 1))
                        if not (b.is_(0) and g == 0):
                            act.wait_ge(wready, b.n(H, 0, 0, g))
                        act.activation(e32[:, h, :], b.bank(*s)[:, 0:N], ACT.Exp, scale=SC,
                                       bias=srow[:, h, 1:2], accum_out=srow[:, h, 2:3]).then_inc(sexp, 1)
                    elif name == "S1":
                        for t in range(NB):
                            act.wait_ge(free, b.job("S", g, t))
                            act.activation(ws[:, 0, g, t, :], e32[:, t, :], ACT.Copy,
                                           scale=srow[:, t, 3:4]).then_inc(whigh, 1)
                    elif name == "ST":
                        act.wait_ge(quad_full, b.n(0, 8, 0, 4 + g + 1))
                        if not (b.is_(1) and g < 2):
                            act.wait_ge(pready, b.n(0, 4, 0, g - 1))
                        act.activation(p32[:, g % 2, :, :], quad[:, :, 0:N + P], ACT.Exp).then_inc(pexp, 1)
                    elif name == "P":
                        act.wait_ge(pmask, b.n(0, 4, 0, g + 1))
                        if g >= 2:
                            act.wait_ge(full, b.job("AV", g - 2, 0))
                        act.activation(ps[:, g % 2, 0, :, :], p32[:, g % 2, :, :], ACT.Copy).then_inc(phigh, 1)
                    elif name == "OM":
                        act.wait_ge(free, b.job("AV", g, 0))
                        act.activation(os_[:, 0, g, :], o32[:, g % 2, :], ACT.Copy).then_inc(ohigh, 1)
                    elif name == "RM":
                        act.wait_ge(rmax, b.n(0, 0, 1, 1))
                        for t in range(NB):
                            act.activation(ex[:, t, :], lg[:, t, :], ACT.Exp, scale=1.0 / W_SCALE,
                                           bias=rrow[:, t, 0:1], accum_out=rrow[:, t, 1:2]).then_inc(rexp, 1)
                            act.activation(etop[:, t, :], top[:, t, :], ACT.Exp, scale=1.0 / W_SCALE,
                                           bias=rrow[:, t, 0:1]).then_inc(rexp, 1)

            bodies(act, emit)

        @block.vector
        def _(dve):
            links = [0]
            dve.memset(mx[:, :, :], 0.0)
            dve.memset(total[:, :], 0.0).then_inc(dve_step, 1)
            dve.wait_ge(dve_step, 1)

            def emit(b):
                links[0] = 0

                def link(ins):
                    ins.then_inc(dve_step, 1)
                    links[0] += 1
                    dve.wait_ge(dve_step, done_before(b.i, LINKS_A, LINKS_B, LINKS_C) + b.i * LINKS_LN + (1 + links[0]))

                def norm(parts):
                    rows = [(at + t, pre[:, t, :], dst[:, t, :]) for at, pre, dst, _ in parts for t in range(NB)]
                    for n, src, _ in rows:
                        last = dve.bn_stats(stats[:, n, :], src)
                    link(last)
                    own_wait(dve, taken)
                    for n, _, _ in rows:
                        last = dve.bn_aggr(mv[:, n, :], stats[:, n, :])
                    link(last)
                    n0, n1 = rows[0][0], rows[-1][0] + 1
                    inverse_root(dve, link, rstd[:, n0:n1], mv[:, n0:n1, 1], root_tmp[:, :, n0:n1])
                    for n, src, dst in rows:
                        last = dve.tensor_scalar(dst, src, mv[:, n, 0:1], rstd[:, n:n + 1], ALU.subtract, ALU.mult)
                        if n % NB == NB - 1:
                            last.then_inc(parts[(n - n0) // NB][3], 1)

                for s in b.steps:
                    name, g, h = s
                    o = b.bank(*s) if s in b.ring else None
                    if s in b.split:
                        dve.wait_ge(high, b.high(*s))
                        src, half, scale = halves(name, g, h, o)
                        if name == "TX":
                            for t in range(NB):
                                last = dve.scalar_tensor_tensor(half(1)[:, t], src[:, t], scale,
                                                                half(0)[:, t], ALU.mult, ALU.subtract)
                            last.then_inc(free, 1)
                        else:
                            dve.scalar_tensor_tensor(half(1), src, scale, half(0), ALU.mult, ALU.subtract)\
                               .then_inc(free, 1)
                    elif name == "S":
                        dve.wait_ge(full, b.job(*s))
                        link(dve.reduce_max(srow[:, h, 0:1], o[:, 0:N], axis=AX.X))
                        dve.tensor_scalar(srow[:, h, 1:2], srow[:, h, 0:1], -SC, None, ALU.mult)\
                           .then_inc(smax, 1)
                    elif name == "S1":
                        for t in range(NB):
                            dve.wait_ge(sexp, b.n(2 * H, 0, 0, 2 * g + t + 1))
                            dve.reciprocal(srow[:, t, 3:4], srow[:, t, 2:3]).then_inc(free, 1)
                    elif name == "S2":
                        dve.wait_ge(whigh, b.n(2 * H, 0, 0, 2 * g + 2))
                        for t in range(NB):
                            last = dve.scalar_tensor_tensor(ws[:, 1, g, t, :], e32[:, t, :], srow[:, t, 3:4],
                                                            ws[:, 0, g, t, :], ALU.mult, ALU.subtract)
                        last.then_inc(wready, 1)
                    elif name == "O":
                        dve.wait_ge(full, b.job(*s))
                        if g == 0:
                            dve.wait_ge(xb_ready, b.n(1, 0, 0, 1))
                        dve.scalar_tensor_tensor(pre[:, g, :], o[:, :], 1.0 / H, xb[:, g, :],
                                                 ALU.mult, ALU.add).then_inc(free, 1)
                    elif name == "LN":
                        parts = []
                        if b.a:
                            dve.wait_ge(free, b.job("O", 1, 0))
                            parts.append((0, pre, x1, ln1))
                        if b.b:
                            dve.wait_ge(free, b.job("OUT", 1, 0))
                            dve.wait_ge(x2_stored, b.n(0, 0, 16, 17 if b.c else 1))
                            parts.append((NB, pre2, x2, ln2))
                        norm(parts)
                    elif name == "M":
                        dve.wait_ge(quad_full, b.n(0, 8, 0, g + 1))
                        own_wait(dve, taken)
                        for qb, lo, n in ((0, 0, P), (1, P, N)):
                            for r in range(4):
                                last = dve.tensor_tensor_reduce(
                                    out=quad[:, r, lo:lo + n], in0=quad[:, r, lo:lo + n],
                                    in1=w["causal"][:, N - n:N], scale=1.0, scalar=-3e38,
                                    op0=ALU.add, op1=ALU.max, accum_out=mx[:, qb, 32 * r + g:32 * r + g + 1])
                        last.then_inc(quad_max, 1)
                    elif name == "MT":
                        dve.wait_ge(full, b.job(*s))
                        dve.tensor_copy(mT[:, g * P:(g + 1) * P], o[:, 0:P]).then_inc(free, 1)
                    elif name == "P":
                        dve.wait_ge(phigh, b.n(0, 4, 0, g + 1))
                        dve.tensor_tensor(ps[:, g % 2, 1, :, :], p32[:, g % 2, :, :], ps[:, g % 2, 0, :, :],
                                          ALU.subtract).then_inc(pready, 1)
                    elif name == "AV":
                        dve.wait_ge(full, b.job(*s))
                        link(dve.reciprocal(rden[:, :], o[:, N:2 * N]))
                        dve.tensor_tensor(o32[:, g % 2, :], o[:, 0:N], rden[:, :], ALU.mult)\
                           .then_inc(free, 1)
                    elif name == "OM":
                        dve.wait_ge(ohigh, b.n(0, 4, 0, g + 1))
                        dve.tensor_tensor(os_[:, 1, g, :], o32[:, g % 2, :], os_[:, 0, g, :], ALU.subtract)\
                           .then_inc(oready, 1)
                    elif name == "OUT":
                        dve.wait_ge(full, b.job(*s))
                        dve.scalar_tensor_tensor(pre2[:, g, :], o[:, :], 1.0 / W_SCALE, x1[:, g, :],
                                                 ALU.mult, ALU.add).then_inc(free, 1)
                    elif name == "R":
                        dve.wait_ge(full, b.job(*s))
                        dve.tensor_copy(lg[:, :, :], o[:, 0:NB * NX].rearrange("p (t n) -> p t n", t=NB))\
                           .then_inc(free, 1)
                        dve.wait_ge(free, b.job(*s))
                        own_wait(dve, taken)
                        for t in range(NB):
                            last = dve.max(top[:, t, :], lg[:, t, :])
                        link(last)
                        dve.tensor_scalar(rrow[:, :, 0:1], top[:, :, 0:1], -1.0 / W_SCALE, None, ALU.mult)\
                           .then_inc(rmax, 1)
                        for t in range(NB):
                            last = dve.max_index(topi[:, t, :], top[:, t, :], lg[:, t, :])
                        link(last)
                        link(dve.tensor_copy(topf[:, :, :], topi[:, :, :]))
                    elif name == "RC":
                        for t in range(NB):
                            last = dve.tensor_tensor(
                                hot[:, t, :, :], w["iota"][:, :].unsqueeze(1).to_broadcast([P, TOPK, NX]),
                                topf[:, t, 0:TOPK].unsqueeze(2).to_broadcast([P, TOPK, NX]), ALU.is_equal)
                        link(last)
                        for t in range(NB):
                            with nc.allow_low_precision(reason="the sum is 0 or 1"):
                                last = dve.tensor_reduce(
                                    chosen[:, t, :], hot[:, t, :, :].rearrange("p k e -> p e k"),
                                    axis=AX.X, op=ALU.add)
                        last.then_inc(chosen_ready, 1)
                    elif name == "RM":
                        dve.wait_ge(rec_used, b.n(0, 0, 1, 1))
                        dve.wait_ge(rexp, b.n(0, 0, 2 * NB, 2 * NB))
                        link(dve.reciprocal(rrow[:, :, 2:3], rrow[:, :, 1:2]))
                        for t in range(NB):
                            dve.tensor_scalar(rec[:, t, :, 1].bitcast(F32), etop[:, t, 0:TOPK], rrow[:, t, 2:3],
                                              1.0 / W_SCALE, ALU.mult, ALU.mult)
                            last = dve.tensor_copy(rec[:, t, :, 0], w["token"][:, t:t + 1].to_broadcast([P, TOPK]))
                        link(last)
                        link(dve.tensor_scalar(w["token"][:, :], w["token"][:, :], float(N), None, ALU.add))
                    elif name == "CT":
                        dve.wait_ge(full, b.job(*s))
                        count = o[:, 0:NB * NX].rearrange("p (t n) -> p t n", t=NB)
                        dve.tensor_scalar(over[:, :, :], count, float(CAP), NO_SLOT, ALU.is_ge, ALU.mult)
                        dve.tensor_tensor(slot[:, :, :], count,
                                          w["first"][:, :].unsqueeze(1).to_broadcast([P, NB, NX]),
                                          ALU.add).then_inc(free, 1)
                        link(dve.tensor_tensor(total[:, :], total[:, :], chosen[:, 0, :], ALU.add))
                        link(dve.tensor_tensor(total[:, :], total[:, :], chosen[:, 1, :], ALU.add))
                    elif name == "RS":
                        dve.wait_ge(free, b.job("CT", 0, 0))
                        link(dve.tensor_tensor(slot[:, :, :], slot[:, :, :], over[:, :, :], ALU.add))
                        for t in range(NB):
                            last = dve.tensor_tensor(hit[:, t, :, :], hot[:, t, :, :],
                                                     slot[:, t, :].unsqueeze(1).to_broadcast([P, TOPK, NX]),
                                                     ALU.mult)
                        link(last)
                        link(dve.tensor_reduce(slotk[:, :, :], hit[:, :, :, :], axis=AX.X, op=ALU.add))
                        dve.tensor_copy(sloti[:, :, :], slotk[:, :, :]).then_inc(rec_ready, 1)
                assert links[0] == LINKS_A * b.a + LINKS_B * b.b + LINKS_C * b.c + LINKS_LN * (b.a or b.b)

            bodies(dve, emit)


MOE = [
    ("WG", 0), ("WU", 0), ("SG", 0), ("SU", 0), ("WG", 1), ("SG", 1), ("X", 0), ("SU", 1), ("WU", 1),
    ("X", 1), ("G", 0), ("SHT", 0), ("SHT", 1), ("U", 0), ("WD", 0), ("G", 1), ("HT", 0), ("U", 1),
    ("D", 0), ("HT", 1), ("WD", 1), ("SD", 0), ("D", 1),
]
MOE_JOBS = {s: n for n, s in enumerate(x for x in MOE if not x[0].startswith("W"))}
MOE_BANK = [n % 8 for n in range(16)] + [6]
MOE_SPLITS = [s for s in MOE if s[0] in ("X", "HT", "SHT")]
MOE_GATES = [s for s in MOE if s[0] in ("G", "SG")]
MOE_UPS = [s for s in MOE if s[0] in ("U", "SU")]
MOE_WEIGHTS = [s for s in MOE if s[0].startswith("W")]
MOE_FREED = [s for u in MOE if not u[0].startswith("W") and u not in MOE_GATES
             for s in ([(u[0].replace("U", "G"), u[1]), u] if u in MOE_UPS else [u])]


def experts(nc, mem, ident, z, w_gate, w_up, w_down, x2_d, x2T_d, table_d, moe_d, shared_stage,
            sgT, suT, sdT):
    BODIES = T // P
    NJ = len(MOE_JOBS)
    HALF = FS // 2
    assert NX == 2 * BODIES and HALF <= 512 and len(MOE_BANK) == NJ
    shared = dict(SG=mem.sb("shared_gate", [P, 2, EC, FS], F16), SU=mem.sb("shared_up", [P, 2, EC, FS], F16),
                  SD=mem.sb("shared_down", [P, 2, SC6, E], F16))
    wf = dict(WG=mem.sb("gate_in", [P, 2, EC * F], F32), WU=mem.sb("up_in", [P, 2, EC * F], F32),
              WD=mem.sb("down_in", [P, 2, FC * E], F32))
    wh = dict(WG=mem.sb("w_gate_split", [P, 2, 2, EC * F], F16), WU=mem.sb("w_up_split", [P, 2, 2, EC * F], F16),
              WD=mem.sb("w_down_split", [P, 2, 2, FC * E], F16))
    records = mem.sb("records", [P, NX, 2], U32)
    gi = mem.sb("gather_index", [P, 2, 1], U32)
    si = mem.sb("scatter_index", [P, 2, 1], U32)
    xg = mem.sb("gathered", [P, 2, E], F32)
    xgs = mem.sb("gathered_T_split", [P, 2, 2, EC, P], F16)
    x2t = mem.sb("x2T_block", [P, 2, EC, P], F16)
    x2n = mem.sb("x2_block", [P, E], F32)
    silu32 = mem.sb("silu_out", [P, 2, F], F32)
    h32 = mem.sb("hidden", [P, 2, F], F32)
    hs = mem.sb("hidden_T_split", [P, 2, 2, FC, P], F16)
    ssilu32 = mem.sb("shared_silu", [P, FS], F32)
    sh32 = mem.sb("shared_hidden", [P, FS], F32)
    shs = mem.sb("shared_hidden_T_split", [P, 2, SC6, P], F16)
    d32 = mem.sb("expert_out", [P, 2, E], F32)
    banks = [mem.ps(f"moe_bank{n}", [P, 512], F32) for n in range(8)]

    shared_high, shared_low = mem.sem("shared_high"), mem.sem("shared_low")
    zero_rows = mem.sem("unused_down_rows_zero")
    sg_in, su_in, sd_in = mem.sem("shared_gate_in"), mem.sem("shared_up_in"), mem.sem("shared_down_in")
    records_in = mem.sem("records_in")
    w_in = {(k, s): mem.sem(f"{k}{s}_in") for k in wf for s in range(2)}
    w_high = mem.sem("expert_weight_high")
    w_low = mem.sem("expert_weight_low")
    x2t_in, x2n_in = mem.sem("x2T_in"), mem.sem("x2_in")
    index_ready = mem.sem("index_ready")
    gathered = [mem.sem(f"gathered{s}") for s in range(2)]
    full, high, free = mem.sem("moe_full"), mem.sem("moe_high"), mem.sem("moe_free")
    silu = mem.sem("silu_ready")
    prod = mem.sem("hidden_ready")
    added = mem.sem("expert_added")
    taken = mem.sem("waits_taken_3")

    def count(order, i, step):
        return i * len(order) + (order.index(step) + 1)

    def job(i, *step):
        return i * NJ + (MOE_JOBS[step] + 1)

    def freed(i, *step):
        return i * NJ + (MOE_FREED.index(step) + 1)

    def bank_of(step):
        return banks[MOE_BANK[MOE_JOBS[step]]]

    def reuse(eng, i, step, first):
        users = [s for s in MOE_JOBS if MOE_BANK[MOE_JOBS[s]] == MOE_BANK[MOE_JOBS[step]]]
        at = users.index(step)
        if at > 0:
            eng.wait_ge(free, freed(i, *users[at - 1]))
        elif not first:
            eng.wait_ge(free, i * NJ + (MOE_FREED.index(users[-1]) + 1 - NJ))

    def bodies(eng, emit):
        emit(0, True)
        with eng.Fori(1, BODIES) as i:
            emit(i, False)

    with nc.Block() as block:
        @block.sync
        def _(sp):
            sp.dma_start(records[:, :, :], table_d.rearrange("(e p) c -> p e c", p=CAP)).then_inc(records_in, 16)

            def emit(i, first):
                if first:
                    for name, a, loaded in (("SG", sgT, sg_in), ("SU", suT, su_in)):
                        sp.dma_start(shared_stage[name].rearrange("p (c n) -> p c n", c=EC),
                                     a.rearrange("(c p) n -> p c n", p=P)).then_inc(loaded, 16)
                for s in range(2):
                    e = 2 * i + s
                    if first and s == 1:
                        dst = shared_stage["SD"].rearrange("p (c n) -> p c n", c=SC6)
                        whole, own = (SC6 - 1) * P, FS - (SC6 - 1) * P
                        sp.dma_start(dst[:, 0:SC6 - 1, :], sdT[0:whole, :].rearrange("(c p) n -> p c n", p=P))\
                          .then_inc(sd_in, 16)
                        sp.dma_start(dst[P - own:P, SC6 - 1, :], sdT[whole:FS, :]).then_inc(sd_in, 16)
                    for k, a in (("WG", w_gate), ("WU", w_up)):
                        if not first:
                            sp.wait_ge(w_low, count(MOE_WEIGHTS, i - 1, (k, s)))
                        sp.dma_start(wf[k][:, s, :],
                                     a[bass.ds(e, 1), :, :].rearrange("o (p c) f -> p (o c f)", c=EC))\
                          .then_inc(w_in[k, s], 16)
                    if s == 0:
                        if not first:
                            sp.wait_ge(full, job(i - 1, "SU", 1))
                        sp.dma_start(x2t[:, :, :, :].rearrange("p a c n -> p (a c n)"),
                                     x2T_d[bass.ds(i, 1), :, :].rearrange("o p n -> p (o n)")).then_inc(x2t_in, 16)
                    if first:
                        sp.wait_ge(zero_rows, 1)
                    else:
                        sp.wait_ge(w_low, count(MOE_WEIGHTS, i - 1, ("WD", s)))
                    down = wf["WD"][:, s, :].rearrange("p (c n) -> p c n", c=FC)
                    sp.dma_start(down[:, 0:FC - 1, :],
                                 w_down[bass.ds(e, 1), 0:(FC - 1) * P, :].rearrange("o (c p) n -> p (o c) n", p=P))\
                      .then_inc(w_in["WD", s], 16)
                    sp.dma_start(down[FC * P - F:P, FC - 1, :],
                                 w_down[bass.ds(e, 1), (FC - 1) * P:F, :].rearrange("o p n -> p (o n)"))\
                      .then_inc(w_in["WD", s], 16)
                if not first:
                    sp.wait_ge(free, freed(i - 1, "SD", 0))
                sp.dma_start(x2n[:, :], x2_d[bass.ds(i * P, P), :]).then_inc(x2n_in, 16)

            bodies(sp, emit)

        @block.gpsimd
        def _(pool):
            def gather(i, first):
                for s in range(2):
                    if not first:
                        pool.wait_ge(gathered[s], 16 * i)
                        pool.wait_ge(full, job(i - 1, "X", s))
                        own_wait(pool, taken)
                    pool.tensor_copy(gi[:, s, :], records[:, bass.ds(2 * i + s, 1), 0]).then_inc(index_ready, 1)
                    pool.wait_ge(index_ready, (4 * i - 2 if not first else 0) + (s + 1))
                    own_wait(pool, taken)
                    pool.indirect_dma_start(xg[:, s, :], None, x2_d,
                                            bass.IndirectOffsetOnAxis(ap=gi[:, s, :], axis=0),
                                            bounds_check=T + CAP - 1).then_inc(gathered[s], 16)

            def add(i, first, gathers_after):
                for s in range(2):
                    pool.wait_ge(free, freed(i, "D", s))
                    if not (first and s == 0):
                        pool.wait_ge(added, 32 * i + 16 * s)
                    own_wait(pool, taken)
                    pool.tensor_copy(si[:, s, :], records[:, bass.ds(2 * i + s, 1), 0]).then_inc(index_ready, 1)
                    pool.wait_ge(index_ready, 4 * i + (2 + gathers_after + s + 1))
                    own_wait(pool, taken)
                    pool.indirect_dma_start(moe_d, bass.IndirectOffsetOnAxis(ap=si[:, s, :], axis=0),
                                            d32[:, s, :], None, bounds_check=T + CAP - 1,
                                            compute_op=ALU.add).then_inc(added, 16)

            pool.wait_ge(records_in, 16)
            gather(0, True)
            gather(1, False)
            add(0, True, 2)
            with pool.Fori(2, BODIES) as i:
                gather(i, False)
                add(i - 1, False, 2)
            add(BODIES - 1, False, 0)
            pool.wait_ge(added, 32 * BODIES)

        @block.tensor
        def _(pe):
            def product(out_, left, right, chunks):
                n = 0
                for c in range(chunks):
                    for a, b in PASSES:
                        last = pe.matmul(out_, left(a, c), right(b, c), start=(n == 0),
                                         stop=(n == 3 * chunks - 1))
                        n += 1
                return last

            def emit(i, first):
                for step in MOE:
                    name, s = step
                    if step not in MOE_JOBS:
                        continue
                    reuse(pe, i, step, first)
                    o = bank_of(step)
                    if name == "X":
                        pe.wait_ge(gathered[s], 16 * i + 16)
                        for c in range(EC):
                            last = pe.transpose(o[:, c * P:(c + 1) * P],
                                                xg[:, s, :].rearrange("p (q c) -> p c q", c=EC)[:, c, :],
                                                ident[:, :])
                    elif name in ("G", "U"):
                        pe.wait_ge(w_low, count(MOE_WEIGHTS, i, ("W" + name, s)))
                        if name == "G":
                            pe.wait_ge(free, freed(i, "X", s))
                        last = product(o[:, 0:F], lambda a, c: xgs[:, s, a, c, :],
                                       lambda b, c: wh["W" + name][:, s, b, c * F:(c + 1) * F], EC)
                    elif name in ("SG", "SU"):
                        if s == 0 and name == "SG":
                            pe.wait_ge(x2t_in, 16 * i + 16)
                        if first:
                            pe.wait_ge(shared_low, 1 if name == "SG" else 2)
                        last = product(o[:, 0:HALF], lambda a, c: x2t[:, a, c, :],
                                       lambda b, c: shared[name][:, b, c, s * HALF:(s + 1) * HALF], EC)
                    elif name == "HT":
                        pe.wait_ge(prod, count(MOE_UPS, i, ("U", s)))
                        for f in range(FC):
                            last = pe.transpose(o[:, f * P:(f + 1) * P], h32[:, s, F_START[f]:F_START[f] + P],
                                                ident[:, :])
                    elif name == "SHT":
                        pe.wait_ge(prod, count(MOE_UPS, i, ("SU", 1)))
                        for f in range(FC):
                            f0 = S_START[FC * s + f]
                            last = pe.transpose(o[:, f * P:(f + 1) * P], sh32[:, f0:f0 + P], ident[:, :])
                    elif name == "D":
                        pe.wait_ge(w_low, count(MOE_WEIGHTS, i, ("WD", s)))
                        pe.wait_ge(free, freed(i, "HT", s))
                        last = product(o[:, :], lambda a, f: hs[:, s, a, f, :],
                                       lambda b, f: wh["WD"][:, s, b, f * E:(f + 1) * E], FC)
                    elif name == "SD":
                        pe.wait_ge(free, freed(i, "SHT", 1))
                        if first:
                            pe.wait_ge(shared_low, 3)
                        last = product(o[:, :], lambda a, f: shs[:, a, f, :],
                                       lambda b, f: shared["SD"][:, b, f, :], SC6)
                    last.then_inc(full, 1)

            bodies(pe, emit)

        def halves(step):
            name, s = step
            if name == "X":
                return EC * P, lambda a: xgs[:, s, a, :, :].rearrange("p c n -> p (c n)")
            if name == "HT":
                return FC * P, lambda a: hs[:, s, a, :, :].rearrange("p f n -> p (f n)")
            return FC * P, lambda a: shs[:, a, FC * s:FC * (s + 1), :].rearrange("p f n -> p (f n)")

        def silu_of(name, s):
            return silu32[:, s, :] if name in ("G", "U") else ssilu32[:, s * HALF:(s + 1) * HALF]

        @block.scalar
        def _(act):
            def split_shared(name):
                act.activation(shared[name][:, 0, :, :].rearrange("p c n -> p (c n)"),
                               shared_stage[name], ACT.Copy, scale=W_SCALE).then_inc(shared_high, 1)

            act.wait_ge(sg_in, 16)
            split_shared("SG")

            def emit(i, first):
                for step in MOE:
                    name, s = step
                    if first and step == ("WD", 0):
                        act.wait_ge(sd_in, 32)
                        act.wait_ge(zero_rows, 1)
                        split_shared("SD")
                    if first and step == ("SU", 0):
                        act.wait_ge(su_in, 16)
                        split_shared("SU")
                    if step in MOE_SPLITS:
                        act.wait_ge(full, job(i, *step))
                        cols, half = halves(step)
                        act.activation(half(0), bank_of(step)[:, 0:cols], ACT.Copy).then_inc(high, 1)
                    elif name in wf:
                        act.wait_ge(w_in[name, s], (16 * i + 16) * (2 if name == "WD" else 1))
                        if not first:
                            act.wait_ge(full, job(i - 1, name[1], s))
                        act.activation(wh[name][:, s, 0, :], wf[name][:, s, :], ACT.Copy, scale=W_SCALE)\
                           .then_inc(w_high, 1)
                    elif step in MOE_GATES:
                        act.wait_ge(full, job(i, *step))
                        if not first:
                            act.wait_ge(prod, count(MOE_UPS, i - 1, ("U" if name == "G" else "SU", s)))
                        act.activation(silu_of(name, s), bank_of(step)[:, 0:F if name == "G" else HALF],
                                       ACT.Silu, scale=1.0 / W_SCALE).then_inc(silu, 1)

            bodies(act, emit)

        @block.vector
        def _(dve):
            dve.memset(shared_stage["SD"][0:SC6 * P - FS, (SC6 - 1) * E:SC6 * E], 0.0)
            for s in range(2):
                last = dve.memset(wf["WD"][0:FC * P - F, s, (FC - 1) * E:FC * E], 0.0)
            last.then_inc(zero_rows, 1)

            def split_shared(n, name):
                dve.wait_ge(shared_high, n + 1)
                dve.scalar_tensor_tensor(shared[name][:, 1, :, :].rearrange("p c n -> p (c n)"),
                                         shared_stage[name], W_SCALE,
                                         shared[name][:, 0, :, :].rearrange("p c n -> p (c n)"),
                                         ALU.mult, ALU.subtract).then_inc(shared_low, 1)
            split_shared(0, "SG")
            dve.wait_ge(records_in, 16)

            def emit(i, first):
                for step in MOE:
                    name, s = step
                    if first and step == ("SU", 0):
                        split_shared(1, "SU")
                    if first and step == ("WD", 0):
                        split_shared(2, "SD")
                    if first and name == "SD":
                        dve.wait_ge(shared_low, 3)
                    if step in MOE_SPLITS:
                        dve.wait_ge(high, count(MOE_SPLITS, i, step))
                        cols, half = halves(step)
                        dve.tensor_tensor(half(1), bank_of(step)[:, 0:cols], half(0), ALU.subtract)\
                           .then_inc(free, 1)
                    elif name in wf:
                        dve.wait_ge(w_high, count(MOE_WEIGHTS, i, step))
                        dve.scalar_tensor_tensor(wh[name][:, s, 1, :], wf[name][:, s, :], W_SCALE,
                                                 wh[name][:, s, 0, :], ALU.mult, ALU.subtract).then_inc(w_low, 1)
                    elif step in MOE_UPS:
                        dve.wait_ge(full, job(i, *step))
                        dve.wait_ge(silu, count(MOE_GATES, i, ("G" if name == "U" else "SG", s)))
                        dst = h32[:, s, :] if name == "U" else sh32[:, s * HALF:(s + 1) * HALF]
                        dve.scalar_tensor_tensor(dst, bank_of(step)[:, 0:F if name == "U" else HALF],
                                                 1.0 / W_SCALE, silu_of(name, s), ALU.mult, ALU.mult)\
                           .then_inc(prod, 1)
                        dve.wait_ge(prod, count(MOE_UPS, i, step))
                        dve.sem_inc(free, 2)
                    elif name == "D":
                        dve.wait_ge(full, job(i, *step))
                        if not first:
                            dve.wait_ge(added, 32 * i + (16 * s - 16))
                        dve.tensor_scalar(d32[:, s, :], bank_of(step)[:, :],
                                          records[:, bass.ds(2 * i + s, 1), 1].bitcast(F32), None, ALU.mult)\
                           .then_inc(free, 1)
                    elif name == "SD":
                        dve.wait_ge(full, job(i, *step))
                        dve.wait_ge(x2n_in, 16 * i + 16)
                        dve.scalar_tensor_tensor(z[:, bass.ds(i, 1), :].rearrange("p o n -> p (o n)"),
                                                 bank_of(step)[:, :], 1.0 / W_SCALE, x2n[:, :],
                                                 ALU.mult, ALU.add).then_inc(free, 1)

            bodies(dve, emit)


def finish(nc, mem, moe_d, z, out):
    R = 4
    TILES = T // (P * R)
    a = mem.sb("expert_rows", [P, 2, R, E], F32)
    r = mem.sb("summed", [P, 2, R, E], F32)
    o = mem.sb("out_rows", [P, 2, R, E], F32)
    stats = mem.sb("final_stats", [P, 2, R, 6], F32)
    mv = mem.sb("final_mean_var", [P, 2, R, 2], F32)
    sc = mem.sb("final_scale_shift", [P, 2, 2, R], F32)
    root_tmp = mem.sb("final_root_tmp", [P, 3, R], F32)
    loaded = [mem.sem(f"rows_loaded{s}") for s in range(2)]
    summed, scaled, normed = mem.sem("summed"), mem.sem("row_scales"), mem.sem("normed")
    stored = [mem.sem(f"rows_stored{s}") for s in range(2)]
    step = mem.sem("final_step")

    def rows(d, n):
        return d[n * P * R:(n + 1) * P * R, :].rearrange("(r p) n -> p r n", r=R)

    with nc.Block() as block:
        @block.sync
        def _(sp):
            for n in range(TILES):
                if n >= 2:
                    sp.wait_ge(summed, n - 1)
                sp.dma_start(a[:, n % 2], rows(moe_d, n)).then_inc(loaded[n % 2], 16)

        @block.vector
        def _(dve):
            links = [0]

            def link(ins):
                ins.then_inc(step, 1)
                links[0] += 1
                dve.wait_ge(step, links[0])

            for n in range(TILES):
                s = n % 2
                dve.wait_ge(loaded[s], 16 * (n // 2 + 1))
                if n >= 2:
                    dve.wait_ge(normed, n - 1)
                dve.tensor_tensor(r[:, s], a[:, s], z[:, n * R:(n + 1) * R, :], ALU.add).then_inc(summed, 1)
                dve.wait_ge(summed, n + 1)
                for k in range(R):
                    last = dve.bn_stats(stats[:, s, k, :], r[:, s, k, :])
                link(last)
                for k in range(R):
                    last = dve.bn_aggr(mv[:, s, k, :], stats[:, s, k, :])
                link(last)
                inverse_root(dve, link, sc[:, s, 0, :], mv[:, s, :, 1], root_tmp)
                link(dve.scalar_tensor_tensor(sc[:, s, 1, :], mv[:, s, :, 0], -1.0, sc[:, s, 0, :],
                                              ALU.mult, ALU.mult))
                dve.sem_inc(scaled, 1)

        @block.scalar
        def _(act):
            for n in range(TILES):
                s = n % 2
                act.wait_ge(scaled, n + 1)
                if n >= 2:
                    act.wait_ge(stored[s], 16 * (n // 2))
                for k in range(R):
                    last = act.activation(o[:, s, k, :], r[:, s, k, :], ACT.Identity, scale=sc[:, s, 0, k:k + 1],
                                          bias=sc[:, s, 1, k:k + 1])
                last.then_inc(normed, 1)
                act.wait_ge(normed, n + 1)
                act.dma_start(rows(out, n), o[:, s]).then_inc(stored[s], 16)
            for s in range(2):
                act.wait_ge(stored[s], 16 * ((TILES + 1 - s) // 2))


def kernel(x, ctx_512, L0_attn_Wq, L0_attn_Wk, L0_attn_Wv, L0_attn_fc_w, L0_attn_fc_b, L0_xattn_Wq,
           L0_xattn_Wkv_expand, L0_xattn_Wout, L0_ffn_gate_w, L0_ffn_w_gate, L0_ffn_w_up, L0_ffn_w_down,
           L0_ffn_sh_gate, L0_ffn_sh_up, L0_ffn_sh_down):
    import numpy as np
    import concourse.bacc as bacc
    from concourse.bass_utils import run_bass_kernel_spmd

    def rows(a):
        return np.ascontiguousarray(a)

    flat = np.asarray(x).reshape(T, E)
    arrays = {
        "x": rows(flat), "xT": rows(flat.T), "ctxT": rows(np.asarray(ctx_512).reshape(T, L).T),
        "wq": rows(L0_attn_Wq), "wk": rows(L0_attn_Wk), "wv": rows(L0_attn_Wv),
        "fcT": rows(np.asarray(L0_attn_fc_w).T), "fcb": rows(L0_attn_fc_b),
        "xwqT": rows(np.asarray(L0_xattn_Wq).T), "wkvT": rows(np.asarray(L0_xattn_Wkv_expand).T),
        "woutT": rows(np.asarray(L0_xattn_Wout).T), "gateT": rows(np.asarray(L0_ffn_gate_w).T),
        "w_gate": rows(L0_ffn_w_gate), "w_up": rows(L0_ffn_w_up), "w_down": rows(L0_ffn_w_down),
        "sgT": rows(np.asarray(L0_ffn_sh_gate).T), "suT": rows(np.asarray(L0_ffn_sh_up).T),
        "sdT": rows(np.asarray(L0_ffn_sh_down).T),
    }
    nc = bacc.Bacc("TRN2", target_bir_lowering=False, num_devices=1)
    args = [nc.dram_tensor(f"in_{k}", a.shape, mybir.dt.from_np(a.dtype), kind="ExternalInput").ap()
            for k, a in arrays.items()]
    out = nc.dram_tensor("out_rows_dram", (T, E), F32, kind="ExternalOutput").ap()
    build(nc, *args, out)
    r = run_bass_kernel_spmd(nc, [{f"in_{k}": a for k, a in arrays.items()}], core_ids=[0])
    return r.results[0]["out_rows_dram"].reshape(B, N, E)
```

```python
import math
from contextlib import ExitStack

import concourse.bass as bass
from concourse import mybir

F32 = mybir.dt.float32
F16 = mybir.dt.float16
U32 = mybir.dt.uint32
ALU = mybir.AluOpType
ACT = mybir.ActivationFunctionType
AX = mybir.AxisListType

P = 128
B, N, E = 16, 256, 512
T = B * N
H = 3
NH, HD, L = 16, 32, 128
NX, F, TOPK, CAP = 64, 352, 6, 128
FS = 2 * F
EC = E // P
NB = N // P
FC = 3
F_START = [0, P, F - P]
SC6 = 6
S_START = [0, P, 2 * P, 3 * P, 4 * P, FS - P]
EPS = 1e-5
W_SCALE = 64.0
SLOTS = NX * CAP
DUMMY = T
NO_SLOT = 16384.0
PASSES = [(0, 0), (0, 1), (1, 0)]


class Memory:

    def __init__(self, nc, stack):
        self.nc, self.stack = nc, stack

    def sb(self, name, shape, dt):
        return self.stack.enter_context(self.nc.sbuf_tensor(name, shape, dt))

    def ps(self, name, shape, dt):
        return self.stack.enter_context(self.nc.psum_tensor(name, shape, dt))

    def sem(self, name):
        return self.nc.alloc_semaphore(name)


class Loads:

    def __init__(self, m, wf, weights, stage, shared):
        self.wf, self.weights, self.stage, self.shared = wf, weights, stage, shared
        self.w_in = {(k, s): m.sem(f"{k}{s}_in") for k in wf for s in range(2)}
        self.shared_in = {k: m.sem(f"{k}_in") for k in ("SG", "SU", "SD")}

    def shared_half(self, sp, name):
        sp.dma_start(self.stage[name].rearrange("p (c n) -> p c n", c=EC),
                     self.shared[name].rearrange("(c p) n -> p c n", p=P)).then_inc(self.shared_in[name], 16)

    def projection(self, sp, name, e, s):
        sp.dma_start(self.wf[name][:, s, :],
                     self.weights[name][bass.ds(e, 1), :, :].rearrange("o (p c) f -> p (o c f)", c=EC))\
          .then_inc(self.w_in[name, s], 16)

    def down(self, sp, e, s):
        to, w_down = self.wf["WD"][:, s, :].rearrange("p (c n) -> p c n", c=FC), self.weights["WD"]
        sp.dma_start(to[:, 0:FC - 1, :],
                     w_down[bass.ds(e, 1), 0:(FC - 1) * P, :].rearrange("o (c p) n -> p (o c) n", p=P))\
          .then_inc(self.w_in["WD", s], 16)
        sp.dma_start(to[FC * P - F:P, FC - 1, :],
                     w_down[bass.ds(e, 1), (FC - 1) * P:F, :].rearrange("o p n -> p (o n)"))\
          .then_inc(self.w_in["WD", s], 16)


class Table:

    def __init__(self, m, table_d):
        self.dram = table_d
        self.slot = m.sb("slot_of_choice", [P, NB, TOPK], U32)
        self.record = m.sb("table_records", [P, NB, TOPK, 2], U32)
        self.ready = m.sem("records_ready")
        self.scattered = m.sem("records_scattered")

    def scatter(self, pool, first, end):
        for tb, c in [(tb, c) for tb in range(NB) for c in range(TOPK)][first:end]:
            pool.indirect_dma_start(
                self.dram, bass.IndirectOffsetOnAxis(ap=self.slot[:, tb, c:c + 1], axis=0),
                self.record[:, tb, c, :], None, bounds_check=SLOTS - 1, oob_is_err=False)\
                .then_inc(self.scattered, 16)


def own_wait(eng, taken):
    eng.sem_inc(taken, 1)


def inverse_root(dve, link, out, variance, tmp):
    v, bits, t = tmp[:, 0], tmp[:, 1], tmp[:, 2]
    link(dve.tensor_scalar(v, variance, EPS, None, ALU.add))
    link(dve.tensor_scalar(bits.bitcast(U32), v.bitcast(U32), 1, None, ALU.logical_shift_right))
    link(dve.tensor_scalar(out.bitcast(U32), bits.bitcast(U32), -1.0, float(0x5F3759DF), ALU.mult, ALU.add))
    for _ in range(3):
        link(dve.tensor_tensor(t, out, out, ALU.mult))
        link(dve.scalar_tensor_tensor(t, t, -0.5, v, ALU.mult, ALU.mult))
        link(dve.scalar_tensor_tensor(out, t, 1.5, out, ALU.add, ALU.mult))


def build(nc, x, xT, ctxT, wq, wk, wv, fcT, fcb, xwqT, wkvT, woutT, gateT, w_gate, w_up, w_down,
          sgT, suT, sdT, out):
    x2_d = nc.dram_tensor("x2_rows", (T + CAP, E), F32).ap()
    x2T_d = nc.dram_tensor("x2_transposed", (T // P, P, 2 * EC * P), F16).ap()
    table_d = nc.dram_tensor("slot_table", (SLOTS, 2), U32).ap()
    moe_d = nc.dram_tensor("expert_sums", (T + CAP, E), F32).ap()
    with ExitStack() as outer:
        m = Memory(nc, outer)
        ident = m.sb("ident", [P, P], F32)
        z = m.sb("x2_plus_shared", [P, T // P, E], F32)
        z_cols = z[:, :, :].rearrange("p t n -> p (t n)")
        stage, col = {}, T // P * E
        for name, cols in (("SU", EC * FS), ("SD", SC6 * E)):
            stage[name] = z_cols[:, col - cols:col]
            col -= cols
        AM = H * EC * E
        am = m.sb("attention_then_expert_weights", [P, 2 * AM], F32)
        wf, col = {}, 0
        for name, cols in (("WG", EC * F), ("WU", EC * F), ("WD", FC * E)):
            wf[name] = am[:, col:col + 2 * cols].rearrange("p (s n) -> p s n", s=2)
            col += 2 * cols
        stage["SG"] = am[:, col:col + EC * FS]
        stage["rest"] = am[:, col + EC * FS:2 * AM]
        table = Table(m, table_d)
        loads = Loads(m, wf, dict(WG=w_gate, WU=w_up, WD=w_down), stage, dict(SG=sgT, SU=suT))
        with ExitStack() as s:
            mem = Memory(nc, s)
            w = dict(
                A=am[:, 0:AM].bitcast(F16).rearrange("p (a h c n) -> p a h c n", a=2, h=H, c=EC),
                M=am[:, AM:2 * AM].bitcast(F16).rearrange("p (a h c n) -> p a h c n", a=2, h=H, c=EC),
                xwq=mem.sb("xwq_split", [P, 2, EC, E], F16),
                wkv=mem.sb("wkv_split", [P, 2, 2 * E], F16),
                wout=mem.sb("wout_split", [P, 2, EC, E], F16),
                gate=mem.sb("gate_split", [P, 2, EC, NX], F16),
                bias=mem.sb("bias_rows", [P, E], F32),
                causal=mem.sb("causal_penalty", [P, N], F32),
                pick=mem.sb("pick_head", [P, EC, P], F16),
                ones=mem.sb("ones", [P, P], F16),
                before=mem.sb("earlier_tokens", [P, P], F16),
                iota=mem.sb("expert_numbers", [P, NX], F32),
                first=mem.sb("first_slots", [P, NX], F32),
                token=mem.sb("token_numbers", [P, NB], F32),
                empty=mem.sb("empty_slots", [P, NX, 2], U32),
                zeros=mem.sb("zero_rows", [P, 2 * E], F32),
                xT_in=mem.sb("xT_in", [P, EC, N], F32),
                xs=mem.sb("xT_split", [P, 2, EC, N], F16),
                xT_loaded=mem.sem("xT_loaded"), xT_split=mem.sem("xT_split_done"), xfer=mem.sem("pool_high_half"),
            )
            with ExitStack() as t:
                prepare(nc, Memory(nc, t), ident, w, z_cols, xT, wq, wk, wv, fcT, fcb, xwqT, wkvT, woutT, gateT)
            with ExitStack() as t:
                attend(nc, Memory(nc, t), ident, w, z_cols, x, xT, ctxT, x2_d, x2T_d, table_d, moe_d,
                       loads, table)
        with ExitStack() as s:
            experts(nc, Memory(nc, s), ident, z, loads, table, x2_d, x2T_d, table_d, moe_d, sdT)
        with ExitStack() as s:
            finish(nc, Memory(nc, s), moe_d, z, out)


def prepare(nc, mem, ident, w, z_cols, xT, wq, wk, wv, fcT, fcb, xwqT, wkvT, woutT, gateT):
    NSTAGE = 4
    stage = z_cols[:, 0:NSTAGE * EC * E].rearrange("p (k n) -> p k n", k=NSTAGE)
    empty_id = mem.sb("empty_ids", [P, NX], F32)
    qs = mem.sb("wq_split", [P, 2, H, EC, E], F16)
    ks = mem.sb("wk_split", [P, 2, H, EC, E], F16)
    at_col = NSTAGE * EC * E
    vs = z_cols[:, at_col:at_col + H * EC * E].bitcast(F16)\
        .rearrange("p (a h c n) -> p a h c n", a=2, h=H, c=EC)
    fs = z_cols[:, at_col + H * EC * E:at_col + (H + 1) * EC * E].bitcast(F16)\
        .rearrange("p (a c n) -> p a c n", a=2, c=EC)
    bank = [mem.ps(f"fold{k}", [P, E], F32) for k in range(4)]

    def rows(a):
        return a.rearrange("(c p) n -> p c n", p=P)

    items = [(rows(fcT), lambda k: fs[:, k, :, :], EC * E)]
    for h in range(H):
        items.append((rows(wv[h]), lambda k, h=h: vs[:, k, h, :, :], EC * E))
        items.append((rows(wq[h]), lambda k, h=h: qs[:, k, h, :, :], EC * E))
        items.append((rows(wk[h]), lambda k, h=h: ks[:, k, h, :, :], EC * E))
    items.append((rows(xwqT), lambda k: w["xwq"][:, k, :, :], EC * E))
    items.append((rows(woutT), lambda k: w["wout"][:, k, :, :], EC * E))
    items.append((rows(wkvT), lambda k: w["wkv"][:, k, :].rearrange("p (c n) -> p c n", c=1), 2 * E))
    items.append((rows(gateT), lambda k: w["gate"][:, k, :, :], EC * NX))
    folds = [(kind, h, c) for h in range(H) for kind in ("M", "A") for c in range(EC)]

    def operands_split(kind, h):
        return 2 + 3 * h if kind == "M" else 4 + 3 * h

    staged = [mem.sem(f"staged{k}") for k in range(NSTAGE)]
    high = mem.sem("weight_high_half")
    low = mem.sem("weight_low_half")
    folded = mem.sem("folded")
    fold_high = mem.sem("fold_high_half")
    fold_low = mem.sem("fold_low_half")
    const = mem.sem("constants")
    bias_in = mem.sem("bias_loaded")

    def at(n):
        src, dst, cols = items[n]
        st = stage[:, n % NSTAGE, 0:cols]
        return st.rearrange("p (c n) -> p c n", c=src.shape[1]), dst

    with nc.Block() as block:
        @block.sync
        def _(sp):
            for n in range(len(items)):
                if n >= NSTAGE:
                    sp.wait_ge(low, n - NSTAGE + 1)
                sp.dma_start(at(n)[0], items[n][0]).then_inc(staged[n % NSTAGE], 16)
            sp.dma_start(w["xT_in"][:, :, :], xT.rearrange("(c p) t -> p c t", p=P)[:, :, 0:N])\
              .then_inc(w["xT_loaded"], 16)
            sp.dma_start(w["bias"][:, :], fcb.rearrange("(a n) -> a n", a=1).broadcast_to([P, E]))\
              .then_inc(bias_in, 16)
            sp.wait_ge(bias_in, 16)

        @block.gpsimd
        def _(pool):
            step = mem.sem("pool_const_step")
            done = [0]

            def then_wait(ins):
                ins.then_inc(step, 1)
                done[0] += 1
                pool.wait_ge(step, done[0])

            then_wait(pool.memset(ident[:, :], 0.0))
            pool.affine_select(out=ident[:, :], in_=ident[:, :], compare_op=ALU.not_equal, fill=1.0,
                               base=0, pattern=[[-1, P]], channel_multiplier=1).then_inc(const, 1)
            pool.memset(w["zeros"][:, :], 0.0).then_inc(const, 1)
            then_wait(pool.memset(w["causal"][:, :], 0.0))
            pool.affine_select(out=w["causal"][:, P:N], in_=w["causal"][:, P:N], compare_op=ALU.is_ge,
                               fill=-1e30, base=0, pattern=[[-1, P]], channel_multiplier=1)\
                .then_inc(const, 1)
            then_wait(pool.memset(w["pick"][:, :, :], 0.0))
            for r in range(4):
                then_wait(pool.affine_select(
                    out=w["pick"][:, :, :], in_=w["pick"][:, :, :], compare_op=ALU.not_equal, fill=-1.0,
                    base=-32 * r, pattern=[[-1, EC], [0, P]], channel_multiplier=1))
            pool.memset(w["ones"][:, :], 1.0).then_inc(const, 1)
            then_wait(pool.memset(w["before"][:, :], 0.0))
            pool.affine_select(out=w["before"][:, :], in_=w["before"][:, :], compare_op=ALU.is_ge,
                               fill=1.0, base=0, pattern=[[-1, P]], channel_multiplier=1).then_inc(const, 1)
            pool.iota(w["iota"][:, :], pattern=[[1, NX]], base=0, channel_multiplier=0,
                      allow_small_or_imprecise_dtypes=True).then_inc(const, 1)
            pool.iota(w["first"][:, :], pattern=[[CAP, NX]], base=0, channel_multiplier=0,
                      allow_small_or_imprecise_dtypes=True).then_inc(const, 1)
            pool.iota(w["token"][:, :], pattern=[[P, NB]], base=0, channel_multiplier=1,
                      allow_small_or_imprecise_dtypes=True).then_inc(const, 1)
            then_wait(pool.iota(empty_id[:, :], pattern=[[0, NX]], base=DUMMY, channel_multiplier=1,
                                allow_small_or_imprecise_dtypes=True))
            then_wait(pool.memset(w["empty"][:, :, :].bitcast(F32), 0.0))
            pool.tensor_copy(w["empty"][:, :, 0], empty_id[:, :]).then_inc(const, 1)
            pool.wait_ge(const, 9)
            pool.wait_ge(w["xT_loaded"], 16)
            pool.tensor_copy(w["xs"][:, 0, :, :], w["xT_in"][:, :, :]).then_inc(w["xfer"], 1)
            pool.wait_ge(w["xfer"], 1)
            pool.tensor_tensor(w["xs"][:, 1, :, :], w["xT_in"][:, :, :], w["xs"][:, 0, :, :], ALU.subtract)\
                .then_inc(w["xT_split"], 1)
            pool.wait_ge(w["xT_split"], 1)

        @block.scalar
        def _(act):
            def split(n):
                act.wait_ge(staged[n % NSTAGE], 16 * (n // NSTAGE + 1))
                src, dst = at(n)
                act.activation(dst(0), src, ACT.Copy, scale=W_SCALE).then_inc(high, 1)

            n = 0
            for j, (kind, h, c) in enumerate(folds):
                while n < min(len(items), operands_split(kind, h) + (c + 2) // 2):
                    split(n)
                    n += 1
                act.wait_ge(folded, j + 1)
                act.activation(w[kind][:, 0, h, c, :], bank[j % 4][:, :], ACT.Copy,
                               scale=1.0 / W_SCALE ** 2).then_inc(fold_high, 1)
            while n < len(items):
                split(n)
                n += 1
            act.wait_ge(high, len(items))
            act.wait_ge(fold_high, len(folds))

        @block.vector
        def _(dve):
            def split(n):
                dve.wait_ge(high, n + 1)
                src, dst = at(n)
                dve.scalar_tensor_tensor(dst(1), src, W_SCALE, dst(0), ALU.mult, ALU.subtract)\
                   .then_inc(low, 1)

            n = 0
            for j, (kind, h, c) in enumerate(folds):
                while n < min(len(items), operands_split(kind, h) + (c + 2) // 2):
                    split(n)
                    n += 1
                dve.wait_ge(fold_high, j + 1)
                dve.scalar_tensor_tensor(w[kind][:, 1, h, c, :], bank[j % 4][:, :], 1.0 / W_SCALE ** 2,
                                         w[kind][:, 0, h, c, :], ALU.mult, ALU.subtract)\
                   .then_inc(fold_low, 1)
            while n < len(items):
                split(n)
                n += 1
            dve.wait_ge(low, len(items))
            dve.wait_ge(fold_low, len(folds))

        @block.tensor
        def _(pe):
            for j, (kind, h, c) in enumerate(folds):
                pe.wait_ge(low, operands_split(kind, h))
                if j >= 4:
                    pe.wait_ge(fold_low, j - 3)
                left = (vs if kind == "M" else qs)
                right = fs if kind == "M" else ks
                k = 0
                for d in range(EC):
                    for a, b in PASSES:
                        moving = right[:, b, d, :] if kind == "M" else right[:, b, h, d, :]
                        last = pe.matmul(bank[j % 4][:, :], left[:, a, h, d, c * P:(c + 1) * P], moving,
                                         start=(k == 0), stop=(k == 3 * EC - 1))
                        k += 1
                last.then_inc(folded, 1)


BODY = [
    ("Y", 0, 0), ("Y", 0, 1), ("V", 0, 0), ("V", 0, 1), ("T", 0, 0), ("T", 1, 0), ("K", 0, 0),
    ("K", 1, 0), ("TX", 0, 0), ("TX", 1, 0), ("Q", 0, 0), ("Q", 1, 0), ("R", 0, 0), ("C", 0, 0),
    ("C", 1, 0), ("M", 0, 0), ("V", 1, 0), ("S", 0, 0), ("S", 0, 1), ("M", 1, 0), ("S1", 0, 0),
    ("Y", 1, 0), ("M", 2, 0), ("Y", 1, 1), ("M", 3, 0), ("S2", 0, 0), ("S", 1, 0), ("S", 1, 1),
    ("S1", 1, 0), ("V", 1, 1), ("MT", 0, 0), ("MT", 1, 0), ("Y", 2, 0), ("ST", 0, 0), ("RC", 0, 0),
    ("S2", 1, 0), ("Y", 2, 1), ("P", 0, 0), ("CT", 0, 0), ("RM", 0, 0), ("ST", 1, 0), ("RS", 0, 0),
    ("P", 1, 0), ("V", 2, 0), ("AV", 0, 0), ("ST", 2, 0), ("OM", 0, 0), ("S", 2, 0), ("S", 2, 1),
    ("S1", 2, 0), ("AV", 1, 0), ("P", 2, 0), ("ST", 3, 0), ("V", 2, 1), ("S2", 2, 0), ("OM", 1, 0),
    ("P", 3, 0), ("AV", 2, 0), ("OM", 2, 0), ("O", 0, 0), ("AV", 3, 0), ("OM", 3, 0), ("O", 1, 0),
    ("OUT", 0, 0), ("OUT", 1, 0), ("LN", 0, 0),
]
A_STEPS = {"Y", "V", "S", "S1", "S2", "O"}
X_READER = [s for s in BODY if s[0] in ("Y", "V", "S")][-1]
C_STEPS = {"TX", "R", "RC", "RM", "CT", "RS"}
RING_STEPS = {"Y", "V", "S", "O", "T", "Q", "K", "C", "MT", "AV", "OUT", "TX", "R", "CT"}
SPLIT_STEPS = {"Y", "V", "T", "Q", "K", "C", "TX"}
RING = 4
RING_A, RING_B, RING_C = 20, 16, 4
LINKS_A, LINKS_B, LINKS_C, LINKS_LN = 6, 4, 12, 14


def done_before(i, per_a, per_b=0, per_c=0):
    if isinstance(i, int):
        return per_a * min(i, B) + per_b * min(max(i - 1, 0), B) + per_c * min(max(i - 2, 0), B)
    return i * (per_a + per_b + per_c) - (per_b + 2 * per_c)


def attend(nc, mem, ident, w, spare, x, xT, ctxT, x2_d, x2T_d, table_d, moe_d, loads, table):
    x_in = mem.sb("x_in", [P, NB, E], F32)
    xT_in, xs = w["xT_in"], w["xs"]
    xT_loaded, xT_split, xfer = w["xT_loaded"], w["xT_split"], w["xfer"]
    c_in = mem.sb("ctx_in", [P, N], F32)
    xb = mem.sb("x_plus_bias", [P, NB, E], F32)
    cs = mem.sb("ctx_split", [P, 2, N], F16)
    e32 = mem.sb("exp_scores", [P, NB, N], F32)
    ws = mem.sb("weights_split", [P, 2, H, NB, N], F16)
    srow = mem.sb("score_rows", [P, NB, 4], F32)
    pre = mem.sb("pre_norm", [P, NB, E], F32)
    stats = mem.sb("stats", [P, 2 * NB, 6], F32)
    mv = mem.sb("mean_var", [P, 2 * NB, 2], F32)
    rstd = mem.sb("rstd", [P, 2 * NB], F32)
    root_tmp = mem.sb("root_tmp", [P, 3, 2 * NB], F32)
    x1 = mem.sb("x1", [P, NB, E], F32)
    x1s = mem.sb("x1T_split", [P, 2, EC, N], F16)
    q = mem.sb("q_split", [P, 2, EC, N], F16)
    k = mem.sb("k_split", [P, 2, EC, N], F16)
    cv = mem.sb("cv_split", [P, 2, NB, E], F16)
    mx = mem.sb("maxima", [P, NB, P], F32)
    mT = mem.sb("maxima_T", [P, N], F16)
    at_col = [0]

    def spare_cols(n):
        at_col[0] += n
        return spare[:, at_col[0] - n:at_col[0]]

    p32 = spare_cols(2 * 4 * (N + P)).rearrange("p (s r n) -> p s r n", s=2, r=4)
    ps = spare_cols(2 * 4 * (N + P)).bitcast(F16).rearrange("p (s a r n) -> p s a r n", s=2, a=2, r=4)
    v = spare[:, T // P * E - H * NB * E:T // P * E].bitcast(F16).rearrange("p (a h t n) -> p a h t n", a=2, h=H, t=NB)
    os_ = spare_cols(EC * N).bitcast(F16).rearrange("p (a c n) -> p a c n", a=2, c=EC)
    x2s = spare_cols(NB * EC * P).bitcast(F16).rearrange("p (t a c n) -> p t a c n", t=NB, a=2, c=EC)
    hot = spare_cols(NB * TOPK * NX).rearrange("p (t k n) -> p t k n", t=NB, k=TOPK)
    hit = spare_cols(NB * TOPK * NX).rearrange("p (t k n) -> p t k n", t=NB, k=TOPK)
    y = spare_cols(EC * N).bitcast(F16).rearrange("p (a c n) -> p a c n", a=2, c=EC)
    pre2 = spare_cols(NB * E).rearrange("p (t n) -> p t n", t=NB)
    x2 = spare_cols(NB * E).rearrange("p (t n) -> p t n", t=NB)
    rden = mem.sb("inv_denominator", [P, N], F32)
    o32 = mem.sb("cross_out", [P, 2, N], F32)
    lg = mem.sb("logits", [P, NB, NX], F32)
    ex = mem.sb("exp_logits", [P, NB, NX], F32)
    top = mem.sb("top8", [P, NB, 8], F32)
    topi = mem.sb("top8_index", [P, NB, 8], U32)
    topf = mem.sb("top8_index_float", [P, NB, 8], F32)
    etop = mem.sb("exp_top8", [P, NB, 8], F32)
    rrow = mem.sb("router_rows", [P, NB, 4], F32)
    chosen = mem.sb("chosen", [P, NB, NX], F16)
    total = mem.sb("chosen_before", [P, NX], F16)
    over = mem.sb("over_capacity", [P, NB, NX], F32)
    slot = mem.sb("slots", [P, NB, NX], F32)
    slotk = mem.sb("slot_of_choice_float", [P, NB, TOPK], F32)
    sloti, rec, rec_ready, scattered = table.slot, table.record, table.ready, table.scattered
    bank = [mem.ps(f"ring{n}", [P, 512], F32) for n in range(RING)]
    quad = mem.ps("quad", [P, 4, 512], F32)

    ctx_loaded, x_loaded = mem.sem("ctx_loaded"), mem.sem("x_loaded")
    ctx_split_, xb_ready = mem.sem("ctx_split_done"), mem.sem("xb_ready")
    full = mem.sem("ring_full")
    high = mem.sem("ring_high_half")
    free = mem.sem("ring_free")
    smax = mem.sem("score_max")
    sexp = mem.sem("score_exp")
    whigh = mem.sem("attention_weight_high")
    wready = mem.sem("attention_weights_ready")
    ln1, ln2 = mem.sem("x1_ready"), mem.sem("x2_ready")
    quad_full = mem.sem("quad_full")
    quad_max = mem.sem("quad_max")
    pexp = mem.sem("quad_exp")
    pmask = mem.sem("causal_masked")
    phigh = mem.sem("p_high_half")
    pready = mem.sem("p_ready")
    ohigh = mem.sem("cross_out_high")
    oready = mem.sem("cross_out_ready")
    x2_stored, x2T_stored = mem.sem("x2_stored"), mem.sem("x2T_stored")
    filled, slots_empty = mem.sem("dram_filled"), mem.sem("slots_empty")
    rmax, rexp = mem.sem("router_max"), mem.sem("router_exp")
    chosen_ready = mem.sem("chosen_ready")
    rec_used = mem.sem("records_used")
    dve_step = mem.sem("dve_step")
    taken = mem.sem("waits_taken")

    FULL = lambda steps: {s: n for n, s in enumerate(x for x in steps if x[0] in RING_STEPS)}
    SPLIT = lambda steps: {s: n for n, s in enumerate(x for x in steps if x[0] in SPLIT_STEPS)}

    class Body:

        def __init__(self, i):
            self.i = i
            self.a = not (isinstance(i, int) and i >= B)
            self.b = not (isinstance(i, int) and not 1 <= i <= B)
            self.c = not (isinstance(i, int) and i < 2)
            self.steps = [s for s in BODY if
                          (self.a if s[0] in A_STEPS else self.c if s[0] in C_STEPS else
                           self.a or self.b if s[0] == "LN" else self.b)]
            self.ring, self.split = FULL(self.steps), SPLIT(self.steps)

        def is_(self, i):
            return isinstance(self.i, int) and self.i == i

        def job(self, *step):
            return done_before(self.i, RING_A, RING_B, RING_C) + (self.ring[step] + 1)

        def last_job(self, *step):
            steps = [s for s in BODY if s in FULL(BODY) and (s[0] in A_STEPS or not self.is_(1))]
            after = len(steps) - 1 - steps.index(step)
            return done_before(self.i, RING_A, RING_B, RING_C) - after

        def high(self, *step):
            return done_before(self.i, 12, 8, 2) + (self.split[step] + 1)

        def n(self, per_a, per_b, per_c, extra):
            return done_before(self.i, per_a, per_b, per_c) + extra

        def bank(self, *step):
            return bank[self.ring[step] % RING]

        def reuse(self, eng, *step):
            j = self.ring[step]
            if not (self.is_(0) and j < RING):
                eng.wait_ge(free, done_before(self.i, RING_A, RING_B, RING_C) + (j - RING + 1))

    def bodies(eng, emit):
        emit(Body(0))
        emit(Body(1))
        with eng.Fori(2, B) as i:
            emit(Body(i))
        emit(Body(B))
        emit(Body(B + 1))

    x_d = x.rearrange("(t p) e -> p t e", p=P)
    xT_d = xT.rearrange("(c p) t -> p c t", p=P)

    with nc.Block() as block:
        @block.sync
        def _(sp):
            def fills():
                sp.dma_start(table_d.rearrange("(e p) c -> p e c", p=CAP), w["empty"][:, :, :])\
                  .then_inc(slots_empty, 16)
                n = 0
                for r in range(0, T, 2 * P):
                    sp.dma_start(moe_d[r:r + 2 * P, :].rearrange("(p r) n -> p (r n)", r=2), w["zeros"][:, :])\
                      .then_inc(filled, 16)
                    n += 1
                for d in (moe_d, x2_d):
                    sp.dma_start(d[T:T + CAP, :], w["zeros"][:, 0:E]).then_inc(filled, 16)
                    n += 1
                return n

            filling = [0]

            def emit(b):
                i = b.i
                if b.a and not b.is_(0):
                    sp.wait_ge(xT_split, b.n(1, 0, 0, 0))
                    sp.dma_start(xT_in[:, :, :], xT_d[:, :, bass.ds(i * N, N)]).then_inc(xT_loaded, 16)
                if b.b:
                    if not b.is_(1):
                        sp.wait_ge(ctx_split_, b.n(0, 1, 0, 0))
                    sp.dma_start(c_in[:, :], ctxT[:, bass.ds((i - 1) * N, N)]).then_inc(ctx_loaded, 16)
                if b.a:
                    if not b.is_(0):
                        sp.wait_ge(xb_ready, b.n(1, 0, 0, 0))
                    sp.dma_start(x_in[:, :, :], x_d[:, bass.ds(i * NB, NB), :]).then_inc(x_loaded, 16)
                if b.c:
                    sp.wait_ge(ln2, b.n(0, 0, 1, 1))
                    sp.dma_start(x2_d[bass.ds((i - 2) * N, N), :].rearrange("(t p) e -> p t e", p=P),
                                 x2[:, :, :]).then_inc(x2_stored, 16)
                    sp.wait_ge(free, b.job("TX", 1, 0))
                    sp.dma_start(x2T_d[bass.ds((i - 2) * NB, NB), :, :].rearrange("t p n -> p t n"),
                                 x2s[:, :, :, :, :].rearrange("p t a c n -> p t (a c n)"))\
                      .then_inc(x2T_stored, 16)
                if b.is_(0):
                    filling[0] = fills()
                if b.is_(B):
                    sp.wait_ge(full, done_before(B, RING_A, RING_B, RING_C))
                    loads.shared_half(sp, "SG")
                    for s in range(2):
                        loads.projection(sp, "WG", s, s)
                        loads.projection(sp, "WU", s, s)
                        if s == 0:
                            loads.shared_half(sp, "SU")
                        loads.down(sp, s, s)

            sp.sem_inc(x2_stored, 1)
            sp.sem_inc(x2T_stored, 1)
            bodies(sp, emit)
            sp.wait_ge(x2_stored, 16 * B + 1)
            sp.wait_ge(x2T_stored, 16 * B + 1)
            sp.wait_ge(filled, 16 * filling[0])

        @block.gpsimd
        def _(pool):
            def emit(b):
                if b.a and not b.is_(0):
                    pool.wait_ge(xT_loaded, b.n(16, 0, 0, 16))
                    pool.wait_ge(full, b.last_job(*X_READER))
                    own_wait(pool, taken)
                    pool.tensor_copy(xs[:, 0, :, :], xT_in[:, :, :]).then_inc(xfer, 1)
                    pool.wait_ge(xfer, b.n(1, 1, 0, 1))
                    pool.tensor_tensor(xs[:, 1, :, :], xT_in[:, :, :], xs[:, 0, :, :], ALU.subtract)\
                        .then_inc(xT_split, 1)
                if b.b:
                    pool.wait_ge(ctx_loaded, b.n(0, 16, 0, 16))
                    if not b.is_(1):
                        pool.wait_ge(full, b.last_job("C", 1, 0))
                    own_wait(pool, taken)
                    pool.tensor_copy(cs[:, 0, :], c_in[:, :]).then_inc(xfer, 1)
                    pool.wait_ge(xfer, b.n(1, 1, 0, 2 if b.a else 1))
                    pool.tensor_tensor(cs[:, 1, :], c_in[:, :], cs[:, 0, :], ALU.subtract)\
                        .then_inc(ctx_split_, 1)
                if b.a:
                    pool.wait_ge(x_loaded, b.n(16, 0, 0, 16))
                    if not b.is_(0):
                        pool.wait_ge(ln1, b.n(1, 0, 0, 0))
                    for t in range(NB):
                        last = pool.tensor_tensor(xb[:, t, :], x_in[:, t, :], w["bias"][:, :], ALU.add)
                    last.then_inc(xb_ready, 1)
                if b.b:
                    for g in range(EC):
                        pool.wait_ge(pexp, b.n(0, 4, 0, g + 1))
                        own_wait(pool, taken)
                        pool.affine_select(
                            out=p32[:, g % 2, :, 0:2 * P], in_=p32[:, g % 2, :, 0:2 * P],
                            compare_op=ALU.is_ge, fill=0.0, base=0, pattern=[[0, 4], [0, 2], [1, P]],
                            channel_multiplier=-1).then_inc(pmask, 1)
                        if b.c and g == 1:
                            pool.wait_ge(rec_ready, b.n(0, 0, 1, 1))
                            own_wait(pool, taken)
                        if b.c and g > 0:
                            table.scatter(pool, (g - 1) * NB * TOPK // (EC - 1), g * NB * TOPK // (EC - 1))
                if b.is_(0):
                    pool.wait_ge(slots_empty, 16)
                    pool.sem_inc(rec_used, 1)
                if b.c and b.b:
                    pool.wait_ge(scattered, 16 * NB * TOPK * b.n(0, 0, 1, 1))
                    pool.sem_inc(rec_used, 1)

            bodies(pool, emit)

        @block.tensor
        def _(pe):
            def product(out_, left, right, chunks, inc=None):
                n = 0
                for c in range(chunks):
                    for a, b in PASSES:
                        last = pe.matmul(out_, left(a, c), right(b, c), start=(n == 0),
                                         stop=(n == 3 * chunks - 1))
                        n += 1
                return last

            def emit(b):
                for s in b.steps:
                    name, g, h = s
                    if s in b.ring:
                        b.reuse(pe, *s)
                        o = b.bank(*s)
                    if name == "Y":
                        if h == 0 and g == 0:
                            pe.wait_ge(xT_split, b.n(1, 0, 0, 1))
                        for l in range(2):
                            f = 2 * h + l
                            last = product(o[:, l * N:(l + 1) * N],
                                           lambda a, c: w["A"][:, a, g, c, f * P:(f + 1) * P],
                                           lambda a, c: xs[:, a, c, :], EC)
                    elif name == "V":
                        last = product(o[:, :], lambda a, c: xs[:, a, c, h * P:(h + 1) * P],
                                       lambda a, c: w["M"][:, a, g, c, :], EC)
                    elif name == "S":
                        pe.wait_ge(free, b.job("Y", g, 1))
                        last = product(o[:, 0:N], lambda a, c: xs[:, a, c, h * P:(h + 1) * P],
                                       lambda a, c: y[:, a, c, :], EC)
                    elif name == "O":
                        pe.wait_ge(free, b.job("V", H - 1, 1))
                        pe.wait_ge(wready, b.n(H, 0, 0, H))
                        last = product(o[:, :],
                                       lambda a, c: ws[:, a, c // NB, c % NB, g * P:(g + 1) * P],
                                       lambda a, c: v[:, a, c // NB, c % NB, :], H * NB)
                    elif name in ("T", "TX"):
                        src = x1 if name == "T" else x2
                        pe.wait_ge(ln1 if name == "T" else ln2, b.n(0, 1, 0, 1) if name == "T" else b.n(0, 0, 1, 1))
                        for l in range(2):
                            for t in range(NB):
                                last = pe.transpose(o[:, (l * NB + t) * P:(l * NB + t + 1) * P],
                                                    src[:, t, (2 * g + l) * P:(2 * g + l + 1) * P],
                                                    ident[:, :])
                    elif name == "Q":
                        pe.wait_ge(free, b.job("T", 1, 0))
                        for l in range(2):
                            d = 2 * g + l
                            last = product(o[:, l * N:(l + 1) * N],
                                           lambda a, c: w["xwq"][:, a, c, d * P:(d + 1) * P],
                                           lambda a, c: x1s[:, a, c, :], EC)
                    elif name == "K":
                        if g == 0:
                            pe.wait_ge(ctx_split_, b.n(0, 1, 0, 1))
                        for l in range(2):
                            d = 2 * g + l
                            last = product(o[:, l * N:(l + 1) * N],
                                           lambda a, c: w["wkv"][:, a, d * P:(d + 1) * P],
                                           lambda a, c: cs[:, a, :], 1)
                    elif name == "C":
                        last = product(o[:, :], lambda a, c: cs[:, a, g * P:(g + 1) * P],
                                       lambda a, c: w["wkv"][:, a, E:2 * E], 1)
                    elif name == "M":
                        if g == 0:
                            pe.wait_ge(free, b.job("K", 1, 0))
                            pe.wait_ge(free, b.job("Q", 1, 0))
                            if not b.is_(1):
                                pe.wait_ge(pexp, b.n(0, 4, 0, 0))
                        else:
                            pe.wait_ge(quad_max, b.n(0, 4, 0, g))
                        for lo, hi, q0 in ((0, P, 0), (P, P + N, P)):
                            for r in range(4):
                                rows = slice(32 * r, 32 * r + 32)
                                last = pe.matmul(quad[:, r, lo:hi], q[rows, 0, g, q0:q0 + P],
                                                 k[rows, 0, g, 0:hi - lo], start=True, stop=True)
                        last.then_inc(quad_full, 1)
                    elif name == "MT":
                        pe.wait_ge(quad_max, b.n(0, 4, 0, 4))
                        last = pe.transpose(o[:, 0:P], mx[:, g, :], ident[:, :])
                    elif name == "ST":
                        if g == 0:
                            pe.wait_ge(free, b.job("MT", 1, 0))
                        else:
                            pe.wait_ge(pexp, b.n(0, 4, 0, g))
                        for lo, hi, k0, q0 in ((0, P, P, P), (P, P + N, 0, 0)):
                            for n, (a, c) in enumerate(PASSES):
                                for r in range(4):
                                    rows = slice(32 * r, 32 * r + 32)
                                    pe.matmul(quad[:, r, lo:hi], k[rows, a, g, k0:k0 + P],
                                              q[rows, c, g, q0:N], start=(n == 0), stop=False)
                            for r in range(4):
                                rows = slice(32 * r, 32 * r + 32)
                                last = pe.matmul(quad[:, r, lo:hi], w["pick"][rows, g, :],
                                                 mT[rows, q0:N], start=False, stop=True)
                        last.then_inc(quad_full, 1)
                    elif name == "AV":
                        pe.wait_ge(pready, b.n(0, 4, 0, g + 1))
                        if g == 0:
                            pe.wait_ge(free, b.job("C", 1, 0))
                        pg = ps[:, g % 2]
                        n = 0
                        for kb, q0, lo in ((0, 0, P), (1, P, 0)):
                            for a, c in PASSES:
                                for r in range(4):
                                    col = (4 * g + r) * HD
                                    pe.matmul(o[32 * r:32 * r + 32, q0:N], cv[:, a, kb, col:col + HD],
                                              ps[:, g % 2, c, r, lo:lo + N - q0],
                                              start=(n == 0), stop=(n == 5), tile_position=(0, 32 * r))
                                n += 1
                        n = 0
                        for kb, q0, lo in ((0, 0, P), (1, P, 0)):
                            for c in range(2):
                                for r in range(4):
                                    last = pe.matmul(o[32 * r:32 * r + 32, N + q0:2 * N],
                                                     w["ones"][:, 0:HD],
                                                     ps[:, g % 2, c, r, lo:lo + N - q0],
                                                     start=(n == 0), stop=(n == 3),
                                                     tile_position=(0, 32 * r))
                                n += 1
                    elif name == "OUT":
                        pe.wait_ge(oready, b.n(0, 4, 0, 4))
                        last = product(o[:, :], lambda a, c: os_[:, a, c, g * P:(g + 1) * P],
                                       lambda a, c: w["wout"][:, a, c, :], EC)
                    elif name == "R":
                        pe.wait_ge(free, b.job("TX", 1, 0))
                        for t in range(NB):
                            last = product(o[:, t * NX:(t + 1) * NX],
                                           lambda a, c: x2s[:, t, a, c, :],
                                           lambda a, c: w["gate"][:, a, c, :], EC)
                    elif name == "CT":
                        pe.wait_ge(chosen_ready, b.n(0, 0, 1, 1))
                        pe.matmul(o[:, 0:NX], w["before"][:, :], chosen[:, 0, :], start=True, stop=False)
                        pe.matmul(o[:, 0:NX], w["ones"][:, :], total[:, :], start=False, stop=True)
                        pe.matmul(o[:, NX:2 * NX], w["before"][:, :], chosen[:, 1, :], start=True, stop=False)
                        pe.matmul(o[:, NX:2 * NX], w["ones"][:, :], total[:, :], start=False, stop=False)
                        last = pe.matmul(o[:, NX:2 * NX], w["ones"][:, :], chosen[:, 0, :], start=False, stop=True)
                    if s in b.ring:
                        last.then_inc(full, 1)

            bodies(pe, emit)

        def halves(name, g, h, o):
            two = o[:, :].rearrange("p (l n) -> p l n", l=2)
            if name == "Y":
                return two, lambda a: y[:, a, 2 * h:2 * h + 2, :], 1.0
            if name == "V":
                return o[:, :], lambda a: v[:, a, g, h, :], 1.0
            if name == "T":
                return two, lambda a: x1s[:, a, 2 * g:2 * g + 2, :], 1.0
            if name == "Q":
                return two, lambda a: q[:, a, 2 * g:2 * g + 2, :], 1.0 / (W_SCALE * math.sqrt(HD))
            if name == "K":
                return two, lambda a: k[:, a, 2 * g:2 * g + 2, :], 1.0 / W_SCALE
            if name == "C":
                return o[:, :], lambda a: cv[:, a, g, :], 1.0 / W_SCALE
            return (o[:, :].rearrange("p (l t n) -> p t l n", l=2, t=NB),
                    lambda a: x2s[:, :, a, 2 * g:2 * g + 2, :], 1.0)

        SC = 1.0 / math.sqrt(E)

        @block.scalar
        def _(act):
            def emit(b):
                for s in b.steps:
                    name, g, h = s
                    if s in b.split:
                        act.wait_ge(full, b.job(*s))
                        if name == "TX" and g == 0:
                            act.wait_ge(x2T_stored, b.n(0, 0, 16, 1))
                        src, half, scale = halves(name, g, h, b.bank(*s))
                        act.activation(half(0), src, ACT.Copy, scale=scale).then_inc(high, 1)
                    elif name == "S":
                        act.wait_ge(smax, b.n(2 * H, 0, 0, 2 * g + h + 1))
                        if not (b.is_(0) and g == 0):
                            act.wait_ge(wready, b.n(H, 0, 0, g))
                        act.activation(e32[:, h, :], b.bank(*s)[:, 0:N], ACT.Exp, scale=SC,
                                       bias=srow[:, h, 1:2], accum_out=srow[:, h, 2:3]).then_inc(sexp, 1)
                    elif name == "S1":
                        for t in range(NB):
                            act.wait_ge(free, b.job("S", g, t))
                            act.activation(ws[:, 0, g, t, :], e32[:, t, :], ACT.Copy,
                                           scale=srow[:, t, 3:4]).then_inc(whigh, 1)
                    elif name == "ST":
                        act.wait_ge(quad_full, b.n(0, 8, 0, 4 + g + 1))
                        if not (b.is_(1) and g < 2):
                            act.wait_ge(pready, b.n(0, 4, 0, g - 1))
                        act.activation(p32[:, g % 2, :, :], quad[:, :, 0:N + P], ACT.Exp).then_inc(pexp, 1)
                    elif name == "P":
                        act.wait_ge(pmask, b.n(0, 4, 0, g + 1))
                        if g >= 2:
                            act.wait_ge(full, b.job("AV", g - 2, 0))
                        act.activation(ps[:, g % 2, 0, :, :], p32[:, g % 2, :, :], ACT.Copy).then_inc(phigh, 1)
                    elif name == "OM":
                        act.wait_ge(free, b.job("AV", g, 0))
                        act.activation(os_[:, 0, g, :], o32[:, g % 2, :], ACT.Copy).then_inc(ohigh, 1)
                    elif name == "RM":
                        act.wait_ge(rmax, b.n(0, 0, 1, 1))
                        for t in range(NB):
                            act.activation(ex[:, t, :], lg[:, t, :], ACT.Exp, scale=1.0 / W_SCALE,
                                           bias=rrow[:, t, 0:1], accum_out=rrow[:, t, 1:2]).then_inc(rexp, 1)
                            act.activation(etop[:, t, :], top[:, t, :], ACT.Exp, scale=1.0 / W_SCALE,
                                           bias=rrow[:, t, 0:1]).then_inc(rexp, 1)

            bodies(act, emit)

        @block.vector
        def _(dve):
            links = [0]
            dve.memset(mx[:, :, :], 0.0)
            dve.memset(total[:, :], 0.0).then_inc(dve_step, 1)
            dve.wait_ge(dve_step, 1)

            def emit(b):
                links[0] = 0

                def link(ins):
                    ins.then_inc(dve_step, 1)
                    links[0] += 1
                    dve.wait_ge(dve_step, done_before(b.i, LINKS_A, LINKS_B, LINKS_C) + b.i * LINKS_LN + (1 + links[0]))

                def norm(parts):
                    rows = [(at + t, pre[:, t, :], dst[:, t, :]) for at, pre, dst, _ in parts for t in range(NB)]
                    for n, src, _ in rows:
                        last = dve.bn_stats(stats[:, n, :], src)
                    link(last)
                    own_wait(dve, taken)
                    for n, _, _ in rows:
                        last = dve.bn_aggr(mv[:, n, :], stats[:, n, :])
                    link(last)
                    n0, n1 = rows[0][0], rows[-1][0] + 1
                    inverse_root(dve, link, rstd[:, n0:n1], mv[:, n0:n1, 1], root_tmp[:, :, n0:n1])
                    for n, src, dst in rows:
                        last = dve.tensor_scalar(dst, src, mv[:, n, 0:1], rstd[:, n:n + 1], ALU.subtract, ALU.mult)
                        if n % NB == NB - 1:
                            last.then_inc(parts[(n - n0) // NB][3], 1)

                for s in b.steps:
                    name, g, h = s
                    o = b.bank(*s) if s in b.ring else None
                    if s in b.split:
                        dve.wait_ge(high, b.high(*s))
                        src, half, scale = halves(name, g, h, o)
                        if name == "TX":
                            for t in range(NB):
                                last = dve.scalar_tensor_tensor(half(1)[:, t], src[:, t], scale,
                                                                half(0)[:, t], ALU.mult, ALU.subtract)
                            last.then_inc(free, 1)
                        else:
                            dve.scalar_tensor_tensor(half(1), src, scale, half(0), ALU.mult, ALU.subtract)\
                               .then_inc(free, 1)
                    elif name == "S":
                        dve.wait_ge(full, b.job(*s))
                        link(dve.reduce_max(srow[:, h, 0:1], o[:, 0:N], axis=AX.X))
                        dve.tensor_scalar(srow[:, h, 1:2], srow[:, h, 0:1], -SC, None, ALU.mult)\
                           .then_inc(smax, 1)
                    elif name == "S1":
                        for t in range(NB):
                            dve.wait_ge(sexp, b.n(2 * H, 0, 0, 2 * g + t + 1))
                            dve.reciprocal(srow[:, t, 3:4], srow[:, t, 2:3]).then_inc(free, 1)
                    elif name == "S2":
                        dve.wait_ge(whigh, b.n(2 * H, 0, 0, 2 * g + 2))
                        for t in range(NB):
                            last = dve.scalar_tensor_tensor(ws[:, 1, g, t, :], e32[:, t, :], srow[:, t, 3:4],
                                                            ws[:, 0, g, t, :], ALU.mult, ALU.subtract)
                        last.then_inc(wready, 1)
                    elif name == "O":
                        dve.wait_ge(full, b.job(*s))
                        if g == 0:
                            dve.wait_ge(xb_ready, b.n(1, 0, 0, 1))
                        dve.scalar_tensor_tensor(pre[:, g, :], o[:, :], 1.0 / H, xb[:, g, :],
                                                 ALU.mult, ALU.add).then_inc(free, 1)
                    elif name == "LN":
                        parts = []
                        if b.a:
                            dve.wait_ge(free, b.job("O", 1, 0))
                            parts.append((0, pre, x1, ln1))
                        if b.b:
                            dve.wait_ge(free, b.job("OUT", 1, 0))
                            dve.wait_ge(x2_stored, b.n(0, 0, 16, 17 if b.c else 1))
                            parts.append((NB, pre2, x2, ln2))
                        norm(parts)
                    elif name == "M":
                        dve.wait_ge(quad_full, b.n(0, 8, 0, g + 1))
                        own_wait(dve, taken)
                        for qb, lo, n in ((0, 0, P), (1, P, N)):
                            for r in range(4):
                                last = dve.tensor_tensor_reduce(
                                    out=quad[:, r, lo:lo + n], in0=quad[:, r, lo:lo + n],
                                    in1=w["causal"][:, N - n:N], scale=1.0, scalar=-3e38,
                                    op0=ALU.add, op1=ALU.max, accum_out=mx[:, qb, 32 * r + g:32 * r + g + 1])
                        last.then_inc(quad_max, 1)
                    elif name == "MT":
                        dve.wait_ge(full, b.job(*s))
                        dve.tensor_copy(mT[:, g * P:(g + 1) * P], o[:, 0:P]).then_inc(free, 1)
                    elif name == "P":
                        dve.wait_ge(phigh, b.n(0, 4, 0, g + 1))
                        dve.tensor_tensor(ps[:, g % 2, 1, :, :], p32[:, g % 2, :, :], ps[:, g % 2, 0, :, :],
                                          ALU.subtract).then_inc(pready, 1)
                    elif name == "AV":
                        dve.wait_ge(full, b.job(*s))
                        link(dve.reciprocal(rden[:, :], o[:, N:2 * N]))
                        dve.tensor_tensor(o32[:, g % 2, :], o[:, 0:N], rden[:, :], ALU.mult)\
                           .then_inc(free, 1)
                    elif name == "OM":
                        dve.wait_ge(ohigh, b.n(0, 4, 0, g + 1))
                        dve.tensor_tensor(os_[:, 1, g, :], o32[:, g % 2, :], os_[:, 0, g, :], ALU.subtract)\
                           .then_inc(oready, 1)
                    elif name == "OUT":
                        dve.wait_ge(full, b.job(*s))
                        dve.scalar_tensor_tensor(pre2[:, g, :], o[:, :], 1.0 / W_SCALE, x1[:, g, :],
                                                 ALU.mult, ALU.add).then_inc(free, 1)
                    elif name == "R":
                        dve.wait_ge(full, b.job(*s))
                        dve.tensor_copy(lg[:, :, :], o[:, 0:NB * NX].rearrange("p (t n) -> p t n", t=NB))\
                           .then_inc(free, 1)
                        dve.wait_ge(free, b.job(*s))
                        own_wait(dve, taken)
                        for t in range(NB):
                            last = dve.max(top[:, t, :], lg[:, t, :])
                        link(last)
                        dve.tensor_scalar(rrow[:, :, 0:1], top[:, :, 0:1], -1.0 / W_SCALE, None, ALU.mult)\
                           .then_inc(rmax, 1)
                        for t in range(NB):
                            last = dve.max_index(topi[:, t, :], top[:, t, :], lg[:, t, :])
                        link(last)
                        link(dve.tensor_copy(topf[:, :, :], topi[:, :, :]))
                    elif name == "RC":
                        for t in range(NB):
                            last = dve.tensor_tensor(
                                hot[:, t, :, :], w["iota"][:, :].unsqueeze(1).to_broadcast([P, TOPK, NX]),
                                topf[:, t, 0:TOPK].unsqueeze(2).to_broadcast([P, TOPK, NX]), ALU.is_equal)
                        link(last)
                        for t in range(NB):
                            with nc.allow_low_precision(reason="the sum is 0 or 1"):
                                last = dve.tensor_reduce(
                                    chosen[:, t, :], hot[:, t, :, :].rearrange("p k e -> p e k"),
                                    axis=AX.X, op=ALU.add)
                        last.then_inc(chosen_ready, 1)
                    elif name == "RM":
                        dve.wait_ge(rec_used, b.n(0, 0, 1, 1))
                        dve.wait_ge(rexp, b.n(0, 0, 2 * NB, 2 * NB))
                        link(dve.reciprocal(rrow[:, :, 2:3], rrow[:, :, 1:2]))
                        for t in range(NB):
                            dve.tensor_scalar(rec[:, t, :, 1].bitcast(F32), etop[:, t, 0:TOPK], rrow[:, t, 2:3],
                                              1.0 / W_SCALE, ALU.mult, ALU.mult)
                            last = dve.tensor_copy(rec[:, t, :, 0], w["token"][:, t:t + 1].to_broadcast([P, TOPK]))
                        link(last)
                        link(dve.tensor_scalar(w["token"][:, :], w["token"][:, :], float(N), None, ALU.add))
                    elif name == "CT":
                        dve.wait_ge(full, b.job(*s))
                        count = o[:, 0:NB * NX].rearrange("p (t n) -> p t n", t=NB)
                        dve.tensor_scalar(over[:, :, :], count, float(CAP), NO_SLOT, ALU.is_ge, ALU.mult)
                        dve.tensor_tensor(slot[:, :, :], count,
                                          w["first"][:, :].unsqueeze(1).to_broadcast([P, NB, NX]),
                                          ALU.add).then_inc(free, 1)
                        link(dve.tensor_tensor(total[:, :], total[:, :], chosen[:, 0, :], ALU.add))
                        link(dve.tensor_tensor(total[:, :], total[:, :], chosen[:, 1, :], ALU.add))
                    elif name == "RS":
                        dve.wait_ge(free, b.job("CT", 0, 0))
                        link(dve.tensor_tensor(slot[:, :, :], slot[:, :, :], over[:, :, :], ALU.add))
                        for t in range(NB):
                            last = dve.tensor_tensor(hit[:, t, :, :], hot[:, t, :, :],
                                                     slot[:, t, :].unsqueeze(1).to_broadcast([P, TOPK, NX]),
                                                     ALU.mult)
                        link(last)
                        link(dve.tensor_reduce(slotk[:, :, :], hit[:, :, :, :], axis=AX.X, op=ALU.add))
                        dve.tensor_copy(sloti[:, :, :], slotk[:, :, :]).then_inc(rec_ready, 1)
                assert links[0] == LINKS_A * b.a + LINKS_B * b.b + LINKS_C * b.c + LINKS_LN * (b.a or b.b)

            bodies(dve, emit)


MOE = [
    ("WG", 0), ("WU", 0), ("SG", 0), ("SU", 0), ("WG", 1), ("SG", 1), ("X", 0), ("SU", 1), ("WU", 1),
    ("X", 1), ("G", 0), ("SHT", 0), ("SHT", 1), ("U", 0), ("WD", 0), ("G", 1), ("HT", 0), ("U", 1),
    ("D", 0), ("HT", 1), ("WD", 1), ("SD", 0), ("D", 1),
]
MOE_JOBS = {s: n for n, s in enumerate(x for x in MOE if not x[0].startswith("W"))}
MOE_BANK = [n % 8 for n in range(16)] + [6]
MOE_SPLITS = [s for s in MOE if s[0] in ("X", "HT", "SHT")]
MOE_GATES = [s for s in MOE if s[0] in ("G", "SG")]
MOE_UPS = [s for s in MOE if s[0] in ("U", "SU")]
MOE_WEIGHTS = [s for s in MOE if s[0].startswith("W")]
MOE_FREED = [s for u in MOE if not u[0].startswith("W") and u not in MOE_GATES
             for s in ([(u[0].replace("U", "G"), u[1]), u] if u in MOE_UPS else [u])]


def experts(nc, mem, ident, z, loads, table, x2_d, x2T_d, table_d, moe_d, sdT):
    BODIES = T // P
    NJ = len(MOE_JOBS)
    HALF = FS // 2
    assert NX == 2 * BODIES and HALF <= 512 and len(MOE_BANK) == NJ
    shared = dict(SG=mem.sb("shared_gate", [P, 2, EC, FS], F16), SU=mem.sb("shared_up", [P, 2, EC, FS], F16),
                  SD=mem.sb("shared_down", [P, 2, SC6, E], F16))
    wf, w_in, shared_stage, shared_in = loads.wf, loads.w_in, loads.stage, loads.shared_in
    wh = dict(WG=mem.sb("w_gate_split", [P, 2, 2, EC * F], F16), WU=mem.sb("w_up_split", [P, 2, 2, EC * F], F16),
              WD=mem.sb("w_down_split", [P, 2, 2, FC * E], F16))
    records = mem.sb("records", [P, NX, 2], U32)
    gi = mem.sb("gather_index", [P, 2, 1], U32)
    si = mem.sb("scatter_index", [P, 2, 1], U32)
    xg = mem.sb("gathered", [P, 2, E], F32)
    xgs = mem.sb("gathered_T_split", [P, 2, 2, EC, P], F16)
    x2t = mem.sb("x2T_block", [P, 2, EC, P], F16)
    x2n = mem.sb("x2_block", [P, E], F32)
    silu32 = mem.sb("silu_out", [P, 2, F], F32)
    h32 = mem.sb("hidden", [P, 2, F], F32)
    hs = mem.sb("hidden_T_split", [P, 2, 2, FC, P], F16)
    ssilu32 = mem.sb("shared_silu", [P, FS], F32)
    sh32 = shared_stage["rest"][:, 0:FS]
    shs = mem.sb("shared_hidden_T_split", [P, 2, SC6, P], F16)
    d32 = shared_stage["SG"][:, 0:2 * E].rearrange("p (s n) -> p s n", s=2)
    banks = [mem.ps(f"moe_bank{n}", [P, 512], F32) for n in range(8)]

    shared_high, shared_low = mem.sem("shared_high"), mem.sem("shared_low")
    zero_rows = mem.sem("unused_down_rows_zero")
    records_in = mem.sem("records_in")
    w_high = mem.sem("expert_weight_high")
    w_low = mem.sem("expert_weight_low")
    x2t_in, x2n_in = mem.sem("x2T_in"), mem.sem("x2_in")
    index_ready = mem.sem("index_ready")
    gathered = [mem.sem(f"gathered{s}") for s in range(2)]
    full, high, free = mem.sem("moe_full"), mem.sem("moe_high"), mem.sem("moe_free")
    silu = mem.sem("silu_ready")
    prod = mem.sem("hidden_ready")
    added = mem.sem("expert_added")
    taken = mem.sem("waits_taken_3")

    def count(order, i, step):
        return i * len(order) + (order.index(step) + 1)

    def job(i, *step):
        return i * NJ + (MOE_JOBS[step] + 1)

    def freed(i, *step):
        return i * NJ + (MOE_FREED.index(step) + 1)

    def bank_of(step):
        return banks[MOE_BANK[MOE_JOBS[step]]]

    def reuse(eng, i, step, first):
        users = [s for s in MOE_JOBS if MOE_BANK[MOE_JOBS[s]] == MOE_BANK[MOE_JOBS[step]]]
        at = users.index(step)
        if at > 0:
            eng.wait_ge(free, freed(i, *users[at - 1]))
        elif not first:
            eng.wait_ge(free, i * NJ + (MOE_FREED.index(users[-1]) + 1 - NJ))

    def bodies(eng, emit):
        emit(0, True)
        with eng.Fori(1, BODIES) as i:
            emit(i, False)

    with nc.Block() as block:
        @block.sync
        def _(sp):
            def emit(i, first):
                for s in range(2):
                    if not first:
                        for k in ("WG", "WU"):
                            sp.wait_ge(w_low, count(MOE_WEIGHTS, i - 1, (k, s)))
                            loads.projection(sp, k, 2 * i + s, s)
                    if s == 0:
                        if not first:
                            sp.wait_ge(full, job(i - 1, "SU", 1))
                        sp.dma_start(x2t[:, :, :, :].rearrange("p a c n -> p (a c n)"),
                                     x2T_d[bass.ds(i, 1), :, :].rearrange("o p n -> p (o n)")).then_inc(x2t_in, 16)
                    if first and s == 0:
                        dst = shared_stage["SD"].rearrange("p (c n) -> p c n", c=SC6)
                        whole, own = (SC6 - 1) * P, FS - (SC6 - 1) * P
                        sp.dma_start(dst[:, 0:SC6 - 1, :], sdT[0:whole, :].rearrange("(c p) n -> p c n", p=P))\
                          .then_inc(shared_in["SD"], 16)
                        sp.dma_start(dst[P - own:P, SC6 - 1, :], sdT[whole:FS, :]).then_inc(shared_in["SD"], 16)
                    if not first:
                        sp.wait_ge(w_low, count(MOE_WEIGHTS, i - 1, ("WD", s)))
                        loads.down(sp, 2 * i + s, s)
                if not first:
                    sp.wait_ge(free, freed(i - 1, "SD", 0))
                sp.dma_start(x2n[:, :], x2_d[bass.ds(i * P, P), :]).then_inc(x2n_in, 16)
                if first:
                    sp.wait_ge(table.scattered, 16 * NB * TOPK * B)
                    sp.dma_start(records[:, :, :], table_d.rearrange("(e p) c -> p e c", p=CAP))\
                      .then_inc(records_in, 16)

            bodies(sp, emit)

        @block.gpsimd
        def _(pool):
            def gather(i, first):
                for s in range(2):
                    if not first:
                        pool.wait_ge(gathered[s], 16 * i)
                        pool.wait_ge(full, job(i - 1, "X", s))
                        own_wait(pool, taken)
                    pool.tensor_copy(gi[:, s, :], records[:, bass.ds(2 * i + s, 1), 0]).then_inc(index_ready, 1)
                    pool.wait_ge(index_ready, (4 * i - 2 if not first else 0) + (s + 1))
                    own_wait(pool, taken)
                    pool.indirect_dma_start(xg[:, s, :], None, x2_d,
                                            bass.IndirectOffsetOnAxis(ap=gi[:, s, :], axis=0),
                                            bounds_check=T + CAP - 1).then_inc(gathered[s], 16)

            def add(i, first, gathers_after):
                for s in range(2):
                    pool.wait_ge(free, freed(i, "D", s))
                    if not (first and s == 0):
                        pool.wait_ge(added, 32 * i + 16 * s)
                    own_wait(pool, taken)
                    pool.tensor_copy(si[:, s, :], records[:, bass.ds(2 * i + s, 1), 0]).then_inc(index_ready, 1)
                    pool.wait_ge(index_ready, 4 * i + (2 + gathers_after + s + 1))
                    own_wait(pool, taken)
                    pool.indirect_dma_start(moe_d, bass.IndirectOffsetOnAxis(ap=si[:, s, :], axis=0),
                                            d32[:, s, :], None, bounds_check=T + CAP - 1,
                                            compute_op=ALU.add).then_inc(added, 16)

            pool.wait_ge(table.ready, B)
            table.scatter(pool, 0, NB * TOPK)
            pool.wait_ge(records_in, 16)
            gather(0, True)
            gather(1, False)
            add(0, True, 2)
            with pool.Fori(2, BODIES) as i:
                gather(i, False)
                add(i - 1, False, 2)
            add(BODIES - 1, False, 0)
            pool.wait_ge(added, 32 * BODIES)

        @block.tensor
        def _(pe):
            def product(out_, left, right, chunks):
                n = 0
                for c in range(chunks):
                    for a, b in PASSES:
                        last = pe.matmul(out_, left(a, c), right(b, c), start=(n == 0),
                                         stop=(n == 3 * chunks - 1))
                        n += 1
                return last

            def emit(i, first):
                for step in MOE:
                    name, s = step
                    if step not in MOE_JOBS:
                        continue
                    reuse(pe, i, step, first)
                    o = bank_of(step)
                    if name == "X":
                        pe.wait_ge(gathered[s], 16 * i + 16)
                        for c in range(EC):
                            last = pe.transpose(o[:, c * P:(c + 1) * P],
                                                xg[:, s, :].rearrange("p (q c) -> p c q", c=EC)[:, c, :],
                                                ident[:, :])
                    elif name in ("G", "U"):
                        pe.wait_ge(w_low, count(MOE_WEIGHTS, i, ("W" + name, s)))
                        if name == "G":
                            pe.wait_ge(free, freed(i, "X", s))
                        last = product(o[:, 0:F], lambda a, c: xgs[:, s, a, c, :],
                                       lambda b, c: wh["W" + name][:, s, b, c * F:(c + 1) * F], EC)
                    elif name in ("SG", "SU"):
                        if s == 0 and name == "SG":
                            pe.wait_ge(x2t_in, 16 * i + 16)
                        if first:
                            pe.wait_ge(shared_low, 1 if name == "SG" else 2)
                        last = product(o[:, 0:HALF], lambda a, c: x2t[:, a, c, :],
                                       lambda b, c: shared[name][:, b, c, s * HALF:(s + 1) * HALF], EC)
                    elif name == "HT":
                        pe.wait_ge(prod, count(MOE_UPS, i, ("U", s)))
                        for f in range(FC):
                            last = pe.transpose(o[:, f * P:(f + 1) * P], h32[:, s, F_START[f]:F_START[f] + P],
                                                ident[:, :])
                    elif name == "SHT":
                        pe.wait_ge(prod, count(MOE_UPS, i, ("SU", 1)))
                        for f in range(FC):
                            f0 = S_START[FC * s + f]
                            last = pe.transpose(o[:, f * P:(f + 1) * P], sh32[:, f0:f0 + P], ident[:, :])
                    elif name == "D":
                        pe.wait_ge(w_low, count(MOE_WEIGHTS, i, ("WD", s)))
                        pe.wait_ge(free, freed(i, "HT", s))
                        last = product(o[:, :], lambda a, f: hs[:, s, a, f, :],
                                       lambda b, f: wh["WD"][:, s, b, f * E:(f + 1) * E], FC)
                    elif name == "SD":
                        pe.wait_ge(free, freed(i, "SHT", 1))
                        if first:
                            pe.wait_ge(shared_low, 3)
                        last = product(o[:, :], lambda a, f: shs[:, a, f, :],
                                       lambda b, f: shared["SD"][:, b, f, :], SC6)
                    last.then_inc(full, 1)

            bodies(pe, emit)

        def halves(step):
            name, s = step
            if name == "X":
                return EC * P, lambda a: xgs[:, s, a, :, :].rearrange("p c n -> p (c n)")
            if name == "HT":
                return FC * P, lambda a: hs[:, s, a, :, :].rearrange("p f n -> p (f n)")
            return FC * P, lambda a: shs[:, a, FC * s:FC * (s + 1), :].rearrange("p f n -> p (f n)")

        def silu_of(name, s):
            return silu32[:, s, :] if name in ("G", "U") else ssilu32[:, s * HALF:(s + 1) * HALF]

        @block.scalar
        def _(act):
            def split_shared(name):
                act.activation(shared[name][:, 0, :, :].rearrange("p c n -> p (c n)"),
                               shared_stage[name], ACT.Copy, scale=W_SCALE).then_inc(shared_high, 1)

            act.wait_ge(shared_in["SG"], 16)
            split_shared("SG")

            def emit(i, first):
                for step in MOE:
                    name, s = step
                    if first and step == ("SG", 1):
                        act.wait_ge(shared_in["SD"], 32)
                        act.wait_ge(zero_rows, 1)
                        split_shared("SD")
                    if first and step == ("SG", 0):
                        act.wait_ge(shared_in["SU"], 16)
                        split_shared("SU")
                    if step in MOE_SPLITS:
                        act.wait_ge(full, job(i, *step))
                        cols, half = halves(step)
                        act.activation(half(0), bank_of(step)[:, 0:cols], ACT.Copy).then_inc(high, 1)
                    elif name in wf:
                        act.wait_ge(w_in[name, s], (16 * i + 16) * (2 if name == "WD" else 1))
                        if not first:
                            act.wait_ge(full, job(i - 1, name[1], s))
                        act.activation(wh[name][:, s, 0, :], wf[name][:, s, :], ACT.Copy, scale=W_SCALE)\
                           .then_inc(w_high, 1)
                    elif step in MOE_GATES:
                        act.wait_ge(full, job(i, *step))
                        if not first:
                            act.wait_ge(prod, count(MOE_UPS, i - 1, ("U" if name == "G" else "SU", s)))
                        act.activation(silu_of(name, s), bank_of(step)[:, 0:F if name == "G" else HALF],
                                       ACT.Silu, scale=1.0 / W_SCALE).then_inc(silu, 1)

            bodies(act, emit)

        @block.vector
        def _(dve):
            dve.memset(shared_stage["SD"][0:SC6 * P - FS, (SC6 - 1) * E:SC6 * E], 0.0)
            for s in range(2):
                last = dve.memset(wf["WD"][0:FC * P - F, s, (FC - 1) * E:FC * E], 0.0)
            last.then_inc(zero_rows, 1)

            def split_shared(n, name):
                dve.wait_ge(shared_high, n + 1)
                dve.scalar_tensor_tensor(shared[name][:, 1, :, :].rearrange("p c n -> p (c n)"),
                                         shared_stage[name], W_SCALE,
                                         shared[name][:, 0, :, :].rearrange("p c n -> p (c n)"),
                                         ALU.mult, ALU.subtract).then_inc(shared_low, 1)
            split_shared(0, "SG")

            def emit(i, first):
                for step in MOE:
                    name, s = step
                    if first and step == ("SG", 0):
                        split_shared(1, "SU")
                    if first and step == ("SG", 1):
                        split_shared(2, "SD")
                    if first and name == "SD":
                        dve.wait_ge(shared_low, 3)
                    if step in MOE_SPLITS:
                        dve.wait_ge(high, count(MOE_SPLITS, i, step))
                        cols, half = halves(step)
                        dve.tensor_tensor(half(1), bank_of(step)[:, 0:cols], half(0), ALU.subtract)\
                           .then_inc(free, 1)
                    elif name in wf:
                        dve.wait_ge(w_high, count(MOE_WEIGHTS, i, step))
                        dve.scalar_tensor_tensor(wh[name][:, s, 1, :], wf[name][:, s, :], W_SCALE,
                                                 wh[name][:, s, 0, :], ALU.mult, ALU.subtract).then_inc(w_low, 1)
                    elif step in MOE_UPS:
                        dve.wait_ge(full, job(i, *step))
                        dve.wait_ge(silu, count(MOE_GATES, i, ("G" if name == "U" else "SG", s)))
                        dst = h32[:, s, :] if name == "U" else sh32[:, s * HALF:(s + 1) * HALF]
                        dve.scalar_tensor_tensor(dst, bank_of(step)[:, 0:F if name == "U" else HALF],
                                                 1.0 / W_SCALE, silu_of(name, s), ALU.mult, ALU.mult)\
                           .then_inc(prod, 1)
                        dve.wait_ge(prod, count(MOE_UPS, i, step))
                        dve.sem_inc(free, 2)
                    elif name == "D":
                        dve.wait_ge(full, job(i, *step))
                        if first:
                            dve.wait_ge(records_in, 16)
                        if not first:
                            dve.wait_ge(added, 32 * i + (16 * s - 16))
                        dve.tensor_scalar(d32[:, s, :], bank_of(step)[:, :],
                                          records[:, bass.ds(2 * i + s, 1), 1].bitcast(F32), None, ALU.mult)\
                           .then_inc(free, 1)
                    elif name == "SD":
                        dve.wait_ge(full, job(i, *step))
                        dve.wait_ge(x2n_in, 16 * i + 16)
                        dve.scalar_tensor_tensor(z[:, bass.ds(i, 1), :].rearrange("p o n -> p (o n)"),
                                                 bank_of(step)[:, :], 1.0 / W_SCALE, x2n[:, :],
                                                 ALU.mult, ALU.add).then_inc(free, 1)

            bodies(dve, emit)


def finish(nc, mem, moe_d, z, out):
    TILES = [2, 4, 8, 8, 6, 4]
    START = [sum(TILES[:n]) for n in range(len(TILES))]
    BLOCKS = T // P
    assert sum(TILES) == BLOCKS
    a = mem.sb("expert_rows", [P, BLOCKS, E], F32)
    stats = mem.sb("final_stats", [P, BLOCKS, 6], F32)
    mv = mem.sb("final_mean_var", [P, BLOCKS, 2], F32)
    scale = mem.sb("final_scale", [P, BLOCKS], F32)
    shift = mem.sb("final_shift", [P, BLOCKS], F32)
    root_tmp = mem.sb("final_root_tmp", [P, 3, BLOCKS], F32)
    loaded = [mem.sem(f"rows_loaded{n}") for n in range(len(TILES))]
    summed, scaled, normed = mem.sem("summed"), mem.sem("row_scales"), mem.sem("normed")
    stored = mem.sem("rows_stored")
    step = mem.sem("final_step")

    def blocks(n):
        return slice(START[n], START[n] + TILES[n])

    def rows(d, n):
        return d[P * START[n]:P * (START[n] + TILES[n]), :].rearrange("(r p) n -> p r n", r=TILES[n])

    with nc.Block() as block:
        @block.sync
        def _(sp):
            for n in range(len(TILES)):
                sp.dma_start(a[:, blocks(n)], rows(moe_d, n)).then_inc(loaded[n], 16)

        @block.gpsimd
        def _(pool):
            for n in range(len(TILES)):
                pool.wait_ge(loaded[n], 16)
                pool.tensor_tensor(a[:, blocks(n)], a[:, blocks(n)], z[:, blocks(n)], ALU.add).then_inc(summed, 1)

        @block.vector
        def _(dve):
            links = [0]

            def link(ins):
                ins.then_inc(step, 1)
                links[0] += 1
                dve.wait_ge(step, links[0])

            for n in range(len(TILES)):
                tile = blocks(n)
                dve.wait_ge(summed, n + 1)
                for k in range(tile.start, tile.stop):
                    last = dve.bn_stats(stats[:, k, :], a[:, k, :])
                link(last)
                for k in range(tile.start, tile.stop):
                    last = dve.bn_aggr(mv[:, k, :], stats[:, k, :])
                link(last)
                inverse_root(dve, link, scale[:, tile], mv[:, tile, 1], root_tmp[:, :, tile])
                dve.scalar_tensor_tensor(shift[:, tile], mv[:, tile, 0], -1.0, scale[:, tile],
                                         ALU.mult, ALU.mult).then_inc(scaled, 1)

        @block.scalar
        def _(act):
            for n in range(len(TILES)):
                tile = blocks(n)
                act.wait_ge(scaled, n + 1)
                for k in range(tile.start, tile.stop):
                    last = act.activation(a[:, k, :], a[:, k, :], ACT.Identity, scale=scale[:, k:k + 1],
                                          bias=shift[:, k:k + 1])
                last.then_inc(normed, 1)
                act.wait_ge(normed, n + 1)
                act.dma_start(rows(out, n), a[:, tile]).then_inc(stored, 16)
            act.wait_ge(stored, 16 * len(TILES))


def kernel(x, ctx_512, L0_attn_Wq, L0_attn_Wk, L0_attn_Wv, L0_attn_fc_w, L0_attn_fc_b, L0_xattn_Wq,
           L0_xattn_Wkv_expand, L0_xattn_Wout, L0_ffn_gate_w, L0_ffn_w_gate, L0_ffn_w_up, L0_ffn_w_down,
           L0_ffn_sh_gate, L0_ffn_sh_up, L0_ffn_sh_down):
    import numpy as np
    import concourse.bacc as bacc
    from concourse.bass_utils import run_bass_kernel_spmd

    def rows(a):
        return np.ascontiguousarray(a)

    flat = np.asarray(x).reshape(T, E)
    arrays = {
        "x": rows(flat), "xT": rows(flat.T), "ctxT": rows(np.asarray(ctx_512).reshape(T, L).T),
        "wq": rows(L0_attn_Wq), "wk": rows(L0_attn_Wk), "wv": rows(L0_attn_Wv),
        "fcT": rows(np.asarray(L0_attn_fc_w).T), "fcb": rows(L0_attn_fc_b),
        "xwqT": rows(np.asarray(L0_xattn_Wq).T), "wkvT": rows(np.asarray(L0_xattn_Wkv_expand).T),
        "woutT": rows(np.asarray(L0_xattn_Wout).T), "gateT": rows(np.asarray(L0_ffn_gate_w).T),
        "w_gate": rows(L0_ffn_w_gate), "w_up": rows(L0_ffn_w_up), "w_down": rows(L0_ffn_w_down),
        "sgT": rows(np.asarray(L0_ffn_sh_gate).T), "suT": rows(np.asarray(L0_ffn_sh_up).T),
        "sdT": rows(np.asarray(L0_ffn_sh_down).T),
    }
    nc = bacc.Bacc("TRN2", target_bir_lowering=False, num_devices=1)
    args = [nc.dram_tensor(f"in_{k}", a.shape, mybir.dt.from_np(a.dtype), kind="ExternalInput").ap()
            for k, a in arrays.items()]
    out = nc.dram_tensor("out_rows_dram", (T, E), F32, kind="ExternalOutput").ap()
    build(nc, *args, out)
    r = run_bass_kernel_spmd(nc, [{f"in_{k}": a for k, a in arrays.items()}], core_ids=[0])
    return r.results[0]["out_rows_dram"].reshape(B, N, E)
```
